# Optimizing a Trainium2 kernel written in Bass

```python
import numpy as np
import jax
import jax.numpy as jnp

def _softmax(x, axis=-1):
    return jax.nn.softmax(x, axis=axis)

def _gelu(x):
    return jax.nn.gelu(x, approximate=True)

def _silu(x):
    return jax.nn.silu(x)

def _sigmoid(x):
    return jax.nn.sigmoid(x)

def _layernorm(x, axis=-1, eps=1e-05):
    m = jnp.mean(x, axis=axis, keepdims=True)
    v = jnp.var(x, axis=axis, keepdims=True)
    return (x - m) / jnp.sqrt(v + eps)

def _scatter_add(tgt, idx, src, axis=0):
    return tgt.at[idx].add(src)

def _segment_sum(src, seg, n):
    return jax.ops.segment_sum(src, seg, n)
kernel_name = 'mk_gnn_resnorm_d2_gnn_r8_528a30'

def setup_inputs(seed: int=0):
    np.random.seed(seed)
    _w = jnp.asarray

    def _rec_inputs():
        import jax
        import jax.numpy as jnp
        _gk = jax.random.key(seed)
        x = -0.000202 + 1 * jax.random.normal(jax.random.fold_in(_gk, 1), (6250, 128), jnp.float32)
        _s = jax.random.randint(jax.random.fold_in(_gk, 2), (100000,), 0, 6250, jnp.int32)
        _d = jax.random.randint(jax.random.fold_in(_gk, 3), (100000,), 0, 6250, jnp.int32)
        _loop = jnp.arange(6250, dtype=jnp.int32)
        src = jnp.concatenate([_s, _d, _loop])
        dst = jnp.concatenate([_d, _s, _loop])
        _o = jnp.argsort(dst, stable=True)
        src = src[_o]
        dst = dst[_o]
        edge_attr_128 = 5.93493e-05 + 1.00006 * jax.random.normal(jax.random.fold_in(_gk, 12), (206250, 128), jnp.float32)
        return (x, src, dst, edge_attr_128)
    x, src, dst, edge_attr_128 = _rec_inputs()

    def _L0_gnn_setup():
        import jax, jax.numpy as jnp
        import numpy as np
        N_NODES = 6250
        N_EDGES = 75000
        F_E, F_X, F_U = (128, 128, 128)
        N_GRAPHS = 32
        HIDDEN = 256
        F_X_OUT = 128
        key = jax.random.key(seed)
        ks = jax.random.split(key, 10)
        x = jax.random.normal(ks[0], (N_NODES, F_X), dtype=jnp.float32)
        edge_index = jax.random.randint(ks[1], (2, N_EDGES), 0, N_NODES, dtype=jnp.int32)
        edge_attr = jax.random.normal(ks[2], (N_EDGES, F_E), dtype=jnp.float32)
        u = jax.random.normal(ks[3], (N_GRAPHS, F_U), dtype=jnp.float32)
        batch = jnp.sort(jax.random.randint(ks[4], (N_NODES,), 0, N_GRAPHS, dtype=jnp.int32))
        f_in = F_E + F_X + F_U
        W1 = jax.random.normal(ks[5], (f_in, HIDDEN), dtype=jnp.float32) / np.sqrt(f_in)
        b1 = jnp.zeros((HIDDEN,), dtype=jnp.float32)
        W2 = jax.random.normal(ks[6], (HIDDEN, F_X_OUT), dtype=jnp.float32) / np.sqrt(HIDDEN)
        b2 = jnp.zeros((F_X_OUT,), dtype=jnp.float32)
        return {'x': x, 'edge_index': edge_index, 'edge_attr': edge_attr, 'u': u, 'batch': batch, 'W1': W1, 'b1': b1, 'W2': W2, 'b2': b2}
    _L0_gnn_all = _L0_gnn_setup()
    _L0_gnn_in = {k: v for k, v in _L0_gnn_all.items() if k in ('u', 'W1', 'b1', 'W2', 'b2')}
    del _L0_gnn_all

    def _L1_gnn_setup():
        import jax, jax.numpy as jnp
        import numpy as np
        N, D, E = (6250, 128, 100000)
        BN_EPS = 1e-05

        def _bn(h, g, beta, m, v):
            return (h - m) * (g * jax.lax.rsqrt(v + BN_EPS)) + beta
        key = jax.random.key(seed)
        ks = jax.random.split(key, 8)
        x = jax.random.normal(ks[0], (N, D), dtype=jnp.float32)
        edge_index = jax.random.randint(ks[1], (2, E), 0, N, dtype=jnp.int64)
        eps = jnp.zeros((), dtype=jnp.float32)
        s = 1.0 / np.sqrt(D)
        W1 = jax.random.uniform(ks[2], (D, D), minval=-s, maxval=s, dtype=jnp.float32)
        b1 = jnp.zeros((D,), dtype=jnp.float32)
        g1 = jnp.ones((D,), dtype=jnp.float32)
        beta1 = jnp.zeros((D,), dtype=jnp.float32)
        m1 = jax.random.normal(ks[3], (D,), dtype=jnp.float32) * 0.1
        v1 = jax.random.uniform(ks[4], (D,), minval=0.5, maxval=1.5, dtype=jnp.float32)
        W2 = jax.random.uniform(ks[5], (D, D), minval=-s, maxval=s, dtype=jnp.float32)
        b2 = jnp.zeros((D,), dtype=jnp.float32)
        g2 = jnp.ones((D,), dtype=jnp.float32)
        beta2 = jnp.zeros((D,), dtype=jnp.float32)
        m2 = jax.random.normal(ks[6], (D,), dtype=jnp.float32) * 0.1
        v2 = jax.random.uniform(ks[7], (D,), minval=0.5, maxval=1.5, dtype=jnp.float32)
        return {'x': x, 'edge_index': edge_index, 'eps': eps, 'W1': W1, 'b1': b1, 'g1': g1, 'beta1': beta1, 'm1': m1, 'v1': v1, 'W2': W2, 'b2': b2, 'g2': g2, 'beta2': beta2, 'm2': m2, 'v2': v2}
    _L1_gnn_all = _L1_gnn_setup()
    _L1_gnn_in = {k: v for k, v in _L1_gnn_all.items() if k in ('eps', 'W1', 'b1', 'g1', 'beta1', 'm1', 'v1', 'W2', 'b2', 'g2', 'beta2', 'm2', 'v2')}
    del _L1_gnn_all
    return {'x': x, 'src': src, 'dst': dst, 'edge_attr_128': edge_attr_128, 'L0_gnn_u': _L0_gnn_in['u'], 'L0_gnn_W1': _L0_gnn_in['W1'], 'L0_gnn_b1': _L0_gnn_in['b1'], 'L0_gnn_W2': _L0_gnn_in['W2'], 'L0_gnn_b2': _L0_gnn_in['b2'], 'L1_gnn_eps': _L1_gnn_in['eps'], 'L1_gnn_W1': _L1_gnn_in['W1'], 'L1_gnn_b1': _L1_gnn_in['b1'], 'L1_gnn_g1': _L1_gnn_in['g1'], 'L1_gnn_beta1': _L1_gnn_in['beta1'], 'L1_gnn_m1': _L1_gnn_in['m1'], 'L1_gnn_v1': _L1_gnn_in['v1'], 'L1_gnn_W2': _L1_gnn_in['W2'], 'L1_gnn_b2': _L1_gnn_in['b2'], 'L1_gnn_g2': _L1_gnn_in['g2'], 'L1_gnn_beta2': _L1_gnn_in['beta2'], 'L1_gnn_m2': _L1_gnn_in['m2'], 'L1_gnn_v2': _L1_gnn_in['v2']}

def reference(x, src, dst, edge_attr_128, L0_gnn_u, L0_gnn_W1, L0_gnn_b1, L0_gnn_W2, L0_gnn_b2, L1_gnn_eps, L1_gnn_W1, L1_gnn_b1, L1_gnn_g1, L1_gnn_beta1, L1_gnn_m1, L1_gnn_v1, L1_gnn_W2, L1_gnn_b2, L1_gnn_g2, L1_gnn_beta2, L1_gnn_m2, L1_gnn_v2):
    import jax
    import jax.numpy as jnp

    def _L0_gnn_ref(x, edge_index, edge_attr, u, batch, W1, b1, W2, b2):
        import jax, jax.numpy as jnp
        import numpy as np
        N_NODES = 6250
        N_EDGES = 75000
        F_E, F_X, F_U = (128, 128, 128)
        N_GRAPHS = 32
        HIDDEN = 256
        F_X_OUT = 128
        col = edge_index[1]
        e_sum = jax.ops.segment_sum(edge_attr, col, num_segments=N_NODES)
        cnt = jax.ops.segment_sum(jnp.ones((edge_attr.shape[0],), edge_attr.dtype), col, num_segments=N_NODES)
        e_agg = e_sum / jnp.maximum(cnt, 1.0)[:, None]
        out = jnp.concatenate([x, e_agg, u[batch]], axis=1)
        h = jax.nn.relu(out @ W1 + b1)
        return h @ W2 + b2

    def _L1_gnn_ref(x, edge_index, eps, W1, b1, g1, beta1, m1, v1, W2, b2, g2, beta2, m2, v2):
        import jax, jax.numpy as jnp
        import numpy as np
        N, D, E = (6250, 128, 100000)
        BN_EPS = 1e-05

        def _bn(h, g, beta, m, v):
            return (h - m) * (g * jax.lax.rsqrt(v + BN_EPS)) + beta
        src, dst = (edge_index[0], edge_index[1])
        n = x.shape[0]
        agg = jax.ops.segment_sum(x[src], dst, num_segments=n)
        h = (1.0 + eps) * x + agg
        h = jax.nn.relu(_bn(h @ W1 + b1, g1, beta1, m1, v1))
        h = _bn(h @ W2 + b2, g2, beta2, m2, v2)
        return h + x
    edge_index = jnp.stack([src, dst])
    batch0 = jnp.zeros((6250,), jnp.int32)
    x = _layernorm(x + _L0_gnn_ref(x, edge_index, edge_attr_128, L0_gnn_u, batch0, L0_gnn_W1, L0_gnn_b1, L0_gnn_W2, L0_gnn_b2), axis=-1)
    x = _layernorm(x + _L1_gnn_ref(x, edge_index, L1_gnn_eps, L1_gnn_W1, L1_gnn_b1, L1_gnn_g1, L1_gnn_beta1, L1_gnn_m1, L1_gnn_v1, L1_gnn_W2, L1_gnn_b2, L1_gnn_g2, L1_gnn_beta2, L1_gnn_m2, L1_gnn_v2), axis=-1)
    return x

_drawn_inputs = setup_inputs


def setup_inputs(seed=0):
    import zlib

    import numpy as np

    out = dict(_drawn_inputs(seed))
    spreads = {'L0_gnn_b1': (0.0, 0.1),
     'L0_gnn_b2': (0.0, 0.1),
     'L1_gnn_b1': (0.0, 0.683),
     'L1_gnn_g1': (1.0, 0.2),
     'L1_gnn_beta1': (0.0, 0.8),
     'L1_gnn_b2': (0.0, 0.298),
     'L1_gnn_g2': (1.0, 0.2),
     'L1_gnn_beta2': (0.0, 0.368)}
    factors = {'L1_gnn_m1': 5.025}
    for name, (base, spread) in spreads.items():
        noise = np.random.default_rng([zlib.crc32(name.encode()), seed]).standard_normal(out[name].shape)
        drawn = base * np.exp(spread * noise) if base else spread * noise
        out[name] = jnp.asarray(drawn.astype(out[name].dtype))
    for name, factor in factors.items():
        out[name] = (out[name] * factor).astype(out[name].dtype)
    return out
```

```python
import concourse.bass as bass
from concourse import mybir
from contextlib import ExitStack

FP32 = mybir.dt.float32
BF16 = mybir.dt.bfloat16
FP16 = mybir.dt.float16
I32 = mybir.dt.int32
U32 = mybir.dt.uint32
ALU = mybir.AluOpType
ACT = mybir.ActivationFunctionType
AX = mybir.AxisListType

N = 6250
E = 206250
D = 128
P = 128
HID = 256
EPP = 8
GROUP = P * EPP
FULL = E // GROUP
NG = FULL + 1
REPEATS = GROUP - (E - FULL * GROUP)
WIN = 48
SWEEP = -(-N // WIN)
TILES = -(-N // P)
NP = TILES * P
TAIL = N - (TILES - 1) * P
ACCW = max(NP, N + WIN, SWEEP * WIN)
BT = 7
BLK = BT * P
NBLK = TILES // BT
HALF = BLK // 2
RING = 4
UNITS = NG // 2
TURNS = (UNITS - 1) // RING
NHOT = 4
SLOTS = 64
PAIRS = P // 2
Q = 8
LOSCALE = 2048.0
EPS = 1e-5
FAR = 100000.0
CLEARED, PARITY_MADE, ROWS_MADE, ABS_MADE, REL_MADE, DISORDER_MADE, BAD_MADE = 2, 5, 11, 20, 21, 27, 31
POOL_FIRST, POOL_MADE = 9, 21
PE_ROWS, PE_BASE, PE_NEXT = 1, 2, 3
ROWS_SPREAD = 3
SMALLS = 15
assert TILES % BT == 0 and TURNS * RING == UNITS - 1 and NG % 2 == 0 and 2 * SLOTS == P and TILES % 2 == 1


def build(nc, x, src, dst, attr, u, w1a, b1a, w2a, b2a, gin_eps, w1b, b1b, g1, be1, m1, v1,
          w2b, b2b, g2, be2, m2, v2, out):
    x1_rows = nc.dram_tensor("x1_rows", [NP, D], FP32, kind="Internal").ap()
    src_pad = nc.dram_tensor("src_pad", [E + SLOTS, 1], I32, kind="Internal").ap()
    ctx = ExitStack()
    with ctx:
        def sb(name, shape, dt=FP32):
            return ctx.enter_context(nc.sbuf_tensor(name, shape, dt))

        def sem(name):
            return ctx.enter_context(nc.semaphore(name))

        ring = sb("ring", [P, RING * 2 * GROUP])
        edges = ring[:, :].rearrange("p (k h j f) -> p k h j f", k=RING, h=2, j=EPP)
        lo_hot = ring[:, :].bitcast(BF16).rearrange("p (b g l q) -> p b g l q", b=2, g=PAIRS // Q, l=P)
        index = sb("index", [P, 4, NG * EPP])
        dst_i = index[:, 0, :].bitcast(I32).rearrange("p (g j) -> p g j", j=EPP)
        src_i = index[:, 1, :].bitcast(I32).rearrange("p (g j) -> p g j", j=EPP)
        rel = index[:, 2, :].rearrange("p (g j) -> p g j", j=EPP)
        left = index[:, 3, :].rearrange("p (g j) -> p g j", j=EPP)
        PT = P * TILES // 2
        hi_hot = index[:, :, :].rearrange("p a c -> p (a c)")[:, 0:2 * PT].bitcast(BF16).rearrange(
            "p (b g h n) -> p b g h n", b=2, g=P // 8, h=TILES)
        acc = sb("acc", [P, 2, ACCW])
        counts16 = acc[:, 0, 0:2 * PT].bitcast(FP16).rearrange("p (b h n) -> p b h n", b=2, h=TILES)
        x16 = acc[:, 1, 0:NP].bitcast(FP16).rearrange("p (t a f) -> p t a f", t=TILES, a=2)
        xn = sb("xn", [P, TILES, D])
        zn = sb("zn", [P, TILES, D])
        scratch = zn[:, :, :].rearrange("p t f -> p (t f)")
        mlp = [scratch[:, 0:4 * BLK].rearrange("p (a c) -> p a c", a=4),
               ring[:, 0:4 * BLK].rearrange("p (a c) -> p a c", a=4)]
        onehot = sb("onehot", [P, NHOT, EPP, WIN])
        hotsum = sb("hotsum", [P, NHOT, WIN], BF16)
        seg = sb("seg", [WIN, 2, D])
        sources = sb("sources", [P, TILES, SLOTS], I32)
        xb = sb("xb", [P, BT, D])
        yn = sb("yn", [P, BT, D])
        stats = sb("stats", [P, BT, 6])
        mv = sb("mv", [P, BT, 2])
        std = sb("std", [P, BT])
        rstd = sb("rstd", [P, BT])
        hi_i = sb("hi_i", [P, 2, SLOTS], I32)
        lo_i = sb("lo_i", [P, 2, SLOTS], I32)
        valid = sb("valid", [P, 2, P], BF16)
        hi_m = sb("hi_m", [P, 2, P], BF16)
        lo_m = sb("lo_m", [P, 2, P], BF16)
        slot = sb("slot", [P, 2, PAIRS + P], BF16)
        lo_iota = sb("lo_iota", [P, P, Q], BF16)
        hi_iota = sb("hi_iota", [P, TILES, 8], BF16)
        slot_no = sb("slot_no", [P, 2, SLOTS])
        iota_i = scratch[:, 0:P * Q].bitcast(I32)
        win_no = sb("win_no", [P, WIN])
        ident = sb("ident", [P, P])
        ident16 = sb("ident16", [P, P], BF16)
        upper = sb("upper", [P, P])
        shift = sb("shift", [P, P])
        last_p = sb("last_p", [1, P])
        ones = sb("ones", [P, P])
        ones16 = sb("ones16", [P, P], BF16)
        pair_sel = sb("pair_sel", [P, PAIRS], BF16)
        part_no = sb("part_no", [P, 1], I32)
        parity_i = sb("parity_i", [P, 1], I32)
        parity = sb("parity", [P, 2])
        next_first = sb("next_first", [1, NG])
        disorder = sb("disorder", [P, 2])
        deg = sb("deg", [P, TILES])
        over = sb("over", [P, TILES])
        start_i = sb("start_i", [P, TILES], I32)
        totals = sb("totals", [TILES, P])
        bad = sb("bad", [P, 2])
        flags_i = sb("flags_i", [1, 2], I32)
        w1a_s = sb("w1a_s", [P, 3, HID])
        w2a_s = sb("w2a_s", [P, 2, D])
        w1b_s = sb("w1b_s", [P, D])
        w2b_s = sb("w2b_s", [P, D])
        COLS = ["b1a0", "b1a1", "u", "b1b", "g1", "be1", "m1", "v1"]
        cols = sb("cols", [P, len(COLS)])
        ROWS = ["b2b", "g2", "be2", "m2", "v2", "eps"]
        rows = sb("rows", [1, len(ROWS), D])
        bias0 = sb("bias0", [P, 2])
        fold = sb("fold", [P, 2])
        std1 = sb("std1", [P, 1])
        std2 = sb("std2", [1, D])
        rowf = sb("rowf", [1, 3, D])
        row_bc = sb("row_bc", [P, 3, D])
        one_eps = sb("one_eps", [P, 1])
        eps_col = sb("eps_col", [P, 1])
        cur = sb("cur", [P, EPP])
        gidx = sb("gidx", [P, EPP], I32)

        psB = [ctx.enter_context(nc.psum_tensor(f"psB{i}", [P, 2, 512], FP32)) for i in range(2)]
        psC = [ctx.enter_context(nc.psum_tensor(f"psC{i}", [P, 512], FP32)) for i in range(4)]
        seg_ps = [psB[0][:, 0, :], psB[0][:, 1, :]]
        turn_ps = [psB[1][:, 0, :], psB[1][:, 1, :]]
        hid_ps = [psB[0][:, 0, :], psB[0][:, 1, :], psB[1][:, 0, :], psB[1][:, 1, :]]

        def col(name):
            return cols[:, COLS.index(name):COLS.index(name) + 1]

        def row(name):
            return rows[0:1, ROWS.index(name), :]

        dst_in, x_in, weights_in, small_in, padded, stored, sources_in = (
            sem(n) for n in ("dst_in", "x_in", "weights_in", "small_in", "padded", "stored", "sources_in"))
        edges_in = [sem(f"edges_in{k}") for k in range(RING)]
        pool_made, dve_made, act_made, pe_made = (sem(n) for n in ("pool_made", "dve_made", "act_made", "pe_made"))
        onehot_ready, hotsum_ready, seg_mm, seg_copied, seg_turned, group_added = (
            sem(n) for n in ("onehot_ready", "hotsum_ready", "seg_mm", "seg_copied", "seg_turned", "group_added"))
        deg_step, total_mm, missed_ready, deg_final, totals_mm, totals_ready, start_mm, start_ready, bad_mm, \
            general_ready = (sem(n) for n in (
                "deg_step", "total_mm", "missed_ready", "deg_final", "totals_mm", "totals_ready", "start_mm",
                "start_ready", "bad_mm", "general_ready"))
        xb_ready, xT_mm, xT_ready, eT_ready, h_mm, h_ready, y_mm, y_read, resid_ready, stats_step, std_ready, normed, \
            hi_copied, lo_diff, split_done = (sem(n) for n in (
                "xb_ready", "xT_mm", "xT_ready", "eT_ready", "h_mm", "h_ready", "y_mm", "y_read", "resid_ready",
                "stats_step", "std_ready", "normed", "hi_copied", "lo_diff", "split_done"))
        slot_step, slot_mm, slot_ready, lo_ready, hi_ready, built, evacuated, summed, z_step, z_ready = (
            sem(n) for n in ("slot_step", "slot_mm", "slot_ready", "lo_ready", "hi_ready", "built", "evacuated",
                             "summed", "z_step", "z_ready"))
        src_in, x1_stored, idx_copied, table_ready, acc_staged = (
            sem(n) for n in ("src_in", "x1_stored", "idx_copied", "table_ready", "acc_staged"))
        SW = [{n: sem(f"sweep{layer}_{n}") for n in ("rows", "rows_seen", "moved", "hot", "sum", "mm", "copied", "turned", "added")}
              for layer in range(2)]

        stats_seen, idx_seen = sem("stats_seen"), sem("idx_seen")

        RING_GROUPS = 2 * RING
        TWO = 2
        ONE = 1

        def make_onehot(buf, table):
            return nc.vector.tensor_tensor(
                out=onehot[:, buf, :, :], in0=table.unsqueeze(2).to_broadcast([P, EPP, WIN]),
                in1=win_no[:, :].unsqueeze(1).to_broadcast([P, EPP, WIN]), op=ALU.is_equal)

        def sum_onehot(buf):
            with nc.allow_low_precision(reason="counts up to EPP are exact in bfloat16"):
                return nc.vector.tensor_reduce(
                    out=hotsum[:, buf, :], in_=onehot[:, buf, :, :].rearrange("p j w -> p w j"), axis=AX.X, op=ALU.add)

        def multiply(out_, buf, data):
            for j in range(EPP):
                last = nc.tensor.matmul(out_[0:WIN, 0:D], onehot[:, buf, j, :], data[:, j, :], start=(j == 0),
                                        stop=(j == EPP - 1))
            return last

        def turn(out_, rows_, buf):
            nc.tensor.matmul(out_[:, WIN:2 * WIN], ones16[:, :], hotsum[:, buf, :], start=True, stop=True)
            return nc.tensor.transpose(out_[:, 0:WIN], rows_, ident[0:WIN, 0:WIN])

        def add_group(base, turned, parts):
            span = acc[:, 0:parts, bass.ds(base, WIN)]
            return nc.vector.tensor_tensor(
                out=span, in0=span, in1=turned[:, 0:parts * WIN].rearrange("p (a w) -> p a w", a=parts), op=ALU.add)

        def group_of(table, g):
            return table[:, bass.ds(g, 1), :].rearrange("p g j -> p (g j)")

        last_edges = attr[E - GROUP:E, :].rearrange("(p j) f -> p j f", j=EPP)

        def sweep_pe(pe, s, rows_inc):
            with pe.Fori(0, NG) as g:
                pe.wait_ge(s["rows"], g * rows_inc + rows_inc)
                pe.sem_inc(s["rows_seen"], 1)
                with pe.Fori(0, SWEEP) as w:
                    step = g * SWEEP + w
                    pe.wait_ge(s["sum"], step + 1)
                    multiply(seg_ps[0], 0, edges[:, 0, 0, :, :]).then_inc(s["mm"], 1)
                    pe.wait_ge(s["copied"], step + 1)
                    turn(turn_ps[0], seg[:, 0, :], 0).then_inc(s["turned"], 1)

        def sweep_act(act, s):
            with act.Fori(0, NG * SWEEP) as step:
                act.wait_ge(s["mm"], step + 1 + ONE)
                nc.scalar.activation(seg[:, 0, :], seg_ps[0][0:WIN, 0:D], ACT.Copy).then_inc(s["copied"], 1)

        def sweep_dve(dve, s, parts, table):
            with dve.Fori(0, NG) as g:
                nc.vector.tensor_copy(cur[:, :], group_of(table, g)).then_inc(s["moved"], 1)
                with dve.Fori(0, SWEEP) as w:
                    step = g * SWEEP + w
                    dve.wait_ge(s["moved"], step + g + 1)
                    make_onehot(0, cur[:, :]).then_inc(s["hot"], 1)
                    dve.wait_ge(s["hot"], step + 1)
                    sum_onehot(0).then_inc(s["sum"], 1)
                    nc.vector.tensor_scalar(cur[:, :], cur[:, :], float(-WIN), None, ALU.add).then_inc(s["moved"], 1)
                    dve.wait_ge(s["turned"], step + 1)
                    add_group(w * WIN, turn_ps[0], parts).then_inc(s["added"], 1)
                    dve.wait_ge(s["added"], step + 1)
                dve.wait_ge(s["moved"], g * (SWEEP + 1) + SWEEP + 1)

        def mlp_pe(pe, n, layer):
            m = mlp[layer]
            pe.wait_ge(xb_ready, n + 1)
            for t in range(BT):
                last = nc.tensor.transpose(psC[t // 4][:, (t % 4) * P:(t % 4 + 1) * P], xb[:, t, :], ident[:, :])
            last.then_inc(xT_mm, 1)
            if layer == 0:
                pe.wait_ge(eT_ready, 3 * n + 3)
            pe.wait_ge(xT_ready, n + 1)
            units = 2 if layer == 0 else 1
            for half in range(2):
                for k in range(units):
                    cols_ = slice(half * HALF, (half + 1) * HALF)
                    out_ = hid_ps[2 * half + k][:, 0:HALF]
                    if layer == 0:
                        nc.tensor.matmul(out_, w1a_s[:, 0, k * P:(k + 1) * P], m[:, 0, cols_], start=True, stop=False)
                        last = nc.tensor.matmul(out_, w1a_s[:, 1, k * P:(k + 1) * P], m[:, 1, cols_], start=False,
                                                stop=True)
                    else:
                        last = nc.tensor.matmul(out_, w1b_s[:, :], m[:, 0, cols_], start=True, stop=True)
                    last.then_inc(h_mm, 1)
            pe.wait_ge(h_ready, 4 * n + 4 if layer == 0 else 2 * n + 2 * NBLK + 2)
            pe.wait_ge(y_read, n + ONE)
            for t in range(BT):
                out_ = psC[2 + t // 4][:, (t % 4) * D:(t % 4 + 1) * D]
                for k in range(units):
                    last = nc.tensor.matmul(out_, m[:, 2 + k, t * P:(t + 1) * P],
                                            w2a_s[:, k, :] if layer == 0 else w2n, start=(k == 0),
                                            stop=(k == units - 1))
            last.then_inc(y_mm, 1)

        w2n = w2b_s[:, :]

        def mlp_act(act, n, layer):
            m = mlp[layer]
            act.wait_ge(xT_mm, n + ONE + 1)
            nc.scalar.activation(m[:, 0, 0:4 * P], psC[0][:, :], ACT.Copy)
            nc.scalar.activation(m[:, 0, 4 * P:BLK], psC[1][:, 0:BLK - 4 * P], ACT.Copy).then_inc(xT_ready, 1)
            act.wait_ge(y_mm, n + ONE)
            units = 2 if layer == 0 else 1
            first = 4 * n if layer == 0 else 2 * n + 2 * NBLK
            for half in range(2):
                for k in range(units):
                    act.wait_ge(h_mm, first + half * units + k + ONE + 1)
                    out_ = m[:, 2 + k, half * HALF:(half + 1) * HALF]
                    in_ = hid_ps[2 * half + k][:, 0:HALF]
                    if layer == 0:
                        ins = nc.scalar.activation(out_, in_, ACT.Relu, bias=bias0[:, k:k + 1])
                    else:
                        ins = nc.scalar.activation(out_, in_, ACT.Relu, bias=fold[:, 1:2], scale=fold[:, 0:1])
                    ins.then_inc(h_ready, 1)
            act.wait_ge(stats_step, 3 * n + 2)
            nc.scalar.activation(std[:, :], mv[:, :, 1], ACT.Sqrt, bias=eps_col[:, :]).then_inc(std_ready, 1)

        def mlp_norm(dve, n, layer, dst_):
            dve.wait_ge(y_mm, n + ONE + 1)
            dve.wait_ge(resid_ready, n + 1)
            for bank, t0, t1 in ((2, 0, 4), (3, 4, BT)):
                y = psC[bank][:, 0:(t1 - t0) * D].rearrange("p (t f) -> p t f", f=D)
                if layer == 0:
                    ins = nc.vector.tensor_tensor(out=yn[:, t0:t1, :], in0=yn[:, t0:t1, :], in1=y, op=ALU.add)
                else:
                    ins = nc.vector.scalar_tensor_tensor(out=yn[:, t0:t1, :], in0=yn[:, t0:t1, :], scalar=2.0,
                                                         in1=y, op0=ALU.mult, op1=ALU.add)
            ins.then_inc(y_read, 1)
            dve.wait_ge(y_read, n + ONE + 1)
            for t in range(BT):
                last = nc.vector.bn_stats(stats[:, t, :], yn[:, t, :])
            last.then_inc(stats_step, 1)
            dve.wait_ge(stats_step, 3 * n + 1)
            dve.sem_inc(stats_seen, 1)
            for t in range(BT):
                last = nc.vector.bn_aggr(mv[:, t, :], stats[:, t, :])
            last.then_inc(stats_step, 1)
            dve.wait_ge(std_ready, n + 1)
            nc.vector.reciprocal(rstd[:, :], std[:, :]).then_inc(stats_step, 1)
            dve.wait_ge(stats_step, 3 * n + 3)
            for t in range(BT):
                last = nc.vector.tensor_scalar(dst_[:, t, :], yn[:, t, :], mv[:, t, 0:1], rstd[:, t:t + 1],
                                               ALU.subtract, ALU.mult)
            last.then_inc(normed, 1)

        def block_of(rows_, b):
            return rows_[:, bass.ds(b * BT, BT), :]

        def tile_masks(dve, t, tb):
            row_ = sources[:, bass.ds(t, 1), :].rearrange("p t s -> p (t s)")
            dve.wait_ge(slot_mm, t + 1)
            nc.vector.tensor_scalar(hi_i[:, tb, :], row_, 7, None, ALU.logical_shift_right).then_inc(slot_step, 1)
            nc.vector.tensor_scalar(lo_i[:, tb, :], row_, P - 1, None, ALU.bitwise_and).then_inc(slot_step, 1)
            nc.vector.tensor_scalar(valid[:, tb, :], slot_no[:, :, :].rearrange("p a s -> p (a s)"),
                                    deg[:, bass.ds(t, 1)], None, ALU.is_lt).then_inc(slot_step, 1)
            dve.wait_ge(slot_step, t * 5 + 3)
            v = valid[:, tb, :].rearrange("p (a s) -> p a s", a=2)
            nc.vector.scalar_tensor_tensor(
                out=hi_m[:, tb, :].rearrange("p (a s) -> p a s", a=2),
                in0=hi_i[:, tb, :].unsqueeze(1).to_broadcast([P, 2, SLOTS]), scalar=1.0, in1=v,
                op0=ALU.add, op1=ALU.mult).then_inc(slot_step, 1)
            nc.vector.tensor_tensor(
                out=lo_m[:, tb, :].rearrange("p (a s) -> p a s", a=2),
                in0=lo_i[:, tb, :].unsqueeze(1).to_broadcast([P, 2, SLOTS]), in1=v, op=ALU.mult
            ).then_inc(slot_step, 1)

        def tile_slots(pe, t, tb):
            pe.wait_ge(slot_step, 5 * t + 5)
            pe.wait_ge(slot_ready, t + ONE)
            nc.tensor.matmul(psC[0][:, 0:PAIRS], lo_m[:, tb, :], pair_sel[:, :], start=True, stop=True)
            nc.tensor.matmul(psC[0][:, PAIRS:PAIRS + P], hi_m[:, tb, :], ident16[:, :], start=True,
                             stop=True).then_inc(slot_mm, 1)

        def tile_slots_act(act, t, tb):
            act.wait_ge(slot_mm, t + TWO + 1)
            act.wait_ge(hi_ready, t + 1)
            nc.scalar.activation(slot[:, tb, :], psC[0][:, 0:PAIRS + P], ACT.Copy).then_inc(slot_ready, 1)

        def tile_onehots(dve, t, tb):
            dve.wait_ge(slot_ready, t + ONE + 1)
            dve.wait_ge(built, 8 * t + 8)
            nc.vector.tensor_tensor(
                out=lo_hot[:, tb, :, :, :],
                in0=slot[:, tb, 0:PAIRS].rearrange("p (g q) -> p g q", q=Q).unsqueeze(2).to_broadcast(
                    [P, PAIRS // Q, P, Q]),
                in1=lo_iota[:, :, :].unsqueeze(1).to_broadcast([P, PAIRS // Q, P, Q]),
                op=ALU.is_equal).then_inc(lo_ready, 1)
            nc.vector.tensor_tensor(
                out=hi_hot[:, tb, :, :, :],
                in0=slot[:, tb, PAIRS:PAIRS + P].rearrange("p (g n) -> p g n", n=8).unsqueeze(2).to_broadcast(
                    [P, P // 8, TILES, 8]),
                in1=hi_iota[:, :, :].unsqueeze(1).to_broadcast([P, P // 8, TILES, 8]),
                op=ALU.is_equal).then_inc(hi_ready, 1)

        def tile_build(pe, t, tb):
            pe.wait_ge(lo_ready, t + 1)
            pe.wait_ge(hi_ready, t + TWO + 1)
            for g in range(PAIRS // Q):
                pe.wait_ge(evacuated, 8 * t + g + 1)
                for k in range(Q):
                    last = nc.tensor.matmul(
                        psB[g % 2][:, k // 4, (k % 4) * 2 * TILES:(k % 4 + 1) * 2 * TILES],
                        lo_hot[:, tb, g, :, k],
                        hi_hot[:, tb, 2 * g + k // 4, :, (2 * k) % 8:(2 * k) % 8 + 2].rearrange("p h n -> p n h"),
                        start=True, stop=True)
                last.then_inc(built, 1)

        def tile_evacuate(act, t, tb):
            act.wait_ge(summed, t + 1)
            for g in range(PAIRS // Q):
                act.wait_ge(built, 8 * t + g + 1 + 2 * 8)
                nc.scalar.activation(
                    counts16[:, tb, :, 2 * Q * g:2 * Q * (g + 1)].rearrange("p h (g n) -> p g n h", g=2),
                    psB[g % 2][:, :, 0:8 * TILES].rearrange("p g (n h) -> p g n h", h=TILES),
                    ACT.Copy).then_inc(evacuated, 1)

        def tile_sum(pe, t, tb):
            pe.wait_ge(evacuated, TWO + 8 * t + 8)
            pe.wait_ge(z_ready, t + 1)
            for h in range(TILES):
                last = nc.tensor.matmul(psC[1 + tb][:, 0:2 * D], counts16[:, tb, h, :],
                                        x16[:, h, :, :].rearrange("p a f -> p (a f)"), start=(h == 0),
                                        stop=(h == TILES - 1))
            last.then_inc(summed, 1)

        def tile_of(rows_, t):
            return rows_[:, bass.ds(t, 1), :].rearrange("p t f -> p (t f)")

        def tile_z(dve, t, tb):
            dve.wait_ge(summed, TWO + t + 1)
            nc.vector.scalar_tensor_tensor(out=tile_of(zn, t), in0=tile_of(xn, t), scalar=one_eps[:, :],
                                           in1=psC[1 + tb][:, 0:D], op0=ALU.mult, op1=ALU.add).then_inc(z_step, 1)
            dve.wait_ge(z_step, t + 1)
            nc.vector.scalar_tensor_tensor(out=tile_of(zn, t), in0=psC[1 + tb][:, D:2 * D], scalar=1.0 / LOSCALE,
                                           in1=tile_of(zn, t), op0=ALU.mult, op1=ALU.add).then_inc(z_ready, 1)

        def over_tiles(eng, body):
            pairs = (TILES - 4) // 2
            for t in range(2):
                body(t, t)
            with eng.Fori(0, pairs) as i:
                for k in range(2):
                    body(i * 2 + (2 + k), k)
            for t in range(2 + 2 * pairs, TILES):
                body(t, t % 2)

        def is_tile(t):
            return not isinstance(t, int) or 0 <= t < TILES

        block = ctx.enter_context(nc.Block())

        @block.sync
        def _(sp):
            sp.dma_start(dst_i[:, 0:FULL, :],
                         dst[0:FULL * GROUP].rearrange("(g p j) -> p g j", p=P, j=EPP)).then_inc(dst_in, 16)
            sp.dma_start(dst_i[:, FULL, :], dst[E - GROUP:E].rearrange("(p j) -> p j", j=EPP)).then_inc(dst_in, 16)

            def load(k, u):
                sp.wait_ge(seg_mm, 2 * u + 2)
                sp.dma_start(edges[:, k, :, :, :],
                             attr[bass.ds(u * (2 * GROUP), 2 * GROUP), :].rearrange("(h p j) f -> p h j f", h=2, j=EPP)
                             ).then_inc(edges_in[k], 16)

            with sp.Fori(0, TURNS) as i:
                for k in range(RING):
                    load(k, i * RING + k)
            sp.wait_ge(seg_mm, 2 * (UNITS - 1) + 2)
            sp.dma_start(edges[:, 0, 0, :, :], attr[(FULL - 1) * GROUP:FULL * GROUP, :].rearrange(
                "(p j) f -> p j f", j=EPP)).then_inc(edges_in[0], 16)
            sp.dma_start(edges[:, 0, 1, :, :], last_edges).then_inc(edges_in[0], 16)

            sp.wait_ge(missed_ready, 1)
            missed = sp.value_load(flags_i[0:1, 0:1])
            with sp.If(missed != 0):
                s = SW[0]
                with sp.Fori(0, FULL) as g:
                    sp.wait_ge(s["mm"], g * SWEEP + ONE)
                    sp.dma_start(edges[:, 0, 0, :, :], attr[bass.ds(g * GROUP, GROUP), :].rearrange(
                        "(p j) f -> p j f", j=EPP)).then_inc(s["rows"], 16)
                sp.wait_ge(s["mm"], FULL * SWEEP + ONE)
                sp.dma_start(edges[:, 0, 0, :, :], last_edges).then_inc(s["rows"], 16)

            sp.wait_ge(general_ready, 1)
            general = sp.value_load(flags_i[0:1, 1:2])
            with sp.If(general != 0):
                sp.dma_start(src_i[:, 0:FULL, :],
                             src[0:FULL * GROUP].rearrange("(g p j) -> p g j", p=P, j=EPP)).then_inc(src_in, 16)
                sp.dma_start(src_i[:, FULL, :], src[E - GROUP:E].rearrange("(p j) -> p j", j=EPP)).then_inc(src_in, 16)
                sp.wait_ge(normed, NBLK + ONE)
                sp.dma_start(x1_rows.rearrange("(t p) f -> p t f", p=P), xn[:, :, :]).then_inc(x1_stored, 16)
                sp.wait_ge(src_in, 32)
                sp.wait_ge(x1_stored, 16)

            with sp.Fori(0, NBLK - 1) as b:
                sp.wait_ge(normed, NBLK + ONE + 1 + b)
                sp.dma_start(out[bass.ds(b * BLK, BLK), :].rearrange("(t p) f -> p t f", p=P),
                             block_of(zn, b)).then_inc(stored, 16)
            sp.wait_ge(normed, 2 * NBLK + ONE)
            sp.dma_start(out[(NBLK - 1) * BLK:(TILES - 1) * P, :].rearrange("(t p) f -> p t f", p=P),
                         zn[:, TILES - BT:TILES - 1, :]).then_inc(stored, 16)
            sp.dma_start(out[(TILES - 1) * P:N, :], zn[0:TAIL, TILES - 1, :]).then_inc(stored, 16)
            sp.wait_ge(stored, 16 * (NBLK + 1))

        @block.gpsimd
        def _(pool):
            made = [0]

            def step(ins):
                made[0] += 1
                ins.then_inc(pool_made, 1)
                pool.wait_ge(pool_made, made[0])

            step(nc.gpsimd.iota(part_no[:, :], [[0, 1]], base=0, channel_multiplier=1))
            step(nc.gpsimd.iota(iota_i[:, 0:WIN], [[1, WIN]], base=0, channel_multiplier=0))
            step(nc.gpsimd.tensor_copy(win_no[:, :], iota_i[:, 0:WIN]))
            step(nc.gpsimd.memset(ones[:, :], 1.0))
            step(nc.gpsimd.memset(ones16[:, :], 1.0))
            step(nc.gpsimd.affine_select(out=ident[:, :], in_=ones[:, :], compare_op=ALU.is_equal, fill=0.0, base=0,
                                         pattern=[[-1, P]], channel_multiplier=1))
            step(nc.gpsimd.affine_select(out=upper[:, :], in_=ones[:, :], compare_op=ALU.is_ge, fill=0.0, base=-1,
                                         pattern=[[1, P]], channel_multiplier=-1))
            step(nc.gpsimd.affine_select(out=shift[:, :], in_=ones[:, :], compare_op=ALU.is_equal, fill=0.0, base=-1,
                                         pattern=[[-1, P]], channel_multiplier=1))
            step(nc.gpsimd.affine_select(out=last_p[:, :], in_=ones[0:1, :], compare_op=ALU.is_ge, fill=0.0,
                                         base=-(P - 1), pattern=[[1, P]], channel_multiplier=0))
            assert made[0] == POOL_FIRST
            pool.wait_ge(dve_made, REL_MADE)
            step(nc.gpsimd.affine_select(out=rel[:, FULL, :], in_=rel[:, FULL, :], compare_op=ALU.is_ge,
                                         fill=-FAR, base=-REPEATS, pattern=[[1, EPP]], channel_multiplier=EPP))
            step(nc.gpsimd.affine_select(out=pair_sel[:, :], in_=ones16[:, 0:PAIRS], compare_op=ALU.is_ge, fill=0.0,
                                         base=0, pattern=[[-2, PAIRS]], channel_multiplier=1))
            step(nc.gpsimd.affine_select(out=pair_sel[:, :], in_=pair_sel[:, :], compare_op=ALU.is_ge, fill=0.0,
                                         base=1, pattern=[[2, PAIRS]], channel_multiplier=-1))
            step(nc.gpsimd.tensor_copy(ident16[:, :], ident[:, :]))
            step(nc.gpsimd.iota(iota_i[:, 0:P], [[0, 2], [1, SLOTS]], base=0, channel_multiplier=0))
            step(nc.gpsimd.tensor_copy(slot_no[:, :, :].rearrange("p a s -> p (a s)"), iota_i[:, 0:P]))
            pool.wait_ge(dve_made, PARITY_MADE)
            for a in range(2):
                step(nc.gpsimd.tensor_scalar(slot_no[:, a, :], slot_no[:, a, :], parity[:, a:a + 1], None, ALU.add))
            step(nc.gpsimd.iota(iota_i[:, :], [[1, P], [0, Q]], base=0, channel_multiplier=0))
            step(nc.gpsimd.tensor_copy(lo_iota[:, :, :].rearrange("p l q -> p (l q)"), iota_i[:, :]))
            step(nc.gpsimd.iota(iota_i[:, 0:TILES * 8], [[1, TILES], [0, 8]], base=1, channel_multiplier=0))
            step(nc.gpsimd.tensor_copy(hi_iota[:, :, :].rearrange("p h n -> p (h n)"), iota_i[:, 0:TILES * 8]))
            assert made[0] == POOL_MADE, made[0]

            def stage(rows_, b, n):
                pool.wait_ge(xT_mm, n + ONE)
                nc.gpsimd.tensor_copy(xb[:, :, :], block_of(rows_, b)).then_inc(xb_ready, 1)

            def residual(b, which):
                nc.gpsimd.tensor_tensor(
                    out=yn[:, :, :], in0=block_of(xn, b),
                    in1=row_bc[:, which, :].unsqueeze(1).to_broadcast([P, BT, D]), op=ALU.add
                ).then_inc(resid_ready, 1)

            pool.wait_ge(x_in, 32)
            pool.wait_ge(act_made, ROWS_SPREAD)
            pool.wait_ge(deg_final, 1)
            for b in range(NBLK):
                stage(xn, b, b)
                pool.wait_ge(split_done, b + ONE)
                residual(b, 0)
                if b == 0:
                    pool.wait_ge(padded, 48)
                    pool.wait_ge(start_ready, 1)
                for t in range(b * BT, (b + 1) * BT):
                    nc.gpsimd.indirect_dma_start(
                        sources[:, t, :], None, src_pad,
                        bass.IndirectOffsetOnAxis(start_i[:, t:t + 1].bitcast(U32), 0)).then_inc(sources_in, 16)

            pool.wait_ge(general_ready, 1)
            general = pool.value_load(flags_i[0:1, 1:2])
            with pool.If(general != 0):
                s = SW[1]
                pool.wait_ge(src_in, 32)
                pool.wait_ge(x1_stored, 16)
                with pool.Fori(0, NG) as g:
                    pool.wait_ge(s["mm"], g * SWEEP + ONE)
                    nc.gpsimd.tensor_copy(gidx[:, :], group_of(src_i, g)).then_inc(idx_copied, 1)
                    pool.wait_ge(idx_copied, g + 1)
                    pool.sem_inc(idx_seen, 1)
                    for j in range(EPP):
                        nc.gpsimd.indirect_dma_start(
                            edges[:, 0, 0, j, :], None, x1_rows,
                            bass.IndirectOffsetOnAxis(gidx[:, j:j + 1].bitcast(U32), 0)).then_inc(s["rows"], 16)
                    pool.wait_ge(s["rows"], g * (16 * EPP) + 16 * EPP)

            pool.wait_ge(z_ready, TWO + TILES)
            with pool.Fori(0, NBLK) as b:
                stage(zn, b, b + NBLK)
                pool.wait_ge(normed, b + NBLK + ONE)
                residual(b, 2)

        @block.scalar
        def _(act):
            act.sem_inc(seg_copied, TWO)
            act.sem_inc(split_done, ONE)
            act.sem_inc(slot_ready, ONE)
            act.sem_inc(evacuated, TWO)
            vectors = [(row("b2b"), b2b), (row("g2"), g2), (row("be2"), be2), (row("m2"), m2), (row("v2"), v2)]
            columns = [("b1b", b1b), ("g1", g1), ("be1", be1), ("m1", m1), ("v1", v1)]
            for dst_, src_ in vectors:
                act.dma_start(dst_, src_.rearrange("(o f) -> o f", o=1)).then_inc(small_in, 16)
            act.dma_start(rowf[0:1, 0, :], b2a.rearrange("(o f) -> o f", o=1)).then_inc(small_in, 16)
            act.dma_start(rows[0:1, ROWS.index("eps"), 0:1], gin_eps).then_inc(small_in, 16)
            for name, src_ in columns:
                act.dma_start(col(name), src_.rearrange("(p o) -> p o", o=1)).then_inc(small_in, 16)
            for k in range(2):
                act.dma_start(cols[:, k:k + 1], b1a[k * P:(k + 1) * P].rearrange("(p o) -> p o", o=1)
                              ).then_inc(small_in, 16)
            act.dma_start(col("u"), u[0, :].rearrange("(p o) -> p o", o=1)).then_inc(small_in, 16)
            act.dma_start(w1a_s[:, :, :], w1a.rearrange("(k p) n -> p k n", p=P)).then_inc(weights_in, 16)
            act.dma_start(w2a_s[:, :, :], w2a.rearrange("(k p) n -> p k n", p=P)).then_inc(weights_in, 16)
            act.dma_start(w1b_s[:, :], w1b).then_inc(weights_in, 16)
            act.dma_start(w2b_s[:, :], w2b).then_inc(weights_in, 16)
            act.wait_ge(dve_made, CLEARED)
            act.dma_start(xn[:, 0:TILES - 1, :],
                          x[0:(TILES - 1) * P, :].rearrange("(t p) f -> p t f", p=P)).then_inc(x_in, 16)
            act.dma_start(xn[0:TAIL, TILES - 1, :], x[(TILES - 1) * P:N, :]).then_inc(x_in, 16)
            act.dma_start(src_pad[0:FULL * GROUP, 0].rearrange("(p c) -> p c", p=P),
                          src[0:FULL * GROUP].rearrange("(p c) -> p c", p=P)).then_inc(padded, 16)
            act.dma_start(src_pad[FULL * GROUP:E, 0].rearrange("(o c) -> o c", o=1),
                          src[FULL * GROUP:E].rearrange("(o c) -> o c", o=1)).then_inc(padded, 16)
            act.dma_start(src_pad[E:E + SLOTS, 0].rearrange("(o c) -> o c", o=1),
                          src[0:SLOTS].rearrange("(o c) -> o c", o=1)).then_inc(padded, 16)

            act.wait_ge(small_in, 16 * SMALLS)
            act.wait_ge(dve_made, CLEARED)
            nc.scalar.activation(std1[:, :], col("v1"), ACT.Sqrt, bias=eps_col[:, :]).then_inc(act_made, 1)
            nc.scalar.activation(std2[:, :], row("v2"), ACT.Sqrt, bias=eps_col[0:1, :]).then_inc(act_made, 1)
            act.wait_ge(pe_made, PE_ROWS)
            nc.scalar.activation(row_bc[:, :, :].rearrange("p a f -> p (a f)"), psC[3][:, 0:3 * D],
                                 ACT.Copy).then_inc(act_made, 1)

            def copy_group(g, buf):
                act.wait_ge(seg_mm, g + RING_GROUPS + 1)
                act.wait_ge(seg_turned, g + 1 + NHOT - TWO)
                nc.scalar.activation(seg[:, buf, :], seg_ps[buf][0:WIN, 0:D], ACT.Copy).then_inc(seg_copied, 1)

            with act.Fori(0, NG // 2) as i:
                for k in range(2):
                    copy_group(i * 2 + k, k)

            act.wait_ge(missed_ready, 1)
            missed = act.value_load(flags_i[0:1, 0:1])
            with act.If(missed != 0):
                sweep_act(act, SW[0])

            act.wait_ge(totals_mm, 1)
            nc.scalar.activation(totals[:, :], psC[1][0:TILES, 0:P], ACT.Copy).then_inc(totals_ready, 1)

            with act.Fori(0, NBLK) as b:
                mlp_act(act, b, 0)
                act.wait_ge(normed, b + ONE + 1)
                high = x16[:, bass.ds(b * BT, BT), 0, :]
                nc.scalar.activation(high, block_of(xn, b), ACT.Copy).then_inc(hi_copied, 1)
                act.wait_ge(lo_diff, b + 1)
                nc.scalar.activation(x16[:, bass.ds(b * BT, BT), 1, :], yn[:, :, :], ACT.Copy,
                                     scale=LOSCALE).then_inc(split_done, 1)

            act.wait_ge(general_ready, 1)
            general = act.value_load(flags_i[0:1, 1:2])
            with act.If(general == 0):
                def body(t, tb):
                    tile_evacuate(act, t, tb)
                    if is_tile(t + 2):
                        tile_slots_act(act, t + 2, tb)

                for t in range(2):
                    tile_slots_act(act, t, t)
                over_tiles(act, body)
            with act.If(general != 0):
                sweep_act(act, SW[1])
                with act.Fori(0, TILES) as t:
                    act.wait_ge(summed, t + TWO)
                    act.wait_ge(SW[1]["added"], NG * SWEEP)
                    nc.scalar.activation(xb[:, 0, :], acc[:, 0, bass.ds(t * P, P)], ACT.Copy).then_inc(acc_staged, 1)

            with act.Fori(0, NBLK) as b:
                mlp_act(act, b + NBLK, 1)

        @block.vector
        def _(dve):
            dve.sem_inc(group_added, TWO)
            dve.sem_inc(y_read, ONE)
            dve.sem_inc(normed, ONE)
            dve.sem_inc(hi_ready, TWO)
            dve.sem_inc(z_ready, TWO)
            made = [0]

            def step(ins):
                made[0] += 1
                ins.then_inc(dve_made, 1)
                dve.wait_ge(dve_made, made[0])

            step(nc.vector.memset(eps_col[:, :], EPS))
            step(nc.vector.memset(xn[:, TILES - 1, :], 0.0))
            assert made[0] == CLEARED
            dve.wait_ge(pool_made, 1)
            step(nc.vector.tensor_scalar(parity_i[:, :], part_no[:, :], 1, None, ALU.bitwise_and))
            step(nc.vector.tensor_scalar(parity[:, 0:1], parity_i[:, :], FAR, None, ALU.mult))
            step(nc.vector.tensor_scalar(parity[:, 1:2], parity[:, 0:1], -1.0, FAR, ALU.mult, ALU.add))
            assert made[0] == PARITY_MADE
            dve.wait_ge(small_in, 16 * SMALLS)
            dve.wait_ge(act_made, 2)
            step(nc.vector.reciprocal(std2[:, :], std2[:, :]))
            step(nc.vector.tensor_tensor(out=rowf[0:1, 1, :], in0=row("g2"), in1=std2[:, :], op=ALU.mult))
            step(nc.vector.tensor_tensor(out=rowf[0:1, 2, :], in0=row("b2b"), in1=row("m2"), op=ALU.subtract))
            step(nc.vector.tensor_tensor(out=rowf[0:1, 2, :], in0=rowf[0:1, 2, :], in1=rowf[0:1, 1, :], op=ALU.mult))
            step(nc.vector.tensor_tensor(out=rowf[0:1, 2, :], in0=rowf[0:1, 2, :], in1=row("be2"), op=ALU.add))
            step(nc.vector.tensor_scalar(rowf[0:1, 2, :], rowf[0:1, 2, :], 0.5, None, ALU.mult))
            assert made[0] == ROWS_MADE, made[0]
            step(nc.vector.reciprocal(std1[:, :], std1[:, :]))
            step(nc.vector.tensor_tensor(out=fold[:, 0:1], in0=col("g1"), in1=std1[:, :], op=ALU.mult))
            step(nc.vector.tensor_tensor(out=fold[:, 1:2], in0=col("b1b"), in1=col("m1"), op=ALU.subtract))
            step(nc.vector.tensor_tensor(out=fold[:, 1:2], in0=fold[:, 1:2], in1=fold[:, 0:1], op=ALU.mult))
            step(nc.vector.tensor_tensor(out=fold[:, 1:2], in0=fold[:, 1:2], in1=col("be1"), op=ALU.add))
            step(nc.vector.memset(acc[:, :, :], 0.0))
            dve.wait_ge(dst_in, 32)
            step(nc.vector.tensor_copy(rel[:, :, :], dst_i[:, :, :]))
            step(nc.vector.memset(next_first[:, :], FAR))
            step(nc.vector.tensor_copy(next_first[0:1, 0:FULL - 1], dst_i[0:1, 1:FULL, 0]))
            assert made[0] == ABS_MADE
            dve.wait_ge(pe_made, PE_NEXT)
            step(nc.vector.tensor_tensor(out=rel[:, :, :], in0=rel[:, :, :],
                                         in1=psC[0][:, 0:NG].unsqueeze(2).to_broadcast([P, NG, EPP]),
                                         op=ALU.subtract))
            assert made[0] == REL_MADE

            def hot(g, buf):
                dve.wait_ge(seg_mm, g + RING_GROUPS - NHOT + 1)
                make_onehot(buf, group_of(rel, g)).then_inc(onehot_ready, 1)
                dve.wait_ge(onehot_ready, g + 1)
                dve.wait_ge(seg_turned, g + 1)
                sum_onehot(buf).then_inc(hotsum_ready, 1)

            def add(g, buf):
                base = dve.value_load(group_of(dst_i[0:1, :, :], g)[:, 0:1], min_val=0, max_val=N - 1)
                dve.wait_ge(seg_turned, g + 1 + NHOT)
                dve.wait_ge(group_added, g + TWO)
                add_group(base, turn_ps[buf], 2).then_inc(group_added, 1)

            dve.wait_ge(pool_made, POOL_FIRST + 1)
            for g in range(2):
                hot(g, g)

            dve.wait_ge(pe_made, PE_ROWS)
            step(nc.vector.tensor_tensor(out=bias0[:, :], in0=cols[:, 0:2], in1=psC[2][:, 0:2], op=ALU.add))
            step(nc.vector.tensor_scalar(one_eps[:, :], psC[2][:, 2:3], 1.0, None, ALU.add))
            dve.wait_ge(act_made, ROWS_SPREAD)
            dve.wait_ge(weights_in, 64)
            step(nc.vector.tensor_tensor(out=w2b_s[:, :], in0=w2b_s[:, :], in1=row_bc[:, 1, :], op=ALU.mult))

            def two_groups(first, k):
                hot(first + 2, (k + 2) % NHOT)
                add(first, k % 2)

            with dve.Fori(0, TURNS) as i:
                for k in range(RING_GROUPS):
                    two_groups(i * RING_GROUPS + k, k)
            for g in range(NG - 2, NG):
                add(g, g % 2)

            dve.wait_ge(pool_made, POOL_MADE)
            before = scratch[:, 0:NG * (EPP - 1)].rearrange("p (g j) -> p g j", j=EPP - 1)
            across = scratch[:, NG * (EPP - 1):NG * EPP]
            step(nc.vector.tensor_tensor(out=before, in0=dst_i[:, :, 0:EPP - 1], in1=dst_i[:, :, 1:EPP],
                                         op=ALU.is_gt))
            step(nc.vector.tensor_tensor(out=across, in0=dst_i[:, :, EPP - 1], in1=psC[1][:, 0:NG], op=ALU.is_gt))
            step(nc.vector.tensor_reduce(out=disorder[:, 0:1], in_=scratch[:, 0:NG * EPP], axis=AX.X, op=ALU.add))

            def degrees(done):
                dve.wait_ge(group_added, NG + TWO)
                with dve.Fori(0, NBLK) as b:
                    dve.wait_ge(deg_step, 2 * b + done + ONE)
                    nc.vector.tensor_tensor(
                        out=yn[:, :, :], in0=acc[:, 1, bass.ds(b * BLK, BLK)].rearrange("p (t f) -> p t f", f=P),
                        in1=ident[:, :].unsqueeze(1).to_broadcast([P, BT, P]), op=ALU.mult).then_inc(deg_step, 1)
                    dve.wait_ge(deg_step, 2 * b + 1 + done + ONE)
                    nc.vector.tensor_reduce(out=deg[:, bass.ds(b * BT, BT)], in_=yn[:, :, :], axis=AX.X,
                                            op=ALU.add).then_inc(deg_step, 1)

            dve.sem_inc(deg_step, ONE)
            degrees(0)
            dve.wait_ge(total_mm, 1)
            step(nc.vector.tensor_reduce(out=bad[:, 0:1], in_=psC[1][:, 0:TILES], axis=AX.X, op=ALU.add))
            step(nc.vector.tensor_scalar(bad[:, 0:1], bad[:, 0:1], float(E), None, ALU.subtract))
            nc.vector.tensor_copy(flags_i[0:1, 0:1], bad[0:1, 0:1]).then_inc(missed_ready, 1)

            table_steps = [0]

            def table_step(ins):
                table_steps[0] += 1
                ins.then_inc(table_ready, 1)
                dve.wait_ge(table_ready, table_steps[0])

            dve.wait_ge(missed_ready, 1)
            missed = dve.value_load(flags_i[0:1, 0:1])
            mask = scratch[:, 0:NG * EPP].rearrange("p (g j) -> p g j", j=EPP)
            with dve.If(missed != 0):
                table_step(nc.vector.tensor_scalar(mask, rel[:, :, :], 0.0, None, ALU.is_lt))
                table_step(nc.vector.scalar_tensor_tensor(out=mask, in0=rel[:, :, :], scalar=float(WIN), in1=mask,
                                                          op0=ALU.is_ge, op1=ALU.add))
                table_step(nc.vector.scalar_tensor_tensor(out=mask, in0=rel[:, :, :], scalar=-FAR, in1=mask,
                                                          op0=ALU.is_gt, op1=ALU.mult))
                table_step(nc.vector.tensor_copy(left[:, :, :], dst_i[:, :, :]))
                table_step(nc.vector.scalar_tensor_tensor(out=left[:, :, :], in0=left[:, :, :], scalar=1.0, in1=mask,
                                                          op0=ALU.add, op1=ALU.mult))
                table_step(nc.vector.tensor_scalar(left[:, :, :], left[:, :, :], -1.0, None, ALU.add))
                sweep_dve(dve, SW[0], 2, left)
                degrees(2 * NBLK)
                dve.wait_ge(deg_step, 4 * NBLK + ONE)
            dve.wait_ge(deg_step, 2 * NBLK + ONE)
            dve.wait_ge(missed_ready, 1)
            nc.vector.tensor_scalar(over[:, :], deg[:, :], float(SLOTS), None, ALU.is_gt).then_inc(deg_final, 1)
            dve.wait_ge(deg_final, 1)
            step(nc.vector.tensor_reduce(out=disorder[:, 1:2], in_=over[:, :], axis=AX.X, op=ALU.add))
            step(nc.vector.tensor_tensor(out=bad[:, 1:2], in0=disorder[:, 0:1], in1=disorder[:, 1:2], op=ALU.add))
            assert made[0] == BAD_MADE, made[0]
            dve.wait_ge(start_mm, 1)
            nc.vector.tensor_copy(start_i[:, :], psC[0][:, 0:TILES]).then_inc(start_ready, 1)
            dve.wait_ge(bad_mm, 1)
            nc.vector.tensor_copy(flags_i[0:1, 1:2], psC[1][0:1, 256:257]).then_inc(general_ready, 1)

            def edge_means(b):
                e = mlp[0][:, 1, :]
                dve.wait_ge(h_mm, 4 * b + ONE)
                nc.vector.tensor_scalar(e, acc[:, 1, bass.ds(b * BLK, BLK)], 1.0, None, ALU.max).then_inc(eT_ready, 1)
                dve.wait_ge(eT_ready, 3 * b + 1)
                nc.vector.reciprocal(e, e).then_inc(eT_ready, 1)
                dve.wait_ge(eT_ready, 3 * b + 2)
                nc.vector.tensor_tensor(out=e, in0=e, in1=acc[:, 0, bass.ds(b * BLK, BLK)],
                                        op=ALU.mult).then_inc(eT_ready, 1)

            def norm_and_split(b):
                mlp_norm(dve, b, 0, block_of(xn, b))
                dve.wait_ge(hi_copied, b + 1)
                nc.vector.tensor_tensor(out=yn[:, :, :], in0=block_of(xn, b), in1=x16[:, bass.ds(b * BT, BT), 0, :],
                                        op=ALU.subtract).then_inc(lo_diff, 1)

            dve.wait_ge(group_added, NG + TWO)
            edge_means(0)
            with dve.Fori(0, NBLK - 1) as b:
                edge_means(b + 1)
                norm_and_split(b)
            norm_and_split(NBLK - 1)

            dve.wait_ge(general_ready, 1)
            general = dve.value_load(flags_i[0:1, 1:2])
            with dve.If(general == 0):
                dve.wait_ge(sources_in, 16 * TILES)
                dve.wait_ge(pool_made, POOL_MADE)
                for t in range(2):
                    tile_masks(dve, t, t)
                tile_onehots(dve, 0, 0)

                def body(t, tb):
                    if is_tile(t + 2):
                        tile_masks(dve, t + 2, tb)
                    if is_tile(t + 1):
                        tile_onehots(dve, t + 1, 1 - tb)
                    if is_tile(t - 1):
                        tile_z(dve, t - 1, 1 - tb)

                over_tiles(dve, body)
                tile_z(dve, TILES - 1, 0)
            with dve.If(general != 0):
                nc.vector.memset(acc[:, 0, :], 0.0).then_inc(hi_ready, 1)
                nc.vector.tensor_scalar(mask, rel[:, :, :], -FAR, None, ALU.is_gt).then_inc(hi_ready, 1)
                nc.vector.tensor_copy(left[:, :, :], dst_i[:, :, :]).then_inc(hi_ready, 1)
                dve.wait_ge(hi_ready, TWO + 3)
                nc.vector.scalar_tensor_tensor(out=left[:, :, :], in0=left[:, :, :], scalar=1.0, in1=mask,
                                               op0=ALU.add, op1=ALU.mult).then_inc(hi_ready, 1)
                dve.wait_ge(hi_ready, TWO + 4)
                nc.vector.tensor_scalar(left[:, :, :], left[:, :, :], -1.0, None, ALU.add).then_inc(hi_ready, 1)
                dve.wait_ge(hi_ready, TWO + 5)
                sweep_dve(dve, SW[1], 1, left)
                with dve.Fori(0, TILES) as t:
                    dve.wait_ge(summed, t + TWO + 1)
                    nc.vector.scalar_tensor_tensor(
                        out=tile_of(zn, t), in0=tile_of(xn, t), scalar=one_eps[:, :], in1=psC[1][:, 0:D],
                        op0=ALU.mult, op1=ALU.add).then_inc(z_ready, 1)

            with dve.Fori(0, NBLK) as b:
                mlp_norm(dve, b + NBLK, 1, block_of(zn, b))

        @block.tensor
        def _(pe):
            pe.sem_inc(seg_mm, RING_GROUPS)
            pe.sem_inc(seg_turned, NHOT)
            pe.sem_inc(xT_mm, ONE)
            pe.sem_inc(y_mm, ONE)
            pe.sem_inc(h_mm, ONE)
            pe.sem_inc(slot_mm, TWO)
            pe.sem_inc(built, 2 * 8)
            pe.sem_inc(summed, TWO)
            for s in SW:
                pe.sem_inc(s["mm"], ONE)
            pe.wait_ge(pool_made, POOL_FIRST)
            pe.wait_ge(small_in, 16 * SMALLS)
            pe.wait_ge(weights_in, 64)
            pe.wait_ge(dve_made, ROWS_MADE)
            for k in range(2):
                nc.tensor.matmul(psC[2][:, k:k + 1], w1a_s[:, 2, k * P:(k + 1) * P], col("u"), start=True, stop=True)
            nc.tensor.matmul(psC[2][:, 2:3], ones[0:1, :], row("eps")[:, 0:1], start=True, stop=True)
            nc.tensor.matmul(psC[3][:, 0:3 * D], ones[0:1, :], rowf[:, :, :].rearrange("o a f -> o (a f)"),
                             start=True, stop=True).then_inc(pe_made, 1)
            pe.wait_ge(dve_made, ABS_MADE)
            nc.tensor.matmul(psC[0][:, 0:NG], ones[0:1, :], rel[0:1, :, 0], start=True, stop=True).then_inc(pe_made, 1)
            nc.tensor.matmul(psC[1][:, 0:NG], shift[:, :], rel[:, :, 0], start=True, stop=False)
            nc.tensor.matmul(psC[1][:, 0:NG], last_p[:, :], next_first[:, :], start=False, stop=True
                             ).then_inc(pe_made, 1)

            def products(g, k, h, buf):
                pe.wait_ge(onehot_ready, g + 1)
                pe.wait_ge(seg_copied, g + 1)
                multiply(seg_ps[buf % 2], buf, edges[:, k, h, :, :]).then_inc(seg_mm, 1)

            def turned(g, buf):
                pe.wait_ge(seg_copied, g + 1 + TWO)
                pe.wait_ge(hotsum_ready, g + 1)
                pe.wait_ge(group_added, g + 1)
                turn(turn_ps[buf % 2], seg[:, buf % 2, :], buf).then_inc(seg_turned, 1)

            def unit(i, k, first):
                pe.wait_ge(edges_in[k], i * 16 + 16)
                for h in range(2):
                    g = first + h
                    products(g, k, h, (2 * k + h) % NHOT)
                    if not (isinstance(g, int) and g == 0):
                        turned(g - 1, (2 * k + h - 1) % NHOT)

            for k in range(RING):
                unit(0, k, 2 * k)
            with pe.Fori(1, TURNS) as i:
                for k in range(RING):
                    unit(i, k, i * RING_GROUPS + 2 * k)
            pe.wait_ge(edges_in[0], TURNS * 16 + 32)
            for h in range(2):
                g = NG - 2 + h
                products(g, 0, h, g % NHOT)
                turned(g - 1, (g - 1) % NHOT)
            turned(NG - 1, (NG - 1) % NHOT)

            pe.wait_ge(deg_step, 2 * NBLK + ONE)
            pe.wait_ge(dve_made, DISORDER_MADE)
            nc.tensor.matmul(psC[1][:, 0:TILES], ones[:, :], deg[:, :], start=True, stop=True).then_inc(total_mm, 1)

            pe.wait_ge(missed_ready, 1)
            missed = pe.value_load(flags_i[0:1, 0:1])
            with pe.If(missed != 0):
                sweep_pe(pe, SW[0], 16)

            pe.wait_ge(deg_final, 1)
            nc.tensor.matmul(psC[1][0:TILES, 0:P], deg[:, :], ones[:, :], start=True, stop=True).then_inc(totals_mm, 1)
            pe.wait_ge(totals_ready, 1)
            nc.tensor.matmul(psC[0][:, 0:TILES], upper[:, :], deg[:, :], start=True, stop=False)
            nc.tensor.matmul(psC[0][:, 0:TILES], totals[:, :], upper[0:TILES, 0:TILES], start=False, stop=True
                             ).then_inc(start_mm, 1)
            pe.wait_ge(dve_made, BAD_MADE)
            nc.tensor.matmul(psC[1][:, 256:257], ones[:, :], bad[:, 1:2], start=True, stop=True).then_inc(bad_mm, 1)
            pe.wait_ge(start_ready, 1)
            pe.wait_ge(general_ready, 1)

            with pe.Fori(0, NBLK) as b:
                mlp_pe(pe, b, 0)

            general = pe.value_load(flags_i[0:1, 1:2])
            pe.wait_ge(split_done, NBLK + ONE)
            with pe.If(general == 0):
                for t in range(2):
                    tile_slots(pe, t, t)

                def body(t, tb):
                    tile_build(pe, t, tb)
                    if is_tile(t + 2):
                        tile_slots(pe, t + 2, tb)
                    if is_tile(t - 1):
                        tile_sum(pe, t - 1, 1 - tb)

                over_tiles(pe, body)
                tile_sum(pe, TILES - 1, 0)
            with pe.If(general != 0):
                sweep_pe(pe, SW[1], 16 * EPP)
                with pe.Fori(0, TILES) as t:
                    pe.wait_ge(acc_staged, t + 1)
                    pe.wait_ge(z_ready, t + TWO)
                    nc.tensor.transpose(psC[1][:, 0:P], xb[:, 0, :], ident[:, :]).then_inc(summed, 1)

            with pe.Fori(0, NBLK) as b:
                mlp_pe(pe, b + NBLK, 1)


_INS = ['x', 'src', 'dst', 'edge_attr_128', 'L0_gnn_u', 'L0_gnn_W1', 'L0_gnn_b1', 'L0_gnn_W2', 'L0_gnn_b2',
        'L1_gnn_eps', 'L1_gnn_W1', 'L1_gnn_b1', 'L1_gnn_g1', 'L1_gnn_beta1', 'L1_gnn_m1', 'L1_gnn_v1',
        'L1_gnn_W2', 'L1_gnn_b2', 'L1_gnn_g2', 'L1_gnn_beta2', 'L1_gnn_m2', 'L1_gnn_v2']


def kernel(**inputs):
    import numpy as _np
    import concourse.bacc as _bacc
    from concourse import mybir as _mybir
    from concourse.bass_utils import run_bass_kernel_spmd as _run

    nc = _bacc.Bacc("TRN2", target_bir_lowering=False, num_devices=1)
    arrays, args = {}, []
    for name in _INS:
        a = _np.ascontiguousarray(inputs[name])
        if a.ndim == 0:
            a = a.reshape(1, 1)
        arrays[f"in_{name}"] = a
        args.append(nc.dram_tensor(f"in_{name}", a.shape, _mybir.dt.from_np(a.dtype), kind="ExternalInput").ap())
    args.append(nc.dram_tensor("out_rows", (N, D), _mybir.dt.float32, kind="ExternalOutput").ap())
    build(nc, *args)
    r = _run(nc, [arrays], core_ids=[0])
    return r.results[0]["out_rows"]
```

```python
import concourse.bass as bass
from concourse import mybir
from contextlib import ExitStack

FP32 = mybir.dt.float32
BF16 = mybir.dt.bfloat16
FP16 = mybir.dt.float16
I32 = mybir.dt.int32
U32 = mybir.dt.uint32
ALU = mybir.AluOpType
ACT = mybir.ActivationFunctionType
AX = mybir.AxisListType

N = 6250
E = 206250
D = 128
P = 128
HID = 256
EPP = 8
GROUP = P * EPP
FULL = E // GROUP
NG = FULL + 1
REPEATS = GROUP - (E - FULL * GROUP)
WIN = 48
SWEEP = -(-N // WIN)
TILES = -(-N // P)
NP = TILES * P
TAIL = N - (TILES - 1) * P
ACCW = max(NP, N + WIN, SWEEP * WIN)
BT = 7
BLK = BT * P
NBLK = TILES // BT
HALF = BLK // 2
RING = 4
UNITS = NG // 2
TURNS = (UNITS - 1) // RING
NHOT = 4
SLOTS = 64
PAIRS = P // 2
Q = 8
LOSCALE = 2048.0
EPS = 1e-5
FAR = 100000.0
CLEARED, PARITY_MADE, ABS_ROWS, ABS_MADE, REL_MADE, ROWS_MADE, DISORDER_MADE, BAD_MADE = 2, 5, 8, 11, 12, 18, 29, 33
POOL_FIRST, POOL_MADE = 9, 21
PE_BASE, PE_NEXT, PE_ROWS = 1, 2, 3
ROWS_SPREAD = 3
SMALLS = 15
SLOTW = PAIRS + P
DEG_STEPS = -(-TILES // 4)
assert TILES % BT == 0 and TURNS * RING == UNITS - 1 and NG % 2 == 0 and 2 * SLOTS == P and TILES % 2 == 1


def build(nc, x, src, dst, attr, u, w1a, b1a, w2a, b2a, gin_eps, w1b, b1b, g1, be1, m1, v1,
          w2b, b2b, g2, be2, m2, v2, out):
    x1_rows = nc.dram_tensor("x1_rows", [NP, D], FP32, kind="Internal").ap()
    src_pad = nc.dram_tensor("src_pad", [E + SLOTS, 1], I32, kind="Internal").ap()
    ctx = ExitStack()
    with ctx:
        def sb(name, shape, dt=FP32):
            return ctx.enter_context(nc.sbuf_tensor(name, shape, dt))

        def sem(name):
            return ctx.enter_context(nc.semaphore(name))

        ring = sb("ring", [P, RING * 2 * GROUP])
        edges = ring[:, :].rearrange("p (k h j f) -> p k h j f", k=RING, h=2, j=EPP)
        lo_hot = ring[:, :].bitcast(BF16).rearrange("p (b g l q) -> p b g l q", b=2, g=PAIRS // Q, l=P)
        index = sb("index", [P, 4, NG * EPP])
        dst_f = index[:, 2, :].rearrange("p (g j) -> p g j", j=EPP)
        src_i = index[:, 1, :].bitcast(I32).rearrange("p (g j) -> p g j", j=EPP)
        rel = index[:, 3, :].rearrange("p (g j) -> p g j", j=EPP)
        left = index[:, 0, :].rearrange("p (g j) -> p g j", j=EPP)
        PT = P * TILES // 2
        hi_hot = index[:, :, :].rearrange("p a c -> p (a c)")[:, 0:2 * PT].bitcast(BF16).rearrange(
            "p (b g h n) -> p b g h n", b=2, g=P // 8, h=TILES)
        acc = sb("acc", [P, 2, ACCW])
        counts16 = acc[:, 0, 0:2 * PT].bitcast(FP16).rearrange("p (b h n) -> p b h n", b=2, h=TILES)
        x16 = acc[:, 1, 0:NP].bitcast(FP16).rearrange("p (t a f) -> p t a f", t=TILES, a=2)
        xn = sb("xn", [P, TILES, D])
        zn = sb("zn", [P, TILES, D])
        scratch = zn[:, :, :].rearrange("p t f -> p (t f)")
        mlp = ring[:, RING * GROUP:RING * GROUP + 4 * BLK].rearrange("p (a c) -> p a c", a=4)
        slot = scratch[:, NP - TILES * SLOTW // 2:NP].bitcast(BF16).rearrange("p (t w) -> p t w", w=SLOTW)
        dst_rows = scratch[:, P * Q:P * Q + 2 * GROUP].rearrange("p (h c) -> p h c", h=2)
        dst_in_i = scratch[:, P * Q + 2 * GROUP:P * Q + 4 * GROUP].bitcast(I32).rearrange("p (h c) -> p h c", h=2)
        onehot = sb("onehot", [P, NHOT, EPP, WIN])
        hotsum = sb("hotsum", [P, NHOT, WIN], BF16)
        seg = sb("seg", [WIN, 2, D])
        sources = sb("sources", [P, 2, BT, SLOTS], I32)
        xb = sb("xb", [P, BT, D])
        yn = sb("yn", [P, 2, BT, D])
        stats = sb("stats", [P, BT, 6])
        mv = sb("mv", [P, BT, 2])
        std = sb("std", [P, BT])
        rstd = sb("rstd", [P, BT])
        hi_i = sb("hi_i", [P, BT, SLOTS], I32)
        lo_i = sb("lo_i", [P, BT, SLOTS], I32)
        sums = sources[:, :, :, :].bitcast(FP32).rearrange("p b t s -> p (b t s)")[:, 0:4 * D].rearrange(
            "p (b c) -> p b c", b=2)
        valid = sb("valid", [P, BT, P], BF16)
        hi_m = sb("hi_m", [P, BT, P], BF16)
        lo_m = sb("lo_m", [P, BT, P], BF16)
        lo_iota = sb("lo_iota", [P, P, Q], BF16)
        hi_iota = sb("hi_iota", [P, TILES, 8], BF16)
        slot_no = sb("slot_no", [P, 2, SLOTS])
        iota_i = scratch[:, 0:P * Q].bitcast(I32)
        win_no = sb("win_no", [P, WIN])
        ident = sb("ident", [P, P])
        ident16 = sb("ident16", [P, P], BF16)
        upper = sb("upper", [P, P])
        shift = sb("shift", [P, P])
        last_p = sb("last_p", [1, P])
        ones = sb("ones", [P, P])
        ones16 = sb("ones16", [P, P], BF16)
        pair_sel = sb("pair_sel", [P, PAIRS], BF16)
        part_no = sb("part_no", [P, 1], I32)
        parity_i = sb("parity_i", [P, 1], I32)
        parity = sb("parity", [P, 2])
        next_first = sb("next_first", [1, NG])
        disorder = sb("disorder", [P, 2])
        deg = sb("deg", [P, TILES])
        rdeg = sb("rdeg", [P, TILES])
        first_i = sb("first_i", [1, NG], I32)
        over = sb("over", [P, TILES])
        start_i = sb("start_i", [P, TILES], I32)
        totals = sb("totals", [TILES, P])
        bad = sb("bad", [P, 2])
        flags_i = sb("flags_i", [1, 2], I32)
        w1a_s = sb("w1a_s", [P, 3, HID])
        w2a_s = sb("w2a_s", [P, 2, D])
        w1b_s = sb("w1b_s", [P, D])
        w2b_s = sb("w2b_s", [P, D])
        COLS = ["b1a0", "b1a1", "u", "b1b", "g1", "be1", "m1", "v1"]
        cols = sb("cols", [P, len(COLS)])
        ROWS = ["b2b", "g2", "be2", "m2", "v2", "eps"]
        rows = sb("rows", [1, len(ROWS), D])
        bias0 = sb("bias0", [P, 2])
        fold = sb("fold", [P, 2])
        std1 = sb("std1", [P, 1])
        std2 = sb("std2", [1, D])
        rowf = sb("rowf", [1, 3, D])
        row_bc = sb("row_bc", [P, 3, D])
        one_eps = sb("one_eps", [P, 1])
        eps_col = sb("eps_col", [P, 1])
        cur = sb("cur", [P, EPP])
        gidx = sb("gidx", [P, EPP], I32)

        psB = [ctx.enter_context(nc.psum_tensor(f"psB{i}", [P, 2, 512], FP32)) for i in range(2)]
        psC = [ctx.enter_context(nc.psum_tensor(f"psC{i}", [P, 512], FP32)) for i in range(4)]
        seg_ps = [psB[0][:, 0, :], psB[0][:, 1, :]]
        turn_ps = [psB[1][:, 0, :], psB[1][:, 1, :]]
        hid_ps = [psB[0][:, 0, :], psB[0][:, 1, :], psB[1][:, 0, :], psB[1][:, 1, :]]

        def col(name):
            return cols[:, COLS.index(name):COLS.index(name) + 1]

        def row(name):
            return rows[0:1, ROWS.index(name), :]

        dst_in, x_in, weights_in, small_in, padded, stored = (
            sem(n) for n in ("dst_in", "x_in", "weights_in", "small_in", "padded", "stored"))
        sources_in = [sem(f"sources_in{k}") for k in range(2)]
        edges_in = [sem(f"edges_in{k}") for k in range(RING)]
        pool_made, dve_made, act_made, pe_made = (sem(n) for n in ("pool_made", "dve_made", "act_made", "pe_made"))
        onehot_ready, hotsum_ready, seg_mm, seg_copied, seg_turned, group_added = (
            sem(n) for n in ("onehot_ready", "hotsum_ready", "seg_mm", "seg_copied", "seg_turned", "group_added"))
        deg_mm, deg_read, total_mm, missed_ready, deg_final, totals_mm, totals_ready, start_mm, start_ready, bad_mm, \
            general_ready, rdeg_ready, spread_mm, spread_done, rows_turned, rows_read = (sem(n) for n in (
                "deg_mm", "deg_read", "total_mm", "missed_ready", "deg_final", "totals_mm", "totals_ready", "start_mm",
                "start_ready", "bad_mm", "general_ready", "rdeg_ready", "spread_mm", "spread_done", "rows_turned",
                "rows_read"))
        xb_ready, xT_mm, xT_ready, eT_ready, h_mm, h_ready, y_mm, y_read, resid_ready, stats_step, std_ready, normed, \
            hi_copied, lo_diff, split_done = (sem(n) for n in (
                "xb_ready", "xT_mm", "xT_ready", "eT_ready", "h_mm", "h_ready", "y_mm", "y_read", "resid_ready",
                "stats_step", "std_ready", "normed", "hi_copied", "lo_diff", "split_done"))
        mask_step, masks_made, slot_mm, slot_ready, lo_ready, hi_ready, built, evacuated, summed, z_ready = (
            sem(n) for n in ("mask_step", "masks_made", "slot_mm", "slot_ready", "lo_ready", "hi_ready", "built", "evacuated",
                             "summed", "z_ready"))
        acc_zero, sums_ready, general_z = (sem(n) for n in ("acc_zero", "sums_ready", "general_z"))
        sums_added = sem("sums_added")
        src_in, x1_stored, idx_copied, table_ready, table1_ready, acc_staged = (
            sem(n) for n in ("src_in", "x1_stored", "idx_copied", "table_ready", "table1_ready", "acc_staged"))
        SW = [{n: sem(f"sweep{layer}_{n}") for n in ("rows", "rows_seen", "moved", "hot", "sum", "mm", "copied", "turned", "added")}
              for layer in range(2)]

        stats_seen, idx_seen = sem("stats_seen"), sem("idx_seen")

        RING_GROUPS = 2 * RING
        TWO = 2
        ONE = 1

        def make_onehot(buf, table):
            return nc.vector.tensor_tensor(
                out=onehot[:, buf, :, :], in0=table.unsqueeze(2).to_broadcast([P, EPP, WIN]),
                in1=win_no[:, :].unsqueeze(1).to_broadcast([P, EPP, WIN]), op=ALU.is_equal)

        def sum_onehot(buf):
            with nc.allow_low_precision(reason="counts up to EPP are exact in bfloat16"):
                return nc.vector.tensor_reduce(
                    out=hotsum[:, buf, :], in_=onehot[:, buf, :, :].rearrange("p j w -> p w j"), axis=AX.X, op=ALU.add)

        def multiply(out_, buf, data):
            for j in range(EPP):
                last = nc.tensor.matmul(out_[0:WIN, 0:D], onehot[:, buf, j, :], data[:, j, :], start=(j == 0),
                                        stop=(j == EPP - 1))
            return last

        def turn(out_, rows_, buf):
            nc.tensor.matmul(out_[:, WIN:2 * WIN], ones16[:, :], hotsum[:, buf, :], start=True, stop=True)
            return nc.tensor.transpose(out_[:, 0:WIN], rows_, ident[0:WIN, 0:WIN])

        def add_group(base, turned, parts):
            span = acc[:, 0:parts, bass.ds(base, WIN)]
            return nc.vector.tensor_tensor(
                out=span, in0=span, in1=turned[:, 0:parts * WIN].rearrange("p (a w) -> p a w", a=parts), op=ALU.add)

        def group_of(table, g):
            return table[:, bass.ds(g, 1), :].rearrange("p g j -> p (g j)")

        last_edges = attr[E - GROUP:E, :].rearrange("(p j) f -> p j f", j=EPP)

        def sweep_pe(pe, s, rows_inc):
            with pe.Fori(0, NG) as g:
                pe.wait_ge(s["rows"], g * rows_inc + rows_inc)
                pe.sem_inc(s["rows_seen"], 1)
                with pe.Fori(0, SWEEP) as w:
                    step = g * SWEEP + w
                    pe.wait_ge(s["sum"], step + 1)
                    multiply(seg_ps[0], 0, edges[:, 0, 0, :, :]).then_inc(s["mm"], 1)
                    pe.wait_ge(s["copied"], step + 1)
                    turn(turn_ps[0], seg[:, 0, :], 0).then_inc(s["turned"], 1)

        def sweep_act(act, s):
            with act.Fori(0, NG * SWEEP) as step:
                act.wait_ge(s["mm"], step + 1 + ONE)
                nc.scalar.activation(seg[:, 0, :], seg_ps[0][0:WIN, 0:D], ACT.Copy).then_inc(s["copied"], 1)

        def sweep_dve(dve, s, parts, table):
            with dve.Fori(0, NG) as g:
                nc.vector.tensor_copy(cur[:, :], group_of(table, g)).then_inc(s["moved"], 1)
                with dve.Fori(0, SWEEP) as w:
                    step = g * SWEEP + w
                    dve.wait_ge(s["moved"], step + g + 1)
                    make_onehot(0, cur[:, :]).then_inc(s["hot"], 1)
                    dve.wait_ge(s["hot"], step + 1)
                    sum_onehot(0).then_inc(s["sum"], 1)
                    nc.vector.tensor_scalar(cur[:, :], cur[:, :], float(-WIN), None, ALU.add).then_inc(s["moved"], 1)
                    dve.wait_ge(s["turned"], step + 1)
                    add_group(w * WIN, turn_ps[0], parts).then_inc(s["added"], 1)
                    dve.wait_ge(s["added"], step + 1)
                dve.wait_ge(s["moved"], g * (SWEEP + 1) + SWEEP + 1)

        def mlp_turn(pe, n):
            pe.wait_ge(xb_ready, n + 1)
            for t in range(BT):
                last = nc.tensor.transpose(psC[t // 4][:, (t % 4) * P:(t % 4 + 1) * P], xb[:, t, :], ident[:, :])
            last.then_inc(xT_mm, 1)

        def mlp_hidden(pe, n, layer, buf=0):
            pe.wait_ge(xT_ready, n + 1)
            if layer == 0:
                pe.wait_ge(slot_ready, n + 1)
                pe.wait_ge(eT_ready, n + 1)
            for half in range(2):
                for k in range(2 - layer):
                    cols_ = slice(half * HALF, (half + 1) * HALF)
                    out_ = hid_ps[2 * half + k + buf][:, 0:HALF]
                    if layer == 0:
                        nc.tensor.matmul(out_, w1a_s[:, 0, k * P:(k + 1) * P], mlp[:, 0, cols_], start=True,
                                         stop=False)
                        last = nc.tensor.matmul(out_, w1a_s[:, 1, k * P:(k + 1) * P], mlp[:, 1, cols_], start=False,
                                                stop=True)
                    else:
                        last = nc.tensor.matmul(out_, w1b_s[:, :], mlp[:, 0, cols_], start=True, stop=True)
                    last.then_inc(h_mm, 1)

        def mlp_out(pe, n, layer, buf=0):
            pe.wait_ge(y_read, n + ONE)
            for t in range(BT):
                out_ = psC[2 + t // 4][:, (t % 4) * D:(t % 4 + 1) * D]
                for k in range(2 - layer):
                    last = nc.tensor.matmul(out_, mlp[:, 2 + k + buf, t * P:(t + 1) * P],
                                            w2a_s[:, k, :] if layer == 0 else w2n, start=(k == 0),
                                            stop=(k == 1 - layer))
            last.then_inc(y_mm, 1)

        def wait_hidden(pe, n, layer):
            pe.wait_ge(h_ready, 4 * n + 4 if layer == 0 else 2 * n + 2 * NBLK + 2)

        w2n = w2b_s[:, :]

        def mlp_turn_act(act, n):
            act.wait_ge(xT_mm, n + ONE + 1)
            nc.scalar.activation(mlp[:, 0, 0:4 * P], psC[0][:, :], ACT.Copy)
            nc.scalar.activation(mlp[:, 0, 4 * P:BLK], psC[1][:, 0:BLK - 4 * P], ACT.Copy).then_inc(xT_ready, 1)

        def mlp_relu(act, n, layer, buf=0):
            act.wait_ge(y_mm, n + ONE - layer)
            units = 2 - layer
            first = 4 * n if layer == 0 else 2 * n + 2 * NBLK
            for half in range(2):
                for k in range(units):
                    act.wait_ge(h_mm, first + half * units + k + ONE + 1)
                    out_ = mlp[:, 2 + k + buf, half * HALF:(half + 1) * HALF]
                    in_ = hid_ps[2 * half + k + buf][:, 0:HALF]
                    if layer == 0:
                        ins = nc.scalar.activation(out_, in_, ACT.Relu, bias=bias0[:, k:k + 1])
                    else:
                        ins = nc.scalar.activation(out_, in_, ACT.Relu, bias=fold[:, 1:2], scale=fold[:, 0:1])
                    ins.then_inc(h_ready, 1)

        def mlp_std(act, n):
            act.wait_ge(stats_step, 3 * n + 2)
            nc.scalar.activation(std[:, :], mv[:, :, 1], ACT.Sqrt, bias=eps_col[:, :]).then_inc(std_ready, 1)

        def mlp_norm(dve, n, layer, buf, dst_):
            yb = yn[:, buf, :, :]
            dve.wait_ge(y_mm, n + ONE + 1)
            dve.wait_ge(resid_ready, n + 1)
            for bank, t0, t1 in ((2, 0, 4), (3, 4, BT)):
                y = psC[bank][:, 0:(t1 - t0) * D].rearrange("p (t f) -> p t f", f=D)
                if layer == 0:
                    ins = nc.vector.tensor_tensor(out=yb[:, t0:t1, :], in0=yb[:, t0:t1, :], in1=y, op=ALU.add)
                else:
                    ins = nc.vector.scalar_tensor_tensor(out=yb[:, t0:t1, :], in0=yb[:, t0:t1, :], scalar=2.0,
                                                         in1=y, op0=ALU.mult, op1=ALU.add)
            ins.then_inc(y_read, 1)
            dve.wait_ge(y_read, n + ONE + 1)
            for t in range(BT):
                last = nc.vector.bn_stats(stats[:, t, :], yb[:, t, :])
            last.then_inc(stats_step, 1)
            dve.wait_ge(stats_step, 3 * n + 1)
            dve.sem_inc(stats_seen, 1)
            for t in range(BT):
                last = nc.vector.bn_aggr(mv[:, t, :], stats[:, t, :])
            last.then_inc(stats_step, 1)
            dve.wait_ge(std_ready, n + 1)
            nc.vector.reciprocal(rstd[:, :], std[:, :]).then_inc(stats_step, 1)
            dve.wait_ge(stats_step, 3 * n + 3)
            for t in range(BT):
                last = nc.vector.tensor_scalar(dst_[:, t, :], yb[:, t, :], mv[:, t, 0:1], rstd[:, t:t + 1],
                                               ALU.subtract, ALU.mult)
            last.then_inc(normed, 1)

        def block_of(rows_, b):
            return rows_[:, bass.ds(b * BT, BT), :]

        def block_masks(dve, b, buf, turn_no):
            m = b * 3
            dve.wait_ge(sources_in[buf], turn_no * (16 * BT) + 16 * BT)
            dve.wait_ge(slot_mm, b + ONE)
            nc.vector.tensor_scalar(hi_i[:, :, :], sources[:, buf, :, :], 7, None, ALU.logical_shift_right
                                    ).then_inc(mask_step, 1)
            nc.vector.tensor_scalar(lo_i[:, :, :], sources[:, buf, :, :], P - 1, None, ALU.bitwise_and
                                    ).then_inc(mask_step, 1)
            nc.vector.tensor_tensor(
                out=valid[:, :, :], in0=slot_no[:, :, :].rearrange("p a s -> p (a s)").unsqueeze(1).to_broadcast(
                    [P, BT, P]),
                in1=deg[:, bass.ds(b * BT, BT)].unsqueeze(2).to_broadcast([P, BT, P]), op=ALU.is_lt
            ).then_inc(mask_step, 1)
            dve.wait_ge(mask_step, m + 3)
            for a in range(2):
                half = slice(a * SLOTS, (a + 1) * SLOTS)
                nc.vector.scalar_tensor_tensor(out=hi_m[:, :, half], in0=hi_i[:, :, :], scalar=1.0,
                                               in1=valid[:, :, half], op0=ALU.add, op1=ALU.mult)
                last = nc.vector.tensor_tensor(out=lo_m[:, :, half], in0=lo_i[:, :, :], in1=valid[:, :, half],
                                               op=ALU.mult)
            last.then_inc(masks_made, 1)

        def block_slots(pe, b):
            pe.wait_ge(masks_made, b + 1)
            for t in range(BT):
                out_ = hid_ps[t // 2][:, (t % 2) * SLOTW:(t % 2 + 1) * SLOTW]
                nc.tensor.matmul(out_[:, 0:PAIRS], lo_m[:, t, :], pair_sel[:, :], start=True, stop=True)
                last = nc.tensor.matmul(out_[:, PAIRS:SLOTW], hi_m[:, t, :], ident16[:, :], start=True, stop=True)
            last.then_inc(slot_mm, 1)

        def block_slots_act(act, b):
            act.wait_ge(slot_mm, b + ONE + 1)
            for bank in range(4):
                n = min(2, BT - 2 * bank)
                last = nc.scalar.activation(
                    slot[:, bass.ds(b * BT + 2 * bank, n), :],
                    hid_ps[bank][:, 0:n * SLOTW].rearrange("p (t w) -> p t w", w=SLOTW), ACT.Copy)
            last.then_inc(slot_ready, 1)

        def tile_onehots(dve, t, tb):
            dve.wait_ge(built, 8 * t + 8)
            nc.vector.tensor_tensor(
                out=lo_hot[:, tb, :, :, :],
                in0=tile_of(slot, t)[:, 0:PAIRS].rearrange("p (g q) -> p g q", q=Q).unsqueeze(2).to_broadcast(
                    [P, PAIRS // Q, P, Q]),
                in1=lo_iota[:, :, :].unsqueeze(1).to_broadcast([P, PAIRS // Q, P, Q]),
                op=ALU.is_equal).then_inc(lo_ready, 1)
            nc.vector.tensor_tensor(
                out=hi_hot[:, tb, :, :, :],
                in0=tile_of(slot, t)[:, PAIRS:SLOTW].rearrange("p (g n) -> p g n", n=8).unsqueeze(2).to_broadcast(
                    [P, P // 8, TILES, 8]),
                in1=hi_iota[:, :, :].unsqueeze(1).to_broadcast([P, P // 8, TILES, 8]),
                op=ALU.is_equal).then_inc(hi_ready, 1)

        def tile_build(pe, t, tb, also=None):
            pe.wait_ge(lo_ready, t + 1)
            pe.wait_ge(hi_ready, t + TWO + 1)
            for g in range(PAIRS // Q):
                pe.wait_ge(evacuated, 8 * t + g + 1)
                for k in range(Q):
                    last = nc.tensor.matmul(
                        psB[g % 2][:, k // 4, (k % 4) * 2 * TILES:(k % 4 + 1) * 2 * TILES],
                        lo_hot[:, tb, g, :, k],
                        hi_hot[:, tb, 2 * g + k // 4, :, (2 * k) % 8:(2 * k) % 8 + 2].rearrange("p h n -> p n h"),
                        start=True, stop=True)
                last.then_inc(built, 1)
                if also is not None and g:
                    also(g)

        def tile_evacuate(act, t, tb):
            act.wait_ge(summed, t + 1)
            for g in range(PAIRS // Q):
                act.wait_ge(built, 8 * t + g + 1 + 2 * 8)
                nc.scalar.activation(
                    counts16[:, tb, :, 2 * Q * g:2 * Q * (g + 1)].rearrange("p h (g n) -> p g n h", g=2),
                    psB[g % 2][:, :, 0:8 * TILES].rearrange("p g (n h) -> p g n h", h=TILES),
                    ACT.Copy).then_inc(evacuated, 1)

        SUM_STEP = TILES // (PAIRS // Q - 1)

        def tile_sum(pe, t, tb, part=None):
            if part in (None, 1):
                pe.wait_ge(evacuated, TWO + 8 * t + 8)
                if not (isinstance(t, int) and t < 2):
                    pe.wait_ge(sums_ready, t - 1)
            steps = range(TILES) if part is None else range((part - 1) * SUM_STEP, part * SUM_STEP)
            for h in steps:
                last = nc.tensor.matmul(psC[2 + tb][:, 0:2 * D], counts16[:, tb, h, :],
                                        x16[:, h, :, :].rearrange("p a f -> p (a f)"), start=(h == 0),
                                        stop=(h == TILES - 1))
            if steps[-1] == TILES - 1:
                last.then_inc(summed, 1)

        def tile_of(rows_, t):
            return rows_[:, bass.ds(t, 1), :].rearrange("p t f -> p (t f)")

        def tile_sums_act(act, t, tb):
            act.wait_ge(summed, TWO + t + 1)
            act.wait_ge(z_ready, t + 1)
            nc.scalar.activation(sums[:, tb, 0:D], psC[2 + tb][:, 0:D], ACT.Copy)
            nc.scalar.activation(sums[:, tb, D:2 * D], psC[2 + tb][:, D:2 * D], ACT.Copy,
                                 scale=1.0 / LOSCALE).then_inc(sums_ready, 1)

        def tile_sums_pool(pool, t, tb):
            pool.wait_ge(sums_ready, t + 1)
            nc.gpsimd.tensor_tensor(out=sums[:, tb, 0:D], in0=sums[:, tb, 0:D], in1=sums[:, tb, D:2 * D],
                                    op=ALU.add).then_inc(sums_added, 1)

        def tile_z(dve, t, tb):
            dve.wait_ge(sums_added, t + 1)
            nc.vector.scalar_tensor_tensor(out=tile_of(zn, t), in0=tile_of(xn, t), scalar=one_eps[:, :],
                                           in1=sums[:, tb, 0:D], op0=ALU.mult, op1=ALU.add).then_inc(z_ready, 1)

        def not_number_or(b, test):
            return not isinstance(b, int) or test(b)

        def over_blocks(eng, body):
            body(0, 0, 0)
            with eng.Fori(0, (NBLK - 3) // 2) as i:
                body(i * 2 + 1, 1, i)
                body(i * 2 + 2, 0, i + 1)
            for b in range(NBLK - 2, NBLK):
                body(b, b % 2, b // 2)

        def over_tiles(eng, body):
            pairs = (TILES - 4) // 2
            for t in range(2):
                body(t, t)
            with eng.Fori(0, pairs) as i:
                for k in range(2):
                    body(i * 2 + (2 + k), k)
            for t in range(2 + 2 * pairs, TILES):
                body(t, t % 2)

        def is_tile(t):
            return not isinstance(t, int) or 0 <= t < TILES

        block = ctx.enter_context(nc.Block())

        @block.sync
        def _(sp):
            sp.dma_start(dst_in_i[:, 0, :], dst[0:P * GROUP].rearrange("(g c) -> g c", g=P)).then_inc(dst_in, 16)
            sp.dma_start(dst_in_i[0:FULL - P, 1, :],
                         dst[P * GROUP:FULL * GROUP].rearrange("(g c) -> g c", c=GROUP)).then_inc(dst_in, 16)
            sp.dma_start(dst_in_i[FULL - P:NG - P, 1, :],
                         dst[E - GROUP:E].rearrange("(g c) -> g c", g=1)).then_inc(dst_in, 16)

            def load(k, u):
                sp.wait_ge(seg_mm, 2 * u + 2)
                sp.dma_start(edges[:, k, :, :, :],
                             attr[bass.ds(u * (2 * GROUP), 2 * GROUP), :].rearrange("(h p j) f -> p h j f", h=2, j=EPP)
                             ).then_inc(edges_in[k], 16)

            with sp.Fori(0, TURNS) as i:
                for k in range(RING):
                    load(k, i * RING + k)
            sp.wait_ge(seg_mm, 2 * (UNITS - 1) + 2)
            sp.dma_start(edges[:, 0, 0, :, :], attr[(FULL - 1) * GROUP:FULL * GROUP, :].rearrange(
                "(p j) f -> p j f", j=EPP)).then_inc(edges_in[0], 16)
            sp.dma_start(edges[:, 0, 1, :, :], last_edges).then_inc(edges_in[0], 16)

            sp.wait_ge(missed_ready, 1)
            missed = sp.value_load(flags_i[0:1, 0:1])
            with sp.If(missed != 0):
                s = SW[0]
                with sp.Fori(0, FULL) as g:
                    sp.wait_ge(s["mm"], g * SWEEP + ONE)
                    sp.dma_start(edges[:, 0, 0, :, :], attr[bass.ds(g * GROUP, GROUP), :].rearrange(
                        "(p j) f -> p j f", j=EPP)).then_inc(s["rows"], 16)
                sp.wait_ge(s["mm"], FULL * SWEEP + ONE)
                sp.dma_start(edges[:, 0, 0, :, :], last_edges).then_inc(s["rows"], 16)

            sp.wait_ge(general_ready, 1)
            general = sp.value_load(flags_i[0:1, 1:2])
            with sp.If(general != 0):
                sp.wait_ge(hi_ready, TWO + 1)
                sp.dma_start(src_i[:, 0:FULL, :],
                             src[0:FULL * GROUP].rearrange("(g p j) -> p g j", p=P, j=EPP)).then_inc(src_in, 16)
                sp.dma_start(src_i[:, FULL, :], src[E - GROUP:E].rearrange("(p j) -> p j", j=EPP)).then_inc(src_in, 16)
                sp.wait_ge(normed, NBLK + ONE)
                sp.dma_start(x1_rows.rearrange("(t p) f -> p t f", p=P), xn[:, :, :]).then_inc(x1_stored, 16)
                sp.wait_ge(src_in, 32)
                sp.wait_ge(x1_stored, 16)

            with sp.Fori(0, NBLK - 1) as b:
                sp.wait_ge(normed, NBLK + ONE + 1 + b)
                sp.dma_start(out[bass.ds(b * BLK, BLK), :].rearrange("(t p) f -> p t f", p=P),
                             block_of(zn, b)).then_inc(stored, 16)
            sp.wait_ge(normed, 2 * NBLK + ONE)
            sp.dma_start(out[(NBLK - 1) * BLK:(TILES - 1) * P, :].rearrange("(t p) f -> p t f", p=P),
                         zn[:, TILES - BT:TILES - 1, :]).then_inc(stored, 16)
            sp.dma_start(out[(TILES - 1) * P:N, :], zn[0:TAIL, TILES - 1, :]).then_inc(stored, 16)
            sp.wait_ge(stored, 16 * (NBLK + 1))

        @block.gpsimd
        def _(pool):
            made = [0]

            def step(ins):
                made[0] += 1
                ins.then_inc(pool_made, 1)
                pool.wait_ge(pool_made, made[0])

            step(nc.gpsimd.iota(part_no[:, :], [[0, 1]], base=0, channel_multiplier=1))
            step(nc.gpsimd.iota(iota_i[:, 0:WIN], [[1, WIN]], base=0, channel_multiplier=0))
            step(nc.gpsimd.tensor_copy(win_no[:, :], iota_i[:, 0:WIN]))
            step(nc.gpsimd.memset(ones[:, :], 1.0))
            step(nc.gpsimd.memset(ones16[:, :], 1.0))
            step(nc.gpsimd.affine_select(out=ident[:, :], in_=ones[:, :], compare_op=ALU.is_equal, fill=0.0, base=0,
                                         pattern=[[-1, P]], channel_multiplier=1))
            step(nc.gpsimd.affine_select(out=upper[:, :], in_=ones[:, :], compare_op=ALU.is_ge, fill=0.0, base=-1,
                                         pattern=[[1, P]], channel_multiplier=-1))
            step(nc.gpsimd.affine_select(out=shift[:, :], in_=ones[:, :], compare_op=ALU.is_equal, fill=0.0, base=-1,
                                         pattern=[[-1, P]], channel_multiplier=1))
            step(nc.gpsimd.affine_select(out=last_p[:, :], in_=ones[0:1, :], compare_op=ALU.is_ge, fill=0.0,
                                         base=-(P - 1), pattern=[[1, P]], channel_multiplier=0))
            assert made[0] == POOL_FIRST
            nc.gpsimd.memset(acc[:, 0, :], 0.0).then_inc(acc_zero, 1)
            pool.wait_ge(dve_made, REL_MADE)
            step(nc.gpsimd.affine_select(out=rel[:, FULL, :], in_=rel[:, FULL, :], compare_op=ALU.is_ge,
                                         fill=-FAR, base=-REPEATS, pattern=[[1, EPP]], channel_multiplier=EPP))
            step(nc.gpsimd.affine_select(out=pair_sel[:, :], in_=ones16[:, 0:PAIRS], compare_op=ALU.is_ge, fill=0.0,
                                         base=0, pattern=[[-2, PAIRS]], channel_multiplier=1))
            step(nc.gpsimd.affine_select(out=pair_sel[:, :], in_=pair_sel[:, :], compare_op=ALU.is_ge, fill=0.0,
                                         base=1, pattern=[[2, PAIRS]], channel_multiplier=-1))
            step(nc.gpsimd.tensor_copy(ident16[:, :], ident[:, :]))
            step(nc.gpsimd.iota(iota_i[:, 0:P], [[0, 2], [1, SLOTS]], base=0, channel_multiplier=0))
            step(nc.gpsimd.tensor_copy(slot_no[:, :, :].rearrange("p a s -> p (a s)"), iota_i[:, 0:P]))
            pool.wait_ge(dve_made, PARITY_MADE)
            for a in range(2):
                step(nc.gpsimd.tensor_scalar(slot_no[:, a, :], slot_no[:, a, :], parity[:, a:a + 1], None, ALU.add))
            step(nc.gpsimd.iota(iota_i[:, :], [[1, P], [0, Q]], base=0, channel_multiplier=0))
            step(nc.gpsimd.tensor_copy(lo_iota[:, :, :].rearrange("p l q -> p (l q)"), iota_i[:, :]))
            step(nc.gpsimd.iota(iota_i[:, 0:TILES * 8], [[1, TILES], [0, 8]], base=1, channel_multiplier=0))
            step(nc.gpsimd.tensor_copy(hi_iota[:, :, :].rearrange("p h n -> p (h n)"), iota_i[:, 0:TILES * 8]))
            assert made[0] == POOL_MADE, made[0]

            def stage(rows_, b, n):
                pool.wait_ge(xT_mm, n + ONE)
                nc.gpsimd.tensor_copy(xb[:, :, :], block_of(rows_, b)).then_inc(xb_ready, 1)

            def residual(b, buf, which):
                nc.gpsimd.tensor_tensor(
                    out=yn[:, buf, :, :], in0=block_of(xn, b),
                    in1=row_bc[:, which, :].unsqueeze(1).to_broadcast([P, BT, D]), op=ALU.add
                ).then_inc(resid_ready, 1)

            pool.wait_ge(x_in, 32)
            pool.wait_ge(act_made, ROWS_SPREAD)

            def load_sources(b):
                for t in range(BT):
                    c = b * BT + t
                    nc.gpsimd.indirect_dma_start(
                        sources[:, b % 2, t, :], None, src_pad,
                        bass.IndirectOffsetOnAxis(start_i[:, c:c + 1].bitcast(U32), 0)).then_inc(sources_in[b % 2], 16)

            stage(xn, 0, 0)
            for b in range(2):
                residual(b, b, 0)
            pool.wait_ge(padded, 48)
            pool.wait_ge(start_ready, 1)
            load_sources(0)
            stage(xn, 1, 1)
            load_sources(1)
            for b in range(2, NBLK):
                stage(xn, b, b)
                pool.wait_ge(masks_made, b - 1)
                load_sources(b)
                pool.wait_ge(split_done, b + ONE - 1)
                residual(b, b % 2, 0)

            pool.wait_ge(general_ready, 1)
            general = pool.value_load(flags_i[0:1, 1:2])
            with pool.If(general == 0):
                def body(t, tb):
                    if isinstance(t, int) and t == TILES - 3:
                        stage(zn, 0, NBLK)
                    tile_sums_pool(pool, t, tb)

                over_tiles(pool, body)
                pool.wait_ge(z_ready, TWO + TILES)
            with pool.If(general != 0):
                s = SW[1]
                pool.wait_ge(src_in, 32)
                pool.wait_ge(x1_stored, 16)
                with pool.Fori(0, NG) as g:
                    pool.wait_ge(s["mm"], g * SWEEP + ONE)
                    nc.gpsimd.tensor_copy(gidx[:, :], group_of(src_i, g)).then_inc(idx_copied, 1)
                    pool.wait_ge(idx_copied, g + 1)
                    pool.sem_inc(idx_seen, 1)
                    for j in range(EPP):
                        nc.gpsimd.indirect_dma_start(
                            edges[:, 0, 0, j, :], None, x1_rows,
                            bass.IndirectOffsetOnAxis(gidx[:, j:j + 1].bitcast(U32), 0)).then_inc(s["rows"], 16)
                    pool.wait_ge(s["rows"], g * (16 * EPP) + 16 * EPP)

                pool.wait_ge(general_z, TILES + ONE)
                stage(zn, 0, NBLK)

            def layer1(b, buf, turn_no):
                if not_number_or(b, lambda n: 0 < n < NBLK - 1):
                    stage(zn, b + 1, b + 1 + NBLK)
                pool.wait_ge(normed, b + NBLK)
                residual(b, buf, 2)
                if not not_number_or(b, lambda n: n > 0):
                    stage(zn, b + 1, b + 1 + NBLK)

            pool.wait_ge(split_done, NBLK + ONE)
            over_blocks(pool, layer1)

        @block.scalar
        def _(act):
            act.sem_inc(seg_copied, TWO)
            act.sem_inc(split_done, ONE)
            act.sem_inc(slot_ready, TWO)
            act.sem_inc(evacuated, TWO)
            vectors = [(row("b2b"), b2b), (row("g2"), g2), (row("be2"), be2), (row("m2"), m2), (row("v2"), v2)]
            columns = [("b1b", b1b), ("g1", g1), ("be1", be1), ("m1", m1), ("v1", v1)]
            for dst_, src_ in vectors:
                act.dma_start(dst_, src_.rearrange("(o f) -> o f", o=1)).then_inc(small_in, 16)
            act.dma_start(rowf[0:1, 0, :], b2a.rearrange("(o f) -> o f", o=1)).then_inc(small_in, 16)
            act.dma_start(rows[0:1, ROWS.index("eps"), 0:1], gin_eps).then_inc(small_in, 16)
            for name, src_ in columns:
                act.dma_start(col(name), src_.rearrange("(p o) -> p o", o=1)).then_inc(small_in, 16)
            for k in range(2):
                act.dma_start(cols[:, k:k + 1], b1a[k * P:(k + 1) * P].rearrange("(p o) -> p o", o=1)
                              ).then_inc(small_in, 16)
            act.dma_start(col("u"), u[0, :].rearrange("(p o) -> p o", o=1)).then_inc(small_in, 16)
            act.dma_start(w1a_s[:, :, :], w1a.rearrange("(k p) n -> p k n", p=P)).then_inc(weights_in, 16)
            act.dma_start(w2a_s[:, :, :], w2a.rearrange("(k p) n -> p k n", p=P)).then_inc(weights_in, 16)
            act.dma_start(w1b_s[:, :], w1b).then_inc(weights_in, 16)
            act.dma_start(w2b_s[:, :], w2b).then_inc(weights_in, 16)
            act.wait_ge(dve_made, CLEARED)
            act.dma_start(xn[:, 0:TILES - 1, :],
                          x[0:(TILES - 1) * P, :].rearrange("(t p) f -> p t f", p=P)).then_inc(x_in, 16)
            act.dma_start(xn[0:TAIL, TILES - 1, :], x[(TILES - 1) * P:N, :]).then_inc(x_in, 16)
            act.dma_start(src_pad[0:FULL * GROUP, 0].rearrange("(p c) -> p c", p=P),
                          src[0:FULL * GROUP].rearrange("(p c) -> p c", p=P)).then_inc(padded, 16)
            act.dma_start(src_pad[FULL * GROUP:E, 0].rearrange("(o c) -> o c", o=1),
                          src[FULL * GROUP:E].rearrange("(o c) -> o c", o=1)).then_inc(padded, 16)
            act.dma_start(src_pad[E:E + SLOTS, 0].rearrange("(o c) -> o c", o=1),
                          src[0:SLOTS].rearrange("(o c) -> o c", o=1)).then_inc(padded, 16)

            for i in range(4):
                act.wait_ge(rows_turned, i + 1)
                nc.scalar.activation(
                    dst_f[:, :, 2 * i:2 * i + 2],
                    hid_ps[i][:, 0:2 * NG].rearrange("p (j g) -> p g j", j=2), ACT.Copy).then_inc(rows_read, 1)

            def copy_group(g, buf):
                act.wait_ge(seg_mm, g + RING_GROUPS + 1)
                act.wait_ge(seg_turned, g + 1 + NHOT - TWO)
                nc.scalar.activation(seg[:, buf, :], seg_ps[buf][0:WIN, 0:D], ACT.Copy).then_inc(seg_copied, 1)

            for g in range(RING_GROUPS - 1):
                copy_group(g, g % 2)
            act.wait_ge(small_in, 16 * SMALLS)
            nc.scalar.activation(std1[:, :], col("v1"), ACT.Sqrt, bias=eps_col[:, :]).then_inc(act_made, 1)
            nc.scalar.activation(std2[:, :], row("v2"), ACT.Sqrt, bias=eps_col[0:1, :]).then_inc(act_made, 1)
            act.wait_ge(pe_made, PE_ROWS)
            nc.scalar.activation(row_bc[:, :, :].rearrange("p a f -> p (a f)"), psC[3][:, 0:3 * D],
                                 ACT.Copy).then_inc(act_made, 1)
            copy_group(RING_GROUPS - 1, 1)
            with act.Fori(RING_GROUPS // 2, NG // 2) as i:
                for k in range(2):
                    copy_group(i * 2 + k, k)

            act.wait_ge(missed_ready, 1)
            missed = act.value_load(flags_i[0:1, 0:1])
            with act.If(missed != 0):
                sweep_act(act, SW[0])

            act.wait_ge(totals_mm, 1)
            nc.scalar.activation(totals[:, :], psC[1][0:TILES, 0:P], ACT.Copy).then_inc(totals_ready, 1)

            for b in range(NBLK):
                act.wait_ge(spread_mm, b + 1)
                cols_ = acc[:, 1, b * BLK:(b + 1) * BLK]
                nc.scalar.activation(cols_[:, 0:4 * P], psB[b % 2][:, 0, :], ACT.Copy)
                nc.scalar.activation(cols_[:, 4 * P:BLK], psB[b % 2][:, 1, 0:BLK - 4 * P],
                                     ACT.Copy).then_inc(spread_done, 1)

            def split(b, buf):
                act.wait_ge(normed, b + ONE + 1)
                nc.scalar.activation(x16[:, bass.ds(b * BT, BT), 0, :], block_of(xn, b), ACT.Copy
                                     ).then_inc(hi_copied, 1)
                act.wait_ge(lo_diff, b + 1)
                nc.scalar.activation(x16[:, bass.ds(b * BT, BT), 1, :], yn[:, buf, :, :], ACT.Copy,
                                     scale=LOSCALE).then_inc(split_done, 1)

            def layer0(b, buf, turn_no):
                mlp_relu(act, b, 0)
                if not_number_or(b, lambda n: n > 0):
                    split(b - 1, 1 - buf)
                if not_number_or(b, lambda n: n + 1 < NBLK):
                    mlp_turn_act(act, b + 1)
                if not_number_or(b, lambda n: n > 0):
                    block_slots_act(act, b - 1)
                if not not_number_or(b, lambda n: n + 1 < NBLK):
                    block_slots_act(act, b)
                mlp_std(act, b)

            mlp_turn_act(act, 0)
            over_blocks(act, layer0)
            split(NBLK - 1, (NBLK - 1) % 2)

            act.wait_ge(general_ready, 1)
            general = act.value_load(flags_i[0:1, 1:2])
            with act.If(general == 0):
                def body(t, tb):
                    tile_evacuate(act, t, tb)
                    if is_tile(t - 1):
                        tile_sums_act(act, t - 1, 1 - tb)

                over_tiles(act, body)
                mlp_turn_act(act, NBLK)
                tile_sums_act(act, TILES - 1, 0)
            with act.If(general != 0):
                sweep_act(act, SW[1])
                with act.Fori(0, TILES) as t:
                    act.wait_ge(summed, t + TWO)
                    act.wait_ge(SW[1]["added"], NG * SWEEP)
                    nc.scalar.activation(xb[:, 0, :], acc[:, 0, bass.ds(t * P, P)], ACT.Copy).then_inc(acc_staged, 1)
                mlp_turn_act(act, NBLK)

            def layer1(b, buf, turn_no):
                if not_number_or(b, lambda n: n + 1 < NBLK):
                    mlp_relu(act, b + NBLK + 1, 1, 1 - buf)
                if not_number_or(b, lambda n: n + 2 < NBLK):
                    mlp_turn_act(act, b + NBLK + 2)
                mlp_std(act, b + NBLK)

            mlp_relu(act, NBLK, 1, 0)
            mlp_turn_act(act, NBLK + 1)
            over_blocks(act, layer1)

        @block.vector
        def _(dve):
            dve.sem_inc(group_added, TWO)
            dve.sem_inc(y_read, ONE)
            dve.sem_inc(normed, ONE)
            dve.sem_inc(hi_ready, TWO)
            dve.sem_inc(general_z, ONE)
            dve.sem_inc(z_ready, TWO)
            made = [0]

            def step(ins):
                made[0] += 1
                ins.then_inc(dve_made, 1)
                dve.wait_ge(dve_made, made[0])

            step(nc.vector.memset(eps_col[:, :], EPS))
            step(nc.vector.memset(xn[:, TILES - 1, :], 0.0))
            assert made[0] == CLEARED
            dve.wait_ge(pool_made, 1)
            step(nc.vector.tensor_scalar(parity_i[:, :], part_no[:, :], 1, None, ALU.bitwise_and))
            step(nc.vector.tensor_scalar(parity[:, 0:1], parity_i[:, :], FAR, None, ALU.mult))
            step(nc.vector.tensor_scalar(parity[:, 1:2], parity[:, 0:1], -1.0, FAR, ALU.mult, ALU.add))
            assert made[0] == PARITY_MADE
            step(nc.vector.memset(acc[:, 1, :], 0.0))
            dve.wait_ge(dst_in, 48)
            step(nc.vector.tensor_copy(dst_rows[:, 0, :], dst_in_i[:, 0, :]))
            step(nc.vector.tensor_copy(dst_rows[0:NG - P, 1, :], dst_in_i[0:NG - P, 1, :]))
            assert made[0] == ABS_ROWS
            dve.wait_ge(rows_read, 4)
            step(nc.vector.memset(next_first[:, :], FAR))
            step(nc.vector.tensor_copy(next_first[0:1, 0:FULL - 1], dst_f[0:1, 1:FULL, 0]))
            step(nc.vector.tensor_copy(first_i[0:1, :], dst_f[0:1, :, 0]))
            assert made[0] == ABS_MADE
            dve.wait_ge(pe_made, PE_NEXT)
            step(nc.vector.tensor_tensor(out=rel[:, :, :], in0=dst_f[:, :, :],
                                         in1=psC[0][:, 0:NG].unsqueeze(2).to_broadcast([P, NG, EPP]),
                                         op=ALU.subtract))
            assert made[0] == REL_MADE

            def hot(g, buf):
                dve.wait_ge(seg_mm, g + RING_GROUPS - NHOT + 1)
                make_onehot(buf, group_of(rel, g)).then_inc(onehot_ready, 1)
                dve.wait_ge(onehot_ready, g + 1)
                dve.wait_ge(seg_turned, g + 1)
                sum_onehot(buf).then_inc(hotsum_ready, 1)

            def add(g, buf):
                base = dve.value_load(first_i[0:1, bass.ds(g, 1)], min_val=0, max_val=N - 1)
                dve.wait_ge(seg_turned, g + 1 + NHOT)
                dve.wait_ge(group_added, g + TWO)
                add_group(base, turn_ps[buf], 2).then_inc(group_added, 1)

            dve.wait_ge(pool_made, POOL_FIRST + 1)
            for g in range(2):
                hot(g, g)

            dve.wait_ge(acc_zero, 1)

            def two_groups(first, k):
                hot(first + 2, (k + 2) % NHOT)
                add(first, k % 2)

            for k in range(RING_GROUPS - 2):
                two_groups(k, k)
            dve.wait_ge(small_in, 16 * SMALLS)
            dve.wait_ge(act_made, 2)
            step(nc.vector.reciprocal(std2[:, :], std2[:, :]))
            step(nc.vector.tensor_tensor(out=rowf[0:1, 1, :], in0=row("g2"), in1=std2[:, :], op=ALU.mult))
            step(nc.vector.tensor_tensor(out=rowf[0:1, 2, :], in0=row("b2b"), in1=row("m2"), op=ALU.subtract))
            step(nc.vector.tensor_tensor(out=rowf[0:1, 2, :], in0=rowf[0:1, 2, :], in1=rowf[0:1, 1, :], op=ALU.mult))
            step(nc.vector.tensor_tensor(out=rowf[0:1, 2, :], in0=rowf[0:1, 2, :], in1=row("be2"), op=ALU.add))
            step(nc.vector.tensor_scalar(rowf[0:1, 2, :], rowf[0:1, 2, :], 0.5, None, ALU.mult))
            assert made[0] == ROWS_MADE, made[0]
            step(nc.vector.reciprocal(std1[:, :], std1[:, :]))
            step(nc.vector.tensor_tensor(out=fold[:, 0:1], in0=col("g1"), in1=std1[:, :], op=ALU.mult))
            step(nc.vector.tensor_tensor(out=fold[:, 1:2], in0=col("b1b"), in1=col("m1"), op=ALU.subtract))
            step(nc.vector.tensor_tensor(out=fold[:, 1:2], in0=fold[:, 1:2], in1=fold[:, 0:1], op=ALU.mult))
            step(nc.vector.tensor_tensor(out=fold[:, 1:2], in0=fold[:, 1:2], in1=col("be1"), op=ALU.add))
            dve.wait_ge(pe_made, PE_ROWS)
            step(nc.vector.tensor_tensor(out=bias0[:, :], in0=cols[:, 0:2], in1=psC[2][:, 0:2], op=ALU.add))
            step(nc.vector.tensor_scalar(one_eps[:, :], psC[2][:, 2:3], 1.0, None, ALU.add))
            dve.wait_ge(act_made, ROWS_SPREAD)
            dve.wait_ge(weights_in, 64)
            step(nc.vector.tensor_tensor(out=w2b_s[:, :], in0=w2b_s[:, :], in1=row_bc[:, 1, :], op=ALU.mult))

            for k in range(RING_GROUPS - 2, RING_GROUPS):
                two_groups(k, k)
            with dve.Fori(1, TURNS) as i:
                for k in range(RING_GROUPS):
                    two_groups(i * RING_GROUPS + k, k)
            for g in range(NG - 2, NG):
                add(g, g % 2)

            dve.wait_ge(pool_made, POOL_MADE)
            before = scratch[:, 0:NG * (EPP - 1)].rearrange("p (g j) -> p g j", j=EPP - 1)
            across = scratch[:, NG * (EPP - 1):NG * EPP]
            step(nc.vector.tensor_tensor(out=before, in0=dst_f[:, :, 0:EPP - 1], in1=dst_f[:, :, 1:EPP],
                                         op=ALU.is_gt))
            step(nc.vector.tensor_tensor(out=across, in0=dst_f[:, :, EPP - 1], in1=psC[1][:, 0:NG], op=ALU.is_gt))
            step(nc.vector.tensor_reduce(out=disorder[:, 0:1], in_=scratch[:, 0:NG * EPP], axis=AX.X, op=ALU.add))

            def degrees(done):
                for i in range(DEG_STEPS):
                    n = min(4, TILES - 4 * i)
                    dve.wait_ge(deg_mm, done + i + 1)
                    nc.vector.tensor_copy(deg[:, 4 * i:4 * i + n],
                                          psC[i % 4][:, 0:n * P].rearrange("p (t c) -> p t c", c=P)[:, :, 0]
                                          ).then_inc(deg_read, 1)

            degrees(0)
            dve.wait_ge(total_mm, 1)
            step(nc.vector.tensor_reduce(out=bad[:, 0:1], in_=psC[1][:, 0:TILES], axis=AX.X, op=ALU.add))
            step(nc.vector.tensor_scalar(bad[:, 0:1], bad[:, 0:1], float(E), None, ALU.subtract))
            nc.vector.tensor_copy(flags_i[0:1, 0:1], bad[0:1, 0:1]).then_inc(missed_ready, 1)

            table_steps = [0]

            def table_step(ins):
                table_steps[0] += 1
                ins.then_inc(table_ready, 1)
                dve.wait_ge(table_ready, table_steps[0])

            dve.wait_ge(missed_ready, 1)
            missed = dve.value_load(flags_i[0:1, 0:1])
            mask = scratch[:, 0:NG * EPP].rearrange("p (g j) -> p g j", j=EPP)
            with dve.If(missed != 0):
                table_step(nc.vector.tensor_scalar(mask, rel[:, :, :], 0.0, None, ALU.is_lt))
                table_step(nc.vector.scalar_tensor_tensor(out=mask, in0=rel[:, :, :], scalar=float(WIN), in1=mask,
                                                          op0=ALU.is_ge, op1=ALU.add))
                table_step(nc.vector.scalar_tensor_tensor(out=mask, in0=rel[:, :, :], scalar=-FAR, in1=mask,
                                                          op0=ALU.is_gt, op1=ALU.mult))
                table_step(nc.vector.tensor_copy(left[:, :, :], dst_f[:, :, :]))
                table_step(nc.vector.scalar_tensor_tensor(out=left[:, :, :], in0=left[:, :, :], scalar=1.0, in1=mask,
                                                          op0=ALU.add, op1=ALU.mult))
                table_step(nc.vector.tensor_scalar(left[:, :, :], left[:, :, :], -1.0, None, ALU.add))
                sweep_dve(dve, SW[0], 2, left)
                degrees(DEG_STEPS)
                dve.wait_ge(deg_read, 2 * DEG_STEPS)
            dve.wait_ge(deg_read, DEG_STEPS)
            dve.wait_ge(missed_ready, 1)
            nc.vector.tensor_scalar(rdeg[:, :], deg[:, :], 1.0, None, ALU.max).then_inc(rdeg_ready, 1)
            dve.wait_ge(rdeg_ready, 1)
            nc.vector.reciprocal(rdeg[:, :], rdeg[:, :]).then_inc(rdeg_ready, 1)
            nc.vector.tensor_scalar(over[:, :], deg[:, :], float(SLOTS), None, ALU.is_gt).then_inc(deg_final, 1)
            dve.wait_ge(deg_final, 1)
            step(nc.vector.tensor_reduce(out=disorder[:, 1:2], in_=over[:, :], axis=AX.X, op=ALU.add))
            step(nc.vector.tensor_tensor(out=bad[:, 1:2], in0=disorder[:, 0:1], in1=disorder[:, 1:2], op=ALU.add))
            assert made[0] == BAD_MADE, made[0]
            dve.wait_ge(start_mm, 1)
            nc.vector.tensor_copy(start_i[:, :], psC[0][:, 0:TILES]).then_inc(start_ready, 1)
            dve.wait_ge(bad_mm, 1)
            nc.vector.tensor_copy(flags_i[0:1, 1:2], psC[1][0:1, 256:257]).then_inc(general_ready, 1)

            def edge_means(b):
                dve.wait_ge(h_mm, 4 * b + ONE)
                nc.vector.tensor_tensor(out=mlp[:, 1, :], in0=acc[:, 1, bass.ds(b * BLK, BLK)],
                                        in1=acc[:, 0, bass.ds(b * BLK, BLK)], op=ALU.mult).then_inc(eT_ready, 1)

            def low_part(b, buf):
                dve.wait_ge(hi_copied, b + 1)
                nc.vector.tensor_tensor(out=yn[:, buf, :, :], in0=block_of(xn, b),
                                        in1=x16[:, bass.ds(b * BT, BT), 0, :], op=ALU.subtract).then_inc(lo_diff, 1)

            def layer0(b, buf, turn_no):
                if not_number_or(b, lambda n: n + 1 < NBLK):
                    edge_means(b + 1)
                if not_number_or(b, lambda n: n > 0):
                    low_part(b - 1, 1 - buf)
                block_masks(dve, b, buf, turn_no)
                if not not_number_or(b, lambda n: n + 1 < NBLK):
                    dve.wait_ge(slot_ready, TWO + 1)
                    tile_onehots(dve, 0, 0)
                mlp_norm(dve, b, 0, buf, block_of(xn, b))

            dve.wait_ge(group_added, NG + TWO)
            dve.wait_ge(spread_done, NBLK)
            edge_means(0)
            over_blocks(dve, layer0)
            low_part(NBLK - 1, (NBLK - 1) % 2)

            dve.wait_ge(general_ready, 1)
            general = dve.value_load(flags_i[0:1, 1:2])
            with dve.If(general == 0):
                dve.wait_ge(slot_ready, TWO + NBLK)

                def body(t, tb):
                    if is_tile(t + 1):
                        tile_onehots(dve, t + 1, 1 - tb)
                    if is_tile(t - 2):
                        tile_z(dve, t - 2, tb)

                over_tiles(dve, body)
                for t in range(TILES - 2, TILES):
                    tile_z(dve, t, t % 2)
            with dve.If(general != 0):
                dve.wait_ge(slot_ready, TWO + NBLK)
                nc.vector.memset(acc[:, 0, :], 0.0).then_inc(table1_ready, 1)
                nc.vector.tensor_scalar(mask, rel[:, :, :], -FAR, None, ALU.is_gt).then_inc(table1_ready, 1)
                nc.vector.tensor_copy(left[:, :, :], dst_f[:, :, :]).then_inc(table1_ready, 1)
                dve.wait_ge(table1_ready, 3)
                nc.vector.scalar_tensor_tensor(out=left[:, :, :], in0=left[:, :, :], scalar=1.0, in1=mask,
                                               op0=ALU.add, op1=ALU.mult).then_inc(table1_ready, 1)
                dve.wait_ge(table1_ready, 4)
                nc.vector.tensor_scalar(left[:, :, :], left[:, :, :], -1.0, None, ALU.add).then_inc(table1_ready, 1)
                dve.wait_ge(table1_ready, 5)
                sweep_dve(dve, SW[1], 1, left)
                with dve.Fori(0, TILES) as t:
                    dve.wait_ge(summed, t + TWO + 1)
                    nc.vector.scalar_tensor_tensor(
                        out=tile_of(zn, t), in0=tile_of(xn, t), scalar=one_eps[:, :], in1=psC[1][:, 0:D],
                        op0=ALU.mult, op1=ALU.add).then_inc(general_z, 1)

            over_blocks(dve, lambda b, buf, turn_no: mlp_norm(dve, b + NBLK, 1, buf, block_of(zn, b)))

        @block.tensor
        def _(pe):
            pe.sem_inc(seg_mm, RING_GROUPS)
            pe.sem_inc(seg_turned, NHOT)
            pe.sem_inc(xT_mm, ONE)
            pe.sem_inc(y_mm, ONE)
            pe.sem_inc(h_mm, ONE)
            pe.sem_inc(slot_mm, ONE)
            pe.sem_inc(built, 2 * 8)
            pe.sem_inc(summed, TWO)
            for s in SW:
                pe.sem_inc(s["mm"], ONE)
            pe.wait_ge(pool_made, POOL_FIRST)
            pe.wait_ge(dve_made, ABS_ROWS)
            for j in range(EPP):
                bank = hid_ps[j // 2]
                nc.tensor.transpose(bank[:, (j % 2) * NG:(j % 2) * NG + P], dst_rows[:, 0, j:GROUP:EPP], ident[:, :])
                last = nc.tensor.transpose(bank[:, (j % 2) * NG + P:(j % 2 + 1) * NG], dst_rows[0:NG - P, 1, j:GROUP:EPP],
                                           ident[0:NG - P, 0:NG - P])
                if j % 2:
                    last.then_inc(rows_turned, 1)
            pe.wait_ge(dve_made, ABS_MADE)
            nc.tensor.matmul(psC[0][:, 0:NG], ones[0:1, :], dst_f[0:1, :, 0], start=True, stop=True
                             ).then_inc(pe_made, 1)
            nc.tensor.matmul(psC[1][:, 0:NG], shift[:, :], dst_f[:, :, 0], start=True, stop=False)
            nc.tensor.matmul(psC[1][:, 0:NG], last_p[:, :], next_first[:, :], start=False, stop=True
                             ).then_inc(pe_made, 1)

            def products(g, k, h, buf):
                pe.wait_ge(onehot_ready, g + 1)
                pe.wait_ge(seg_copied, g + 1)
                multiply(seg_ps[buf % 2], buf, edges[:, k, h, :, :]).then_inc(seg_mm, 1)

            def turned(g, buf):
                pe.wait_ge(seg_copied, g + 1 + TWO)
                pe.wait_ge(hotsum_ready, g + 1)
                pe.wait_ge(group_added, g + 1)
                turn(turn_ps[buf % 2], seg[:, buf % 2, :], buf).then_inc(seg_turned, 1)

            def unit(i, k, first):
                pe.wait_ge(edges_in[k], i * 16 + 16)
                for h in range(2):
                    g = first + h
                    products(g, k, h, (2 * k + h) % NHOT)
                    if not (isinstance(g, int) and g == 0):
                        turned(g - 1, (2 * k + h - 1) % NHOT)

            for k in range(RING):
                unit(0, k, 2 * k)
            pe.wait_ge(small_in, 16 * SMALLS)
            pe.wait_ge(weights_in, 64)
            pe.wait_ge(dve_made, ROWS_MADE)
            for k in range(2):
                nc.tensor.matmul(psC[2][:, k:k + 1], w1a_s[:, 2, k * P:(k + 1) * P], col("u"), start=True, stop=True)
            nc.tensor.matmul(psC[2][:, 2:3], ones[0:1, :], row("eps")[:, 0:1], start=True, stop=True)
            nc.tensor.matmul(psC[3][:, 0:3 * D], ones[0:1, :], rowf[:, :, :].rearrange("o a f -> o (a f)"),
                             start=True, stop=True).then_inc(pe_made, 1)
            with pe.Fori(1, TURNS) as i:
                for k in range(RING):
                    unit(i, k, i * RING_GROUPS + 2 * k)
            pe.wait_ge(edges_in[0], TURNS * 16 + 32)
            for h in range(2):
                g = NG - 2 + h
                products(g, 0, h, g % NHOT)
                turned(g - 1, (g - 1) % NHOT)
            turned(NG - 1, (NG - 1) % NHOT)

            def degrees(done):
                for i in range(DEG_STEPS):
                    if done + i >= 4:
                        pe.wait_ge(deg_read, done + i - 3)
                    for t in range(4 * i, min(4 * i + 4, TILES)):
                        last = nc.tensor.transpose(psC[i % 4][:, (t % 4) * P:(t % 4 + 1) * P],
                                                   acc[:, 1, t * P:(t + 1) * P], ident[:, :])
                    last.then_inc(deg_mm, 1)
                pe.wait_ge(deg_read, done + DEG_STEPS)

            pe.wait_ge(group_added, NG + TWO)
            pe.wait_ge(dve_made, DISORDER_MADE)
            degrees(0)
            nc.tensor.matmul(psC[1][:, 0:TILES], ones[:, :], deg[:, :], start=True, stop=True).then_inc(total_mm, 1)

            pe.wait_ge(missed_ready, 1)
            missed = pe.value_load(flags_i[0:1, 0:1])
            with pe.If(missed != 0):
                sweep_pe(pe, SW[0], 16)
                pe.wait_ge(SW[0]["added"], NG * SWEEP)
                degrees(DEG_STEPS)

            pe.wait_ge(deg_final, 1)
            nc.tensor.matmul(psC[1][0:TILES, 0:P], deg[:, :], ones[:, :], start=True, stop=True).then_inc(totals_mm, 1)
            pe.wait_ge(totals_ready, 1)
            nc.tensor.matmul(psC[0][:, 0:TILES], upper[:, :], deg[:, :], start=True, stop=False)
            nc.tensor.matmul(psC[0][:, 0:TILES], totals[:, :], upper[0:TILES, 0:TILES], start=False, stop=True
                             ).then_inc(start_mm, 1)
            pe.wait_ge(dve_made, BAD_MADE)
            nc.tensor.matmul(psC[1][:, 256:257], ones[:, :], bad[:, 1:2], start=True, stop=True).then_inc(bad_mm, 1)
            pe.wait_ge(start_ready, 1)
            pe.wait_ge(general_ready, 1)

            mlp_turn(pe, 0)
            pe.wait_ge(rdeg_ready, 2)
            for b in range(NBLK):
                if b >= 2:
                    pe.wait_ge(spread_done, b - 1)
                for t in range(BT):
                    c = b * BT + t
                    last = nc.tensor.transpose(psB[b % 2][:, t // 4, (t % 4) * P:(t % 4 + 1) * P],
                                               rdeg[:, c:c + 1].to_broadcast([P, P]), ident[:, :])
                last.then_inc(spread_mm, 1)
            pe.wait_ge(spread_done, NBLK)

            def layer0(b, buf, turn_no):
                mlp_hidden(pe, b, 0)
                if not_number_or(b, lambda n: n + 1 < NBLK):
                    mlp_turn(pe, b + 1)
                wait_hidden(pe, b, 0)
                if not_number_or(b, lambda n: n > 0):
                    block_slots(pe, b - 1)
                mlp_out(pe, b, 0)

            over_blocks(pe, layer0)
            pe.wait_ge(slot_ready, TWO + NBLK - 1)
            block_slots(pe, NBLK - 1)
            pe.wait_ge(slot_ready, TWO + NBLK)

            general = pe.value_load(flags_i[0:1, 1:2])
            with pe.If(general == 0):
                def body(t, tb):
                    if isinstance(t, int) and t == 1:
                        pe.wait_ge(split_done, NBLK + ONE)
                    tile_build(pe, t, tb, (lambda g: tile_sum(pe, t - 1, 1 - tb, g)) if is_tile(t - 1) else None)

                over_tiles(pe, body)
                mlp_turn(pe, NBLK)
                tile_sum(pe, TILES - 1, 0)
            with pe.If(general != 0):
                sweep_pe(pe, SW[1], 16 * EPP)
                with pe.Fori(0, TILES) as t:
                    pe.wait_ge(acc_staged, t + 1)
                    pe.wait_ge(general_z, t + ONE)
                    nc.tensor.transpose(psC[1][:, 0:P], xb[:, 0, :], ident[:, :]).then_inc(summed, 1)
                pe.wait_ge(general_z, TILES + ONE)
                mlp_turn(pe, NBLK)

            def layer1(b, buf, turn_no):
                if not_number_or(b, lambda n: n + 1 < NBLK):
                    mlp_hidden(pe, b + NBLK + 1, 1, 1 - buf)
                if not_number_or(b, lambda n: n + 2 < NBLK):
                    mlp_turn(pe, b + NBLK + 2)
                wait_hidden(pe, b + NBLK, 1)
                mlp_out(pe, b + NBLK, 1, buf)

            mlp_hidden(pe, NBLK, 1, 0)
            mlp_turn(pe, NBLK + 1)
            over_blocks(pe, layer1)


_INS = ['x', 'src', 'dst', 'edge_attr_128', 'L0_gnn_u', 'L0_gnn_W1', 'L0_gnn_b1', 'L0_gnn_W2', 'L0_gnn_b2',
        'L1_gnn_eps', 'L1_gnn_W1', 'L1_gnn_b1', 'L1_gnn_g1', 'L1_gnn_beta1', 'L1_gnn_m1', 'L1_gnn_v1',
        'L1_gnn_W2', 'L1_gnn_b2', 'L1_gnn_g2', 'L1_gnn_beta2', 'L1_gnn_m2', 'L1_gnn_v2']


def kernel(**inputs):
    import numpy as _np
    import concourse.bacc as _bacc
    from concourse import mybir as _mybir
    from concourse.bass_utils import run_bass_kernel_spmd as _run

    nc = _bacc.Bacc("TRN2", target_bir_lowering=False, num_devices=1)
    arrays, args = {}, []
    for name in _INS:
        a = _np.ascontiguousarray(inputs[name])
        if a.ndim == 0:
            a = a.reshape(1, 1)
        arrays[f"in_{name}"] = a
        args.append(nc.dram_tensor(f"in_{name}", a.shape, _mybir.dt.from_np(a.dtype), kind="ExternalInput").ap())
    args.append(nc.dram_tensor("out_rows", (N, D), _mybir.dt.float32, kind="ExternalOutput").ap())
    build(nc, *args)
    r = _run(nc, [arrays], core_ids=[0])
    return r.results[0]["out_rows"]
```

```python
import concourse.bass as bass
from concourse import mybir
from contextlib import ExitStack

FP32 = mybir.dt.float32
BF16 = mybir.dt.bfloat16
FP16 = mybir.dt.float16
I32 = mybir.dt.int32
U32 = mybir.dt.uint32
ALU = mybir.AluOpType
ACT = mybir.ActivationFunctionType
AX = mybir.AxisListType

N = 6250
E = 206250
D = 128
P = 128
HID = 256
EPP = 8
GROUP = P * EPP
FULL = E // GROUP
NG = FULL + 1
REPEATS = GROUP - (E - FULL * GROUP)
WIN = 48
SWEEP = -(-N // WIN)
TILES = -(-N // P)
NP = TILES * P
TAIL = N - (TILES - 1) * P
ACCW = max(NP, N + WIN, SWEEP * WIN)
BT = 7
BLK = BT * P
NBLK = TILES // BT
HALF = BLK // 2
RING = 4
UNITS = NG // 2
TURNS = (UNITS - 1) // RING
NHOT = 4
SLOTS = 64
PAIRS = P // 2
Q = 8
LOSCALE = 2048.0
EPS = 1e-5
FAR = 100000.0
CLEARED, PARITY_MADE, ABS_ROWS, ABS_MADE, REL_MADE, ROWS_MADE, BIAS_MADE, BAD_MADE = 2, 5, 7, 10, 11, 17, 24, 31
POOL_FIRST, POOL_MADE = 9, 21
PE_BASE, PE_ROWS = 1, 3
ROWS_SPREAD = 3
SMALLS = 15
SLOTW = PAIRS + P
DEG_STEPS = -(-TILES // 4)
assert TILES % BT == 0 and TURNS * RING == UNITS - 1 and NG % 2 == 0 and 2 * SLOTS == P and TILES % 2 == 1


def build(nc, x, src, dst, attr, u, w1a, b1a, w2a, b2a, gin_eps, w1b, b1b, g1, be1, m1, v1,
          w2b, b2b, g2, be2, m2, v2, out):
    x1_rows = nc.dram_tensor("x1_rows", [NP, D], FP32, kind="Internal").ap()
    src_pad = nc.dram_tensor("src_pad", [E + SLOTS, 1], I32, kind="Internal").ap()
    ctx = ExitStack()
    with ctx:
        def sb(name, shape, dt=FP32):
            return ctx.enter_context(nc.sbuf_tensor(name, shape, dt))

        def sem(name):
            return ctx.enter_context(nc.semaphore(name))

        ring = sb("ring", [P, RING * 2 * GROUP])
        edges = ring[:, :].rearrange("p (k h j f) -> p k h j f", k=RING, h=2, j=EPP)
        lo_hot = ring[:, :].bitcast(BF16).rearrange("p (b g l q) -> p b g l q", b=2, g=PAIRS // Q, l=P)
        index = sb("index", [P, 4, NG * EPP])
        dst_f = index[:, 2, :].rearrange("p (g j) -> p g j", j=EPP)
        src_i = index[:, 1, :].bitcast(I32).rearrange("p (g j) -> p g j", j=EPP)
        rel = index[:, 3, :].rearrange("p (g j) -> p g j", j=EPP)
        left = index[:, 0, :].rearrange("p (g j) -> p g j", j=EPP)
        PT = P * TILES // 2
        hi_hot = index[:, :, :].rearrange("p a c -> p (a c)")[:, 0:2 * PT].bitcast(BF16).rearrange(
            "p (b g h n) -> p b g h n", b=2, g=P // 8, h=TILES)
        acc = sb("acc", [P, 2, ACCW])
        counts16 = acc[:, 0, 0:2 * PT].bitcast(FP16).rearrange("p (b h n) -> p b h n", b=2, h=TILES)
        x16 = acc[:, 1, 0:NP].bitcast(FP16).rearrange("p (t a f) -> p t a f", t=TILES, a=2)
        xn = sb("xn", [P, TILES, D])
        zn = sb("zn", [P, TILES, D])
        scratch = zn[:, :, :].rearrange("p t f -> p (t f)")
        mlp = ring[:, RING * GROUP:RING * GROUP + 4 * BLK].rearrange("p (a c) -> p a c", a=4)
        slot = scratch[:, NP - TILES * SLOTW // 2:NP].bitcast(BF16).rearrange("p (t w) -> p t w", w=SLOTW)
        dst_rows = scratch[:, P * Q:P * Q + 2 * GROUP].rearrange("p (h c) -> p h c", h=2)
        dst_in_i = scratch[:, P * Q + 2 * GROUP:P * Q + 4 * GROUP].bitcast(I32).rearrange("p (h c) -> p h c", h=2)
        onehot = sb("onehot", [P, NHOT, EPP, WIN])
        hotsum = sb("hotsum", [P, NHOT, WIN], BF16)
        seg = sb("seg", [WIN, 2, D])
        sources = sb("sources", [P, 2, BT, SLOTS], I32)
        acc_tile = sb("acc_tile", [P, P])
        yn = sb("yn", [P, 2, BT, D])
        stats = sb("stats", [P, BT, 6])
        mv = sb("mv", [P, BT, 2])
        std = sb("std", [P, BT])
        rstd = sb("rstd", [P, BT])
        hi_i = sb("hi_i", [P, BT, SLOTS], I32)
        lo_i = sb("lo_i", [P, BT, SLOTS], I32)
        sums = sources[:, :, :, :].bitcast(FP32).rearrange("p b t s -> p (b t s)")[:, 0:4 * D].rearrange(
            "p (b c) -> p b c", b=2)
        valid = sb("valid", [P, BT, P], BF16)
        hi_m = sb("hi_m", [P, BT, P], BF16)
        lo_m = sb("lo_m", [P, BT, P], BF16)
        lo_iota = sb("lo_iota", [P, P, Q], BF16)
        hi_iota = sb("hi_iota", [P, TILES, 8], BF16)
        slot_no = sb("slot_no", [P, 2, SLOTS])
        iota_i = scratch[:, 0:P * Q].bitcast(I32)
        win_no = sb("win_no", [P, WIN])
        ident = sb("ident", [P, P])
        ident16 = sb("ident16", [P, P], BF16)
        upper = sb("upper", [P, P])
        shift = sb("shift", [P, P])
        last_p = sb("last_p", [1, P])
        ones = sb("ones", [P, P])
        ones16 = sb("ones16", [P, P], BF16)
        pair_sel = sb("pair_sel", [P, PAIRS], BF16)
        part_no = sb("part_no", [P, 1], I32)
        parity_i = sb("parity_i", [P, 1], I32)
        parity = sb("parity", [P, 2])
        next_first = sb("next_first", [1, NG])
        disorder = sb("disorder", [P, 2])
        deg = sb("deg", [P, TILES])
        rdeg = sb("rdeg", [P, TILES])
        first_i = sb("first_i", [1, NG], I32)
        over = sb("over", [P, TILES])
        start_i = sb("start_i", [P, TILES], I32)
        totals = sb("totals", [TILES, P])
        bad = sb("bad", [P, 2])
        flags_i = sb("flags_i", [1, 2], I32)
        w1a_s = sb("w1a_s", [P, 3, HID])
        w2a_s = sb("w2a_s", [P, 2, D])
        w1b_s = sb("w1b_s", [P, D])
        w2b_s = sb("w2b_s", [P, D])
        COLS = ["b1a0", "b1a1", "u", "b1b", "g1", "be1", "m1", "v1"]
        cols = sb("cols", [P, len(COLS)])
        ROWS = ["b2b", "g2", "be2", "m2", "v2", "eps"]
        rows = sb("rows", [1, len(ROWS), D])
        bias0 = sb("bias0", [P, 2])
        fold = sb("fold", [P, 2])
        std1 = sb("std1", [P, 1])
        std2 = sb("std2", [1, D])
        rowf = sb("rowf", [1, 3, D])
        row_bc = sb("row_bc", [P, 3, D])
        one_eps = sb("one_eps", [P, 1])
        eps_col = sb("eps_col", [P, 1])
        cur = sb("cur", [P, EPP])
        gidx = sb("gidx", [P, EPP], I32)

        psB = [ctx.enter_context(nc.psum_tensor(f"psB{i}", [P, 2, 512], FP32)) for i in range(2)]
        psC = [ctx.enter_context(nc.psum_tensor(f"psC{i}", [P, 512], FP32)) for i in range(4)]
        seg_ps = [psB[0][:, 0, :], psB[0][:, 1, :]]
        turn_ps = [psB[1][:, 0, :], psB[1][:, 1, :]]
        hid_ps = [psB[0][:, 0, :], psB[0][:, 1, :], psB[1][:, 0, :], psB[1][:, 1, :]]

        def col(name):
            return cols[:, COLS.index(name):COLS.index(name) + 1]

        def row(name):
            return rows[0:1, ROWS.index(name), :]

        dst_in, x_in, weights_in, small_in, padded, stored = (
            sem(n) for n in ("dst_in", "x_in", "weights_in", "small_in", "padded", "stored"))
        sources_in = [sem(f"sources_in{k}") for k in range(2)]
        edges_in = [sem(f"edges_in{k}") for k in range(RING)]
        pool_made, dve_made, act_made, pe_made = (sem(n) for n in ("pool_made", "dve_made", "act_made", "pe_made"))
        onehot_ready, hotsum_ready, seg_mm, seg_copied, seg_turned, group_added = (
            sem(n) for n in ("onehot_ready", "hotsum_ready", "seg_mm", "seg_copied", "seg_turned", "group_added"))
        deg_mm, deg_read, total_mm, missed_ready, deg_final, totals_mm, totals_ready, start_mm, start_ready, bad_mm, \
            general_ready, rdeg_ready, spread_mm, spread_act, spread_dve, rows_turned, rows_read = (sem(n) for n in (
                "deg_mm", "deg_read", "total_mm", "missed_ready", "deg_final", "totals_mm", "totals_ready", "start_mm",
                "start_ready", "bad_mm", "general_ready", "rdeg_ready", "spread_mm", "spread_act", "spread_dve",
                "rows_turned", "rows_read"))
        xT_mm, xT_ready, eT_ready, h_mm, h_ready, y_mm, y_read, resid_ready, stats_step, std_ready, normed, \
            hi_copied, lo_diff, split_done = (sem(n) for n in (
                "xT_mm", "xT_ready", "eT_ready", "h_mm", "h_ready", "y_mm", "y_read", "resid_ready",
                "stats_step", "std_ready", "normed", "hi_copied", "lo_diff", "split_done"))
        mask_step, masks_made, slot_mm, slot_ready, lo_ready, hi_ready, built, evacuated, summed, z_ready = (
            sem(n) for n in ("mask_step", "masks_made", "slot_mm", "slot_ready", "lo_ready", "hi_ready", "built",
                             "evacuated", "summed", "z_ready"))
        acc_zero, sums_ready, sums_added, general_z = (
            sem(n) for n in ("acc_zero", "sums_ready", "sums_added", "general_z"))
        src_in, x1_stored, idx_copied, table_ready, table1_ready, acc_staged = (
            sem(n) for n in ("src_in", "x1_stored", "idx_copied", "table_ready", "table1_ready", "acc_staged"))
        SW = [{n: sem(f"sweep{layer}_{n}") for n in (
            "rows", "rows_seen", "moved", "hot", "sum", "mm", "copied", "turned", "added")} for layer in range(2)]

        stats_seen, idx_seen = sem("stats_seen"), sem("idx_seen")

        RING_GROUPS = 2 * RING
        TWO = 2
        ONE = 1

        def make_onehot(buf, table):
            return nc.vector.tensor_tensor(
                out=onehot[:, buf, :, :], in0=table.unsqueeze(2).to_broadcast([P, EPP, WIN]),
                in1=win_no[:, :].unsqueeze(1).to_broadcast([P, EPP, WIN]), op=ALU.is_equal)

        def sum_onehot(buf):
            with nc.allow_low_precision(reason="counts up to EPP are exact in bfloat16"):
                return nc.vector.tensor_reduce(
                    out=hotsum[:, buf, :], in_=onehot[:, buf, :, :].rearrange("p j w -> p w j"), axis=AX.X, op=ALU.add)

        def multiply(out_, buf, data):
            for j in range(EPP):
                last = nc.tensor.matmul(out_[0:WIN, 0:D], onehot[:, buf, j, :], data[:, j, :], start=(j == 0),
                                        stop=(j == EPP - 1))
            return last

        def turn(out_, rows_, buf):
            nc.tensor.matmul(out_[:, WIN:2 * WIN], ones16[:, :], hotsum[:, buf, :], start=True, stop=True)
            return nc.tensor.transpose(out_[:, 0:WIN], rows_, ident[0:WIN, 0:WIN])

        def add_group(base, turned, parts):
            span = acc[:, 0:parts, bass.ds(base, WIN)]
            return nc.vector.tensor_tensor(
                out=span, in0=span, in1=turned[:, 0:parts * WIN].rearrange("p (a w) -> p a w", a=parts), op=ALU.add)

        def group_of(table, g):
            return table[:, bass.ds(g, 1), :].rearrange("p g j -> p (g j)")

        last_edges = attr[E - GROUP:E, :].rearrange("(p j) f -> p j f", j=EPP)

        def sweep_pe(pe, s, rows_inc):
            with pe.Fori(0, NG) as g:
                pe.wait_ge(s["rows"], g * rows_inc + rows_inc)
                pe.sem_inc(s["rows_seen"], 1)
                with pe.Fori(0, SWEEP) as w:
                    step = g * SWEEP + w
                    pe.wait_ge(s["sum"], step + 1)
                    multiply(seg_ps[0], 0, edges[:, 0, 0, :, :]).then_inc(s["mm"], 1)
                    pe.wait_ge(s["copied"], step + 1)
                    turn(turn_ps[0], seg[:, 0, :], 0).then_inc(s["turned"], 1)

        def sweep_act(act, s):
            with act.Fori(0, NG * SWEEP) as step:
                act.wait_ge(s["mm"], step + 1 + ONE)
                nc.scalar.activation(seg[:, 0, :], seg_ps[0][0:WIN, 0:D], ACT.Copy).then_inc(s["copied"], 1)

        def sweep_dve(dve, s, parts, table):
            with dve.Fori(0, NG) as g:
                nc.vector.tensor_copy(cur[:, :], group_of(table, g)).then_inc(s["moved"], 1)
                with dve.Fori(0, SWEEP) as w:
                    step = g * SWEEP + w
                    dve.wait_ge(s["moved"], step + g + 1)
                    make_onehot(0, cur[:, :]).then_inc(s["hot"], 1)
                    dve.wait_ge(s["hot"], step + 1)
                    sum_onehot(0).then_inc(s["sum"], 1)
                    nc.vector.tensor_scalar(cur[:, :], cur[:, :], float(-WIN), None, ALU.add).then_inc(s["moved"], 1)
                    dve.wait_ge(s["turned"], step + 1)
                    add_group(w * WIN, turn_ps[0], parts).then_inc(s["added"], 1)
                    dve.wait_ge(s["added"], step + 1)
                dve.wait_ge(s["moved"], g * (SWEEP + 1) + SWEEP + 1)

        def mlp_turn(pe, rows_, b):
            for t in range(BT):
                last = nc.tensor.transpose(psC[t // 4][:, (t % 4) * P:(t % 4 + 1) * P], rows_[:, b * BT + t, :],
                                           ident[:, :])
            last.then_inc(xT_mm, 1)

        def mlp_hidden(pe, n, layer, buf=0):
            pe.wait_ge(xT_ready, n + 1)
            if layer == 0:
                pe.wait_ge(slot_ready, n + 1)
                pe.wait_ge(eT_ready, n + 1)
            for half in range(2):
                for k in range(2 - layer):
                    cols_ = slice(half * HALF, (half + 1) * HALF)
                    out_ = hid_ps[2 * half + k + buf][:, 0:HALF]
                    if layer == 0:
                        nc.tensor.matmul(out_, w1a_s[:, 0, k * P:(k + 1) * P], mlp[:, 0, cols_], start=True,
                                         stop=False)
                        last = nc.tensor.matmul(out_, w1a_s[:, 1, k * P:(k + 1) * P], mlp[:, 1, cols_], start=False,
                                                stop=True)
                    else:
                        last = nc.tensor.matmul(out_, w1b_s[:, :], mlp[:, 0, cols_], start=True, stop=True)
                    last.then_inc(h_mm, 1)

        def mlp_out(pe, n, layer, buf=0):
            pe.wait_ge(y_read, n + ONE)
            for t in range(BT):
                out_ = psC[2 + t // 4][:, (t % 4) * D:(t % 4 + 1) * D]
                for k in range(2 - layer):
                    last = nc.tensor.matmul(out_, mlp[:, 2 + k + buf, t * P:(t + 1) * P],
                                            w2a_s[:, k, :] if layer == 0 else w2n, start=(k == 0),
                                            stop=(k == 1 - layer))
            last.then_inc(y_mm, 1)

        def wait_hidden(pe, n, layer):
            pe.wait_ge(h_ready, 4 * n + 4 if layer == 0 else 2 * n + 2 * NBLK + 2)

        w2n = w2b_s[:, :]

        def mlp_turn_act(act, n):
            act.wait_ge(xT_mm, n + ONE + 1)
            nc.scalar.activation(mlp[:, 0, 0:4 * P], psC[0][:, :], ACT.Copy)
            nc.scalar.activation(mlp[:, 0, 4 * P:BLK], psC[1][:, 0:BLK - 4 * P], ACT.Copy).then_inc(xT_ready, 1)

        def mlp_relu(act, n, layer, buf=0):
            act.wait_ge(y_mm, n + ONE - layer)
            units = 2 - layer
            first = 4 * n if layer == 0 else 2 * n + 2 * NBLK
            for half in range(2):
                for k in range(units):
                    act.wait_ge(h_mm, first + half * units + k + ONE + 1)
                    out_ = mlp[:, 2 + k + buf, half * HALF:(half + 1) * HALF]
                    in_ = hid_ps[2 * half + k + buf][:, 0:HALF]
                    if layer == 0:
                        ins = nc.scalar.activation(out_, in_, ACT.Relu, bias=bias0[:, k:k + 1])
                    else:
                        ins = nc.scalar.activation(out_, in_, ACT.Relu, bias=fold[:, 1:2], scale=fold[:, 0:1])
                    ins.then_inc(h_ready, 1)

        def mlp_std(act, n):
            act.wait_ge(stats_step, 3 * n + 2)
            nc.scalar.activation(std[:, :], mv[:, :, 1], ACT.Sqrt, bias=eps_col[:, :]).then_inc(std_ready, 1)

        def mlp_norm(dve, n, layer, buf, dst_):
            yb = yn[:, buf, :, :]
            dve.wait_ge(y_mm, n + ONE + 1)
            dve.wait_ge(resid_ready, n + 1)
            for bank, t0, t1 in ((2, 0, 4), (3, 4, BT)):
                y = psC[bank][:, 0:(t1 - t0) * D].rearrange("p (t f) -> p t f", f=D)
                if layer == 0:
                    ins = nc.vector.tensor_tensor(out=yb[:, t0:t1, :], in0=yb[:, t0:t1, :], in1=y, op=ALU.add)
                else:
                    ins = nc.vector.scalar_tensor_tensor(out=yb[:, t0:t1, :], in0=yb[:, t0:t1, :], scalar=2.0,
                                                         in1=y, op0=ALU.mult, op1=ALU.add)
            ins.then_inc(y_read, 1)
            dve.wait_ge(y_read, n + ONE + 1)
            for t in range(BT):
                last = nc.vector.bn_stats(stats[:, t, :], yb[:, t, :])
            last.then_inc(stats_step, 1)
            dve.wait_ge(stats_step, 3 * n + 1)
            dve.sem_inc(stats_seen, 1)
            for t in range(BT):
                last = nc.vector.bn_aggr(mv[:, t, :], stats[:, t, :])
            last.then_inc(stats_step, 1)
            dve.wait_ge(std_ready, n + 1)
            nc.vector.reciprocal(rstd[:, :], std[:, :]).then_inc(stats_step, 1)
            dve.wait_ge(stats_step, 3 * n + 3)
            for t in range(BT):
                last = nc.vector.tensor_scalar(dst_[:, t, :], yb[:, t, :], mv[:, t, 0:1], rstd[:, t:t + 1],
                                               ALU.subtract, ALU.mult)
            last.then_inc(normed, 1)

        def block_of(rows_, b):
            return rows_[:, bass.ds(b * BT, BT), :]

        def block_masks(dve, b, buf, turn_no):
            m = b * 3
            dve.wait_ge(sources_in[buf], turn_no * (16 * BT) + 16 * BT)
            dve.wait_ge(slot_mm, b + ONE)
            nc.vector.tensor_scalar(hi_i[:, :, :], sources[:, buf, :, :], 7, None, ALU.logical_shift_right
                                    ).then_inc(mask_step, 1)
            nc.vector.tensor_scalar(lo_i[:, :, :], sources[:, buf, :, :], P - 1, None, ALU.bitwise_and
                                    ).then_inc(mask_step, 1)
            nc.vector.tensor_tensor(
                out=valid[:, :, :], in0=slot_no[:, :, :].rearrange("p a s -> p (a s)").unsqueeze(1).to_broadcast(
                    [P, BT, P]),
                in1=deg[:, bass.ds(b * BT, BT)].unsqueeze(2).to_broadcast([P, BT, P]), op=ALU.is_lt
            ).then_inc(mask_step, 1)
            dve.wait_ge(mask_step, m + 3)
            for a in range(2):
                half = slice(a * SLOTS, (a + 1) * SLOTS)
                nc.vector.scalar_tensor_tensor(out=hi_m[:, :, half], in0=hi_i[:, :, :], scalar=1.0,
                                               in1=valid[:, :, half], op0=ALU.add, op1=ALU.mult)
                last = nc.vector.tensor_tensor(out=lo_m[:, :, half], in0=lo_i[:, :, :], in1=valid[:, :, half],
                                               op=ALU.mult)
            last.then_inc(masks_made, 1)

        def block_slots(pe, b):
            pe.wait_ge(masks_made, b + 1)
            for t in range(BT):
                out_ = hid_ps[t // 2][:, (t % 2) * SLOTW:(t % 2 + 1) * SLOTW]
                nc.tensor.matmul(out_[:, 0:PAIRS], lo_m[:, t, :], pair_sel[:, :], start=True, stop=True)
                last = nc.tensor.matmul(out_[:, PAIRS:SLOTW], hi_m[:, t, :], ident16[:, :], start=True, stop=True)
            last.then_inc(slot_mm, 1)

        def block_slots_act(act, b):
            act.wait_ge(slot_mm, b + ONE + 1)
            for bank in range(4):
                n = min(2, BT - 2 * bank)
                last = nc.scalar.activation(
                    slot[:, bass.ds(b * BT + 2 * bank, n), :],
                    hid_ps[bank][:, 0:n * SLOTW].rearrange("p (t w) -> p t w", w=SLOTW), ACT.Copy)
            last.then_inc(slot_ready, 1)

        def tile_onehots(dve, t, tb):
            dve.wait_ge(built, 8 * t + 8)
            nc.vector.tensor_tensor(
                out=lo_hot[:, tb, :, :, :],
                in0=tile_of(slot, t)[:, 0:PAIRS].rearrange("p (g q) -> p g q", q=Q).unsqueeze(2).to_broadcast(
                    [P, PAIRS // Q, P, Q]),
                in1=lo_iota[:, :, :].unsqueeze(1).to_broadcast([P, PAIRS // Q, P, Q]),
                op=ALU.is_equal).then_inc(lo_ready, 1)
            nc.vector.tensor_tensor(
                out=hi_hot[:, tb, :, :, :],
                in0=tile_of(slot, t)[:, PAIRS:SLOTW].rearrange("p (g n) -> p g n", n=8).unsqueeze(2).to_broadcast(
                    [P, P // 8, TILES, 8]),
                in1=hi_iota[:, :, :].unsqueeze(1).to_broadcast([P, P // 8, TILES, 8]),
                op=ALU.is_equal).then_inc(hi_ready, 1)

        def tile_build(pe, t, tb, also=None):
            pe.wait_ge(lo_ready, t + 1)
            pe.wait_ge(hi_ready, t + TWO + 1)
            for g in range(PAIRS // Q):
                pe.wait_ge(evacuated, 8 * t + g + 1)
                for k in range(Q):
                    last = nc.tensor.matmul(
                        psB[g % 2][:, k // 4, (k % 4) * 2 * TILES:(k % 4 + 1) * 2 * TILES],
                        lo_hot[:, tb, g, :, k],
                        hi_hot[:, tb, 2 * g + k // 4, :, (2 * k) % 8:(2 * k) % 8 + 2].rearrange("p h n -> p n h"),
                        start=True, stop=True)
                last.then_inc(built, 1)
                if also is not None and g:
                    also(g)

        def tile_evacuate(act, t, tb):
            act.wait_ge(summed, t + 1)
            for g in range(PAIRS // Q):
                act.wait_ge(built, 8 * t + g + 1 + 2 * 8)
                nc.scalar.activation(
                    counts16[:, tb, :, 2 * Q * g:2 * Q * (g + 1)].rearrange("p h (g n) -> p g n h", g=2),
                    psB[g % 2][:, :, 0:8 * TILES].rearrange("p g (n h) -> p g n h", h=TILES),
                    ACT.Copy).then_inc(evacuated, 1)

        SUM_STEP = TILES // (PAIRS // Q - 1)

        def tile_sum(pe, t, tb, part=None):
            if part in (None, 1):
                pe.wait_ge(evacuated, TWO + 8 * t + 8)
                if not (is_number(t, 0) or is_number(t, 1)):
                    pe.wait_ge(sums_ready, t - 1)
            steps = range(TILES) if part is None else range((part - 1) * SUM_STEP, part * SUM_STEP)
            for h in steps:
                last = nc.tensor.matmul(psC[2 + tb][:, 0:2 * D], counts16[:, tb, h, :],
                                        x16[:, h, :, :].rearrange("p a f -> p (a f)"), start=(h == 0),
                                        stop=(h == TILES - 1))
            if steps[-1] == TILES - 1:
                last.then_inc(summed, 1)

        def tile_of(rows_, t):
            return rows_[:, bass.ds(t, 1), :].rearrange("p t f -> p (t f)")

        def tile_sums_act(act, t, tb):
            act.wait_ge(summed, TWO + t + 1)
            act.wait_ge(z_ready, t + 1)
            nc.scalar.activation(sums[:, tb, 0:D], psC[2 + tb][:, 0:D], ACT.Copy)
            nc.scalar.activation(sums[:, tb, D:2 * D], psC[2 + tb][:, D:2 * D], ACT.Copy,
                                 scale=1.0 / LOSCALE).then_inc(sums_ready, 1)

        def tile_sums_pool(pool, t, tb):
            pool.wait_ge(sums_ready, t + 1)
            nc.gpsimd.tensor_tensor(out=sums[:, tb, 0:D], in0=sums[:, tb, 0:D], in1=sums[:, tb, D:2 * D],
                                    op=ALU.add).then_inc(sums_added, 1)

        def tile_z(dve, t, tb):
            dve.wait_ge(sums_added, t + 1)
            nc.vector.scalar_tensor_tensor(out=tile_of(zn, t), in0=tile_of(xn, t), scalar=one_eps[:, :],
                                           in1=sums[:, tb, 0:D], op0=ALU.mult, op1=ALU.add).then_inc(z_ready, 1)

        def is_number(step, value):
            return isinstance(step, int) and step == value

        def is_block(b):
            return not isinstance(b, int) or 0 <= b < NBLK

        def over_blocks(eng, body):
            body(0, 0, 0)
            with eng.Fori(0, (NBLK - 3) // 2) as i:
                body(i * 2 + 1, 1, i)
                body(i * 2 + 2, 0, i + 1)
            for b in range(NBLK - 2, NBLK):
                body(b, b % 2, b // 2)

        def over_tiles(eng, body):
            fours = (TILES - 4) // 4
            for t in range(2):
                body(t, t)
            with eng.Fori(0, fours) as i:
                for k in range(4):
                    body(i * 4 + (2 + k), k % 2)
            for t in range(2 + 4 * fours, TILES):
                body(t, t % 2)

        def is_tile(t):
            return not isinstance(t, int) or 0 <= t < TILES

        block = ctx.enter_context(nc.Block())

        @block.sync
        def _(sp):
            sp.dma_start(dst_in_i[:, 0, :], dst[0:P * GROUP].rearrange("(g c) -> g c", g=P)).then_inc(dst_in, 16)
            sp.dma_start(dst_in_i[0:FULL - P, 1, :],
                         dst[P * GROUP:FULL * GROUP].rearrange("(g c) -> g c", c=GROUP)).then_inc(dst_in, 16)
            sp.dma_start(dst_in_i[FULL - P:NG - P, 1, :],
                         dst[E - GROUP:E].rearrange("(g c) -> g c", g=1)).then_inc(dst_in, 16)

            def load(k, u):
                sp.wait_ge(seg_mm, 2 * u + 2)
                sp.dma_start(edges[:, k, :, :, :],
                             attr[bass.ds(u * (2 * GROUP), 2 * GROUP), :].rearrange("(h p j) f -> p h j f", h=2, j=EPP)
                             ).then_inc(edges_in[k], 16)

            for k in range(RING):
                load(k, k)
            vectors = [(row("b2b"), b2b), (row("g2"), g2), (row("be2"), be2), (row("m2"), m2), (row("v2"), v2)]
            columns = [("b1b", b1b), ("g1", g1), ("be1", be1), ("m1", m1), ("v1", v1)]
            for dst_, src_ in vectors:
                sp.dma_start(dst_, src_.rearrange("(o f) -> o f", o=1)).then_inc(small_in, 16)
            sp.dma_start(rowf[0:1, 0, :], b2a.rearrange("(o f) -> o f", o=1)).then_inc(small_in, 16)
            sp.dma_start(rows[0:1, ROWS.index("eps"), 0:1], gin_eps).then_inc(small_in, 16)
            for name, src_ in columns:
                sp.dma_start(col(name), src_.rearrange("(p o) -> p o", o=1)).then_inc(small_in, 16)
            for k in range(2):
                sp.dma_start(cols[:, k:k + 1], b1a[k * P:(k + 1) * P].rearrange("(p o) -> p o", o=1)
                              ).then_inc(small_in, 16)
            sp.dma_start(col("u"), u[0, :].rearrange("(p o) -> p o", o=1)).then_inc(small_in, 16)
            sp.dma_start(w1a_s[:, :, :], w1a.rearrange("(k p) n -> p k n", p=P)).then_inc(weights_in, 16)
            sp.dma_start(w2a_s[:, :, :], w2a.rearrange("(k p) n -> p k n", p=P)).then_inc(weights_in, 16)
            sp.dma_start(w1b_s[:, :], w1b).then_inc(weights_in, 16)
            sp.dma_start(w2b_s[:, :], w2b).then_inc(weights_in, 16)
            sp.wait_ge(dve_made, CLEARED)
            sp.dma_start(xn[:, 0:TILES - 1, :],
                          x[0:(TILES - 1) * P, :].rearrange("(t p) f -> p t f", p=P)).then_inc(x_in, 16)
            sp.dma_start(xn[0:TAIL, TILES - 1, :], x[(TILES - 1) * P:N, :]).then_inc(x_in, 16)
            sp.dma_start(src_pad[0:FULL * GROUP, 0].rearrange("(p c) -> p c", p=P),
                          src[0:FULL * GROUP].rearrange("(p c) -> p c", p=P)).then_inc(padded, 16)
            sp.dma_start(src_pad[FULL * GROUP:E, 0].rearrange("(o c) -> o c", o=1),
                          src[FULL * GROUP:E].rearrange("(o c) -> o c", o=1)).then_inc(padded, 16)
            sp.dma_start(src_pad[E:E + SLOTS, 0].rearrange("(o c) -> o c", o=1),
                          src[0:SLOTS].rearrange("(o c) -> o c", o=1)).then_inc(padded, 16)

            with sp.Fori(1, TURNS) as i:
                for k in range(RING):
                    load(k, i * RING + k)
            sp.wait_ge(seg_mm, 2 * (UNITS - 1) + 2)
            sp.dma_start(edges[:, 0, 0, :, :], attr[(FULL - 1) * GROUP:FULL * GROUP, :].rearrange(
                "(p j) f -> p j f", j=EPP)).then_inc(edges_in[0], 16)
            sp.dma_start(edges[:, 0, 1, :, :], last_edges).then_inc(edges_in[0], 16)

            sp.wait_ge(missed_ready, 1)
            missed = sp.value_load(flags_i[0:1, 0:1])
            with sp.If(missed != 0):
                s = SW[0]
                with sp.Fori(0, FULL) as g:
                    sp.wait_ge(s["mm"], g * SWEEP + ONE)
                    sp.dma_start(edges[:, 0, 0, :, :], attr[bass.ds(g * GROUP, GROUP), :].rearrange(
                        "(p j) f -> p j f", j=EPP)).then_inc(s["rows"], 16)
                sp.wait_ge(s["mm"], FULL * SWEEP + ONE)
                sp.dma_start(edges[:, 0, 0, :, :], last_edges).then_inc(s["rows"], 16)

            sp.wait_ge(general_ready, 1)
            general = sp.value_load(flags_i[0:1, 1:2])
            with sp.If(general != 0):
                sp.wait_ge(hi_ready, TWO + 1)
                sp.dma_start(src_i[:, 0:FULL, :],
                             src[0:FULL * GROUP].rearrange("(g p j) -> p g j", p=P, j=EPP)).then_inc(src_in, 16)
                sp.dma_start(src_i[:, FULL, :], src[E - GROUP:E].rearrange("(p j) -> p j", j=EPP)).then_inc(src_in, 16)
                sp.wait_ge(normed, NBLK + ONE)
                sp.dma_start(x1_rows.rearrange("(t p) f -> p t f", p=P), xn[:, :, :]).then_inc(x1_stored, 16)
                sp.wait_ge(src_in, 32)
                sp.wait_ge(x1_stored, 16)

            with sp.Fori(0, NBLK - 1) as b:
                sp.wait_ge(normed, NBLK + ONE + 1 + b)
                sp.dma_start(out[bass.ds(b * BLK, BLK), :].rearrange("(t p) f -> p t f", p=P),
                             block_of(zn, b)).then_inc(stored, 16)
            sp.wait_ge(normed, 2 * NBLK + ONE)
            sp.dma_start(out[(NBLK - 1) * BLK:(TILES - 1) * P, :].rearrange("(t p) f -> p t f", p=P),
                         zn[:, TILES - BT:TILES - 1, :]).then_inc(stored, 16)
            sp.dma_start(out[(TILES - 1) * P:N, :], zn[0:TAIL, TILES - 1, :]).then_inc(stored, 16)
            sp.wait_ge(stored, 16 * (NBLK + 1))

        @block.gpsimd
        def _(pool):
            made = [0]

            def step(ins):
                made[0] += 1
                ins.then_inc(pool_made, 1)
                pool.wait_ge(pool_made, made[0])

            step(nc.gpsimd.iota(part_no[:, :], [[0, 1]], base=0, channel_multiplier=1))
            step(nc.gpsimd.iota(iota_i[:, 0:WIN], [[1, WIN]], base=0, channel_multiplier=0))
            step(nc.gpsimd.tensor_copy(win_no[:, :], iota_i[:, 0:WIN]))
            step(nc.gpsimd.memset(ones[:, :], 1.0))
            step(nc.gpsimd.memset(ones16[:, :], 1.0))
            step(nc.gpsimd.affine_select(out=ident[:, :], in_=ones[:, :], compare_op=ALU.is_equal, fill=0.0, base=0,
                                         pattern=[[-1, P]], channel_multiplier=1))
            step(nc.gpsimd.affine_select(out=upper[:, :], in_=ones[:, :], compare_op=ALU.is_ge, fill=0.0, base=-1,
                                         pattern=[[1, P]], channel_multiplier=-1))
            step(nc.gpsimd.affine_select(out=shift[:, :], in_=ones[:, :], compare_op=ALU.is_equal, fill=0.0, base=-1,
                                         pattern=[[-1, P]], channel_multiplier=1))
            step(nc.gpsimd.affine_select(out=last_p[:, :], in_=ones[0:1, :], compare_op=ALU.is_ge, fill=0.0,
                                         base=-(P - 1), pattern=[[1, P]], channel_multiplier=0))
            assert made[0] == POOL_FIRST
            nc.gpsimd.memset(acc[:, :, :], 0.0).then_inc(acc_zero, 1)
            pool.wait_ge(dve_made, REL_MADE)
            step(nc.gpsimd.affine_select(out=rel[:, FULL, :], in_=rel[:, FULL, :], compare_op=ALU.is_ge,
                                         fill=-FAR, base=-REPEATS, pattern=[[1, EPP]], channel_multiplier=EPP))
            step(nc.gpsimd.affine_select(out=pair_sel[:, :], in_=ones16[:, 0:PAIRS], compare_op=ALU.is_ge, fill=0.0,
                                         base=0, pattern=[[-2, PAIRS]], channel_multiplier=1))
            step(nc.gpsimd.affine_select(out=pair_sel[:, :], in_=pair_sel[:, :], compare_op=ALU.is_ge, fill=0.0,
                                         base=1, pattern=[[2, PAIRS]], channel_multiplier=-1))
            step(nc.gpsimd.tensor_copy(ident16[:, :], ident[:, :]))
            step(nc.gpsimd.iota(iota_i[:, 0:P], [[0, 2], [1, SLOTS]], base=0, channel_multiplier=0))
            step(nc.gpsimd.tensor_copy(slot_no[:, :, :].rearrange("p a s -> p (a s)"), iota_i[:, 0:P]))
            pool.wait_ge(dve_made, PARITY_MADE)
            for a in range(2):
                step(nc.gpsimd.tensor_scalar(slot_no[:, a, :], slot_no[:, a, :], parity[:, a:a + 1], None, ALU.add))
            step(nc.gpsimd.iota(iota_i[:, :], [[1, P], [0, Q]], base=0, channel_multiplier=0))
            step(nc.gpsimd.tensor_copy(lo_iota[:, :, :].rearrange("p l q -> p (l q)"), iota_i[:, :]))
            step(nc.gpsimd.iota(iota_i[:, 0:TILES * 8], [[1, TILES], [0, 8]], base=1, channel_multiplier=0))
            step(nc.gpsimd.tensor_copy(hi_iota[:, :, :].rearrange("p h n -> p (h n)"), iota_i[:, 0:TILES * 8]))
            assert made[0] == POOL_MADE, made[0]

            def residual(b, buf, which):
                nc.gpsimd.tensor_tensor(
                    out=yn[:, buf, :, :], in0=block_of(xn, b),
                    in1=row_bc[:, which, :].unsqueeze(1).to_broadcast([P, BT, D]), op=ALU.add
                ).then_inc(resid_ready, 1)

            pool.wait_ge(x_in, 32)
            pool.wait_ge(act_made, ROWS_SPREAD)

            def load_sources(b):
                for t in range(BT):
                    c = b * BT + t
                    nc.gpsimd.indirect_dma_start(
                        sources[:, b % 2, t, :], None, src_pad,
                        bass.IndirectOffsetOnAxis(start_i[:, c:c + 1].bitcast(U32), 0)).then_inc(sources_in[b % 2], 16)

            def low_part(b):
                pool.wait_ge(hi_copied, b + 1)
                nc.gpsimd.tensor_tensor(out=yn[:, b % 2, :, :], in0=xn[:, b * BT:(b + 1) * BT, :],
                                        in1=x16[:, b * BT:(b + 1) * BT, 0, :], op=ALU.subtract).then_inc(lo_diff, 1)

            for b in range(2):
                residual(b, b, 0)
            pool.wait_ge(padded, 48)
            pool.wait_ge(start_ready, 1)
            for b in range(2):
                load_sources(b)
            for b in range(2, NBLK):
                pool.wait_ge(masks_made, b - 1)
                load_sources(b)
                low_part(b - 2)
                pool.wait_ge(split_done, b + ONE - 1)
                residual(b, b % 2, 0)
            for b in range(NBLK - 2, NBLK):
                low_part(b)

            pool.wait_ge(general_ready, 1)
            general = pool.value_load(flags_i[0:1, 1:2])
            with pool.If(general == 0):
                over_tiles(pool, lambda t, tb: tile_sums_pool(pool, t, tb))
            with pool.If(general != 0):
                s = SW[1]
                pool.wait_ge(src_in, 32)
                pool.wait_ge(x1_stored, 16)
                with pool.Fori(0, NG) as g:
                    pool.wait_ge(s["mm"], g * SWEEP + ONE)
                    nc.gpsimd.tensor_copy(gidx[:, :], group_of(src_i, g)).then_inc(idx_copied, 1)
                    pool.wait_ge(idx_copied, g + 1)
                    pool.sem_inc(idx_seen, 1)
                    for j in range(EPP):
                        nc.gpsimd.indirect_dma_start(
                            edges[:, 0, 0, j, :], None, x1_rows,
                            bass.IndirectOffsetOnAxis(gidx[:, j:j + 1].bitcast(U32), 0)).then_inc(s["rows"], 16)
                    pool.wait_ge(s["rows"], g * (16 * EPP) + 16 * EPP)


            def layer1(b, buf, turn_no):
                pool.wait_ge(normed, b + NBLK)
                residual(b, buf, 2)

            pool.wait_ge(split_done, NBLK + ONE)
            over_blocks(pool, layer1)

        @block.scalar
        def _(act):
            act.sem_inc(seg_copied, TWO)
            act.sem_inc(split_done, ONE)
            act.sem_inc(slot_ready, TWO)
            act.sem_inc(evacuated, TWO)
            for i in range(4):
                act.wait_ge(rows_turned, i + 1)
                nc.scalar.activation(
                    dst_f[:, :, 2 * i:2 * i + 2],
                    hid_ps[i][:, 0:2 * NG].rearrange("p (j g) -> p g j", j=2), ACT.Copy).then_inc(rows_read, 1)

            def copy_group(g, buf):
                act.wait_ge(seg_mm, g + RING_GROUPS + 1)
                act.wait_ge(seg_turned, g + 1 + NHOT - TWO)
                nc.scalar.activation(seg[:, buf, :], seg_ps[buf][0:WIN, 0:D], ACT.Copy).then_inc(seg_copied, 1)

            for g in range(2):
                copy_group(g, g)
            act.wait_ge(small_in, 16 * SMALLS)
            nc.scalar.activation(std1[:, :], col("v1"), ACT.Sqrt, bias=eps_col[:, :]).then_inc(act_made, 1)
            nc.scalar.activation(std2[:, :], row("v2"), ACT.Sqrt, bias=eps_col[0:1, :]).then_inc(act_made, 1)
            for g in range(2, RING_GROUPS):
                copy_group(g, g % 2)
            act.wait_ge(pe_made, PE_ROWS)
            nc.scalar.activation(row_bc[:, :, :].rearrange("p a f -> p (a f)"), psC[1][:, 0:3 * D],
                                 ACT.Copy).then_inc(act_made, 1)
            with act.Fori(RING_GROUPS // 2, NG // 2) as i:
                for k in range(2):
                    copy_group(i * 2 + k, k)

            act.wait_ge(missed_ready, 1)
            missed = act.value_load(flags_i[0:1, 0:1])
            with act.If(missed != 0):
                sweep_act(act, SW[0])

            act.wait_ge(totals_mm, 1)
            nc.scalar.activation(totals[:, :], psC[1][0:TILES, 0:P], ACT.Copy).then_inc(totals_ready, 1)

            mlp_turn_act(act, 0)
            for b in range(NBLK):
                act.wait_ge(spread_mm, b + 1)
                nc.scalar.activation(acc[:, 1, b * BLK:b * BLK + 4 * P], psB[b % 2][:, 0, :],
                                     ACT.Copy).then_inc(spread_act, 1)

            def high_part(b):
                act.wait_ge(normed, b + ONE + 1)
                nc.scalar.activation(x16[:, bass.ds(b * BT, BT), 0, :], block_of(xn, b), ACT.Copy
                                     ).then_inc(hi_copied, 1)

            def low_part(b, buf):
                act.wait_ge(lo_diff, b + 1)
                nc.scalar.activation(x16[:, bass.ds(b * BT, BT), 1, :], yn[:, buf, :, :], ACT.Copy,
                                     scale=LOSCALE).then_inc(split_done, 1)

            def layer0(b, buf, turn_no):
                mlp_relu(act, b, 0)
                if is_block(b - 1):
                    high_part(b - 1)
                if is_block(b + 1):
                    mlp_turn_act(act, b + 1)
                if is_block(b - 1):
                    block_slots_act(act, b - 1)
                if not is_block(b + 1):
                    block_slots_act(act, b)
                mlp_std(act, b)
                if is_block(b - 1):
                    low_part(b - 1, 1 - buf)

            def last_parts():
                high_part(NBLK - 1)
                low_part(NBLK - 1, (NBLK - 1) % 2)

            over_blocks(act, layer0)
            act.wait_ge(general_ready, 1)
            general = act.value_load(flags_i[0:1, 1:2])
            with act.If(general == 0):
                def body(t, tb):
                    if is_number(t, TILES - 1):
                        act.wait_ge(built, 2 * 8 + 8 * t)
                        mlp_turn_act(act, NBLK)
                    tile_evacuate(act, t, tb)
                    if is_number(t, 0):
                        last_parts()
                    if is_tile(t - 1):
                        tile_sums_act(act, t - 1, 1 - tb)

                over_tiles(act, body)
                mlp_relu(act, NBLK, 1, 0)
                mlp_turn_act(act, NBLK + 1)
                tile_sums_act(act, TILES - 1, 0)
            with act.If(general != 0):
                last_parts()
                sweep_act(act, SW[1])
                with act.Fori(0, TILES) as t:
                    act.wait_ge(summed, t + TWO)
                    act.wait_ge(SW[1]["added"], NG * SWEEP)
                    nc.scalar.activation(acc_tile[:, :], acc[:, 0, bass.ds(t * P, P)], ACT.Copy).then_inc(acc_staged, 1)
                mlp_turn_act(act, NBLK)
                mlp_relu(act, NBLK, 1, 0)
                mlp_turn_act(act, NBLK + 1)

            def layer1(b, buf, turn_no):
                if is_block(b + 1):
                    mlp_relu(act, b + NBLK + 1, 1, 1 - buf)
                if is_block(b + 2):
                    mlp_turn_act(act, b + NBLK + 2)
                mlp_std(act, b + NBLK)

            over_blocks(act, layer1)

        @block.vector
        def _(dve):
            dve.sem_inc(group_added, TWO)
            dve.sem_inc(y_read, ONE)
            dve.sem_inc(normed, ONE)
            dve.sem_inc(hi_ready, TWO)
            dve.sem_inc(general_z, ONE)
            dve.sem_inc(z_ready, TWO)
            made = [0]

            def step(ins):
                made[0] += 1
                ins.then_inc(dve_made, 1)
                dve.wait_ge(dve_made, made[0])

            step(nc.vector.memset(eps_col[:, :], EPS))
            step(nc.vector.memset(xn[:, TILES - 1, :], 0.0))
            assert made[0] == CLEARED
            dve.wait_ge(pool_made, 1)
            step(nc.vector.tensor_scalar(parity_i[:, :], part_no[:, :], 1, None, ALU.bitwise_and))
            step(nc.vector.tensor_scalar(parity[:, 0:1], parity_i[:, :], FAR, None, ALU.mult))
            step(nc.vector.tensor_scalar(parity[:, 1:2], parity[:, 0:1], -1.0, FAR, ALU.mult, ALU.add))
            assert made[0] == PARITY_MADE
            dve.wait_ge(dst_in, 48)
            step(nc.vector.tensor_copy(dst_rows[:, 0, :], dst_in_i[:, 0, :]))
            step(nc.vector.tensor_copy(dst_rows[0:NG - P, 1, :], dst_in_i[0:NG - P, 1, :]))
            assert made[0] == ABS_ROWS
            dve.wait_ge(rows_read, 4)
            step(nc.vector.memset(next_first[:, :], FAR))
            step(nc.vector.tensor_copy(next_first[0:1, 0:FULL - 1], dst_f[0:1, 1:FULL, 0]))
            step(nc.vector.tensor_copy(first_i[0:1, :], dst_f[0:1, :, 0]))
            assert made[0] == ABS_MADE
            dve.wait_ge(pe_made, PE_BASE)
            step(nc.vector.tensor_tensor(out=rel[:, :, :], in0=dst_f[:, :, :],
                                         in1=psC[0][:, 0:NG].unsqueeze(2).to_broadcast([P, NG, EPP]),
                                         op=ALU.subtract))
            assert made[0] == REL_MADE

            def hot(g, buf):
                dve.wait_ge(seg_mm, g + RING_GROUPS - NHOT + 1)
                make_onehot(buf, group_of(rel, g)).then_inc(onehot_ready, 1)
                dve.wait_ge(onehot_ready, g + 1)
                dve.wait_ge(seg_turned, g + 1)
                sum_onehot(buf).then_inc(hotsum_ready, 1)

            def add(g, buf):
                base = dve.value_load(first_i[0:1, bass.ds(g, 1)], min_val=0, max_val=N - 1)
                dve.wait_ge(seg_turned, g + 1 + NHOT)
                dve.wait_ge(group_added, g + TWO)
                add_group(base, turn_ps[buf], 2).then_inc(group_added, 1)

            dve.wait_ge(pool_made, POOL_FIRST + 1)
            for g in range(2):
                hot(g, g)

            dve.wait_ge(acc_zero, 1)

            def two_groups(first, k):
                hot(first + 2, (k + 2) % NHOT)
                add(first, k % 2)

            for k in range(3):
                two_groups(k, k)
            dve.wait_ge(small_in, 16 * SMALLS)
            dve.wait_ge(act_made, 2)
            step(nc.vector.reciprocal(std2[:, :], std2[:, :]))
            two_groups(3, 3)
            step(nc.vector.tensor_tensor(out=rowf[0:1, 1, :], in0=row("g2"), in1=std2[:, :], op=ALU.mult))
            step(nc.vector.tensor_tensor(out=rowf[0:1, 2, :], in0=row("b2b"), in1=row("m2"), op=ALU.subtract))
            two_groups(4, 4)
            step(nc.vector.tensor_tensor(out=rowf[0:1, 2, :], in0=rowf[0:1, 2, :], in1=rowf[0:1, 1, :], op=ALU.mult))
            step(nc.vector.tensor_tensor(out=rowf[0:1, 2, :], in0=rowf[0:1, 2, :], in1=row("be2"), op=ALU.add))
            two_groups(5, 5)
            step(nc.vector.tensor_scalar(rowf[0:1, 2, :], rowf[0:1, 2, :], 0.5, None, ALU.mult))
            assert made[0] == ROWS_MADE, made[0]
            step(nc.vector.reciprocal(std1[:, :], std1[:, :]))
            step(nc.vector.tensor_tensor(out=fold[:, 0:1], in0=col("g1"), in1=std1[:, :], op=ALU.mult))
            two_groups(6, 6)
            step(nc.vector.tensor_tensor(out=fold[:, 1:2], in0=col("b1b"), in1=col("m1"), op=ALU.subtract))
            step(nc.vector.tensor_tensor(out=fold[:, 1:2], in0=fold[:, 1:2], in1=fold[:, 0:1], op=ALU.mult))
            step(nc.vector.tensor_tensor(out=fold[:, 1:2], in0=fold[:, 1:2], in1=col("be1"), op=ALU.add))
            two_groups(7, 7)
            assert RING_GROUPS == 8
            with dve.Fori(1, TURNS) as i:
                for k in range(RING_GROUPS):
                    two_groups(i * RING_GROUPS + k, k)
            for g in range(NG - 2, NG):
                add(g, g % 2)

            dve.wait_ge(pe_made, PE_ROWS)
            step(nc.vector.tensor_tensor(out=bias0[:, :], in0=cols[:, 0:2], in1=psC[2][:, 0:2], op=ALU.add))
            step(nc.vector.tensor_scalar(one_eps[:, :], psC[2][:, 2:3], 1.0, None, ALU.add))
            assert made[0] == BIAS_MADE, made[0]
            dve.wait_ge(pool_made, POOL_MADE)

            def degrees(done):
                for i in range(DEG_STEPS):
                    n = min(4, TILES - 4 * i)
                    dve.wait_ge(deg_mm, done + i + 1)
                    nc.vector.tensor_copy(deg[:, 4 * i:4 * i + n],
                                          psC[i % 3][:, 0:n * P].rearrange("p (t c) -> p t c", c=P)[:, :, 0]
                                          ).then_inc(deg_read, 1)

            degrees(0)
            dve.wait_ge(total_mm, 1)
            step(nc.vector.tensor_reduce(out=bad[:, 0:1], in_=psC[1][:, 0:TILES], axis=AX.X, op=ALU.add))
            step(nc.vector.tensor_scalar(bad[:, 0:1], bad[:, 0:1], float(E), None, ALU.subtract))
            nc.vector.tensor_copy(flags_i[0:1, 0:1], bad[0:1, 0:1]).then_inc(missed_ready, 1)

            table_steps = [0]

            def table_step(ins):
                table_steps[0] += 1
                ins.then_inc(table_ready, 1)
                dve.wait_ge(table_ready, table_steps[0])

            dve.wait_ge(missed_ready, 1)
            missed = dve.value_load(flags_i[0:1, 0:1])
            mask = scratch[:, 0:NG * EPP].rearrange("p (g j) -> p g j", j=EPP)
            with dve.If(missed != 0):
                table_step(nc.vector.tensor_scalar(mask, rel[:, :, :], 0.0, None, ALU.is_lt))
                table_step(nc.vector.scalar_tensor_tensor(out=mask, in0=rel[:, :, :], scalar=float(WIN), in1=mask,
                                                          op0=ALU.is_ge, op1=ALU.add))
                table_step(nc.vector.scalar_tensor_tensor(out=mask, in0=rel[:, :, :], scalar=-FAR, in1=mask,
                                                          op0=ALU.is_gt, op1=ALU.mult))
                table_step(nc.vector.tensor_copy(left[:, :, :], dst_f[:, :, :]))
                table_step(nc.vector.scalar_tensor_tensor(out=left[:, :, :], in0=left[:, :, :], scalar=1.0, in1=mask,
                                                          op0=ALU.add, op1=ALU.mult))
                table_step(nc.vector.tensor_scalar(left[:, :, :], left[:, :, :], -1.0, None, ALU.add))
                sweep_dve(dve, SW[0], 2, left)
                degrees(DEG_STEPS)
                dve.wait_ge(deg_read, 2 * DEG_STEPS)
            dve.wait_ge(deg_read, DEG_STEPS)
            dve.wait_ge(missed_ready, 1)
            nc.vector.tensor_scalar(rdeg[:, :], deg[:, :], 1.0, None, ALU.max).then_inc(rdeg_ready, 1)
            dve.wait_ge(rdeg_ready, 1)
            nc.vector.reciprocal(rdeg[:, :], rdeg[:, :]).then_inc(rdeg_ready, 1)
            nc.vector.tensor_scalar(over[:, :], deg[:, :], float(SLOTS), None, ALU.is_gt).then_inc(deg_final, 1)
            dve.wait_ge(deg_final, 1)
            step(nc.vector.tensor_reduce(out=disorder[:, 1:2], in_=over[:, :], axis=AX.X, op=ALU.add))
            dve.wait_ge(start_mm, 1)
            nc.vector.tensor_copy(start_i[:, :], psC[0][:, 0:TILES]).then_inc(start_ready, 1)
            def edge_means(b):
                dve.wait_ge(h_mm, 4 * b + ONE)
                dve.wait_ge(spread_act, b + 1)
                nc.vector.tensor_tensor(out=mlp[:, 1, :], in0=acc[:, 1, bass.ds(b * BLK, BLK)],
                                        in1=acc[:, 0, bass.ds(b * BLK, BLK)], op=ALU.mult).then_inc(eT_ready, 1)

            for b in range(NBLK):
                dve.wait_ge(spread_mm, b + 1)
                nc.vector.tensor_copy(acc[:, 1, b * BLK + 4 * P:(b + 1) * BLK], psB[b % 2][:, 1, 0:BLK - 4 * P]
                                      ).then_inc(spread_dve, 1)
                if b == 1:
                    dve.wait_ge(spread_dve, 1)
                    edge_means(0)
            dve.wait_ge(spread_dve, NBLK)
            before = scratch[:, 0:NG * (EPP - 1)].rearrange("p (g j) -> p g j", j=EPP - 1)
            across = scratch[:, NG * (EPP - 1):NG * EPP]
            step(nc.vector.tensor_tensor(out=before, in0=dst_f[:, :, 0:EPP - 1], in1=dst_f[:, :, 1:EPP],
                                         op=ALU.is_gt))
            step(nc.vector.tensor_tensor(out=across, in0=dst_f[:, :, EPP - 1], in1=psC[3][:, 0:NG], op=ALU.is_gt))
            step(nc.vector.tensor_reduce(out=disorder[:, 0:1], in_=scratch[:, 0:NG * EPP], axis=AX.X, op=ALU.add))

            step(nc.vector.tensor_tensor(out=bad[:, 1:2], in0=disorder[:, 0:1], in1=disorder[:, 1:2], op=ALU.add))
            assert made[0] == BAD_MADE, made[0]
            dve.wait_ge(act_made, ROWS_SPREAD)
            dve.wait_ge(weights_in, 64)
            step(nc.vector.tensor_tensor(out=w2b_s[:, :], in0=w2b_s[:, :], in1=row_bc[:, 1, :], op=ALU.mult))

            def layer0(b, buf, turn_no):
                if is_block(b + 1):
                    edge_means(b + 1)
                else:
                    dve.wait_ge(slot_ready, TWO + 1)
                    tile_onehots(dve, 0, 0)
                block_masks(dve, b, buf, turn_no)
                mlp_norm(dve, b, 0, buf, block_of(xn, b))

            dve.wait_ge(group_added, NG + TWO)
            dve.wait_ge(bad_mm, 1)
            nc.vector.tensor_copy(flags_i[0:1, 1:2], psC[2][0:1, 0:1]).then_inc(general_ready, 1)
            over_blocks(dve, layer0)

            dve.wait_ge(general_ready, 1)
            general = dve.value_load(flags_i[0:1, 1:2])
            with dve.If(general == 0):
                dve.wait_ge(slot_ready, TWO + NBLK)

                def body(t, tb):
                    if is_tile(t + 1):
                        tile_onehots(dve, t + 1, 1 - tb)
                    if is_tile(t - 2):
                        tile_z(dve, t - 2, tb)

                over_tiles(dve, body)
                for t in range(TILES - 2, TILES):
                    tile_z(dve, t, t % 2)
            with dve.If(general != 0):
                dve.wait_ge(slot_ready, TWO + NBLK)
                nc.vector.memset(acc[:, 0, :], 0.0).then_inc(table1_ready, 1)
                nc.vector.tensor_scalar(mask, rel[:, :, :], -FAR, None, ALU.is_gt).then_inc(table1_ready, 1)
                nc.vector.tensor_copy(left[:, :, :], dst_f[:, :, :]).then_inc(table1_ready, 1)
                dve.wait_ge(table1_ready, 3)
                nc.vector.scalar_tensor_tensor(out=left[:, :, :], in0=left[:, :, :], scalar=1.0, in1=mask,
                                               op0=ALU.add, op1=ALU.mult).then_inc(table1_ready, 1)
                dve.wait_ge(table1_ready, 4)
                nc.vector.tensor_scalar(left[:, :, :], left[:, :, :], -1.0, None, ALU.add).then_inc(table1_ready, 1)
                dve.wait_ge(table1_ready, 5)
                sweep_dve(dve, SW[1], 1, left)
                with dve.Fori(0, TILES) as t:
                    dve.wait_ge(summed, t + TWO + 1)
                    nc.vector.scalar_tensor_tensor(
                        out=tile_of(zn, t), in0=tile_of(xn, t), scalar=one_eps[:, :], in1=psC[1][:, 0:D],
                        op0=ALU.mult, op1=ALU.add).then_inc(general_z, 1)

            over_blocks(dve, lambda b, buf, turn_no: mlp_norm(dve, b + NBLK, 1, buf, block_of(zn, b)))

        @block.tensor
        def _(pe):
            pe.sem_inc(seg_mm, RING_GROUPS)
            pe.sem_inc(seg_turned, NHOT)
            pe.sem_inc(xT_mm, ONE)
            pe.sem_inc(y_mm, ONE)
            pe.sem_inc(h_mm, ONE)
            pe.sem_inc(slot_mm, ONE)
            pe.sem_inc(built, 2 * 8)
            pe.sem_inc(summed, TWO)
            for s in SW:
                pe.sem_inc(s["mm"], ONE)
            pe.wait_ge(pool_made, POOL_FIRST)
            pe.wait_ge(dve_made, ABS_ROWS)
            for j in range(EPP):
                bank = hid_ps[j // 2]
                nc.tensor.transpose(bank[:, (j % 2) * NG:(j % 2) * NG + P], dst_rows[:, 0, j:GROUP:EPP], ident[:, :])
                last = nc.tensor.transpose(bank[:, (j % 2) * NG + P:(j % 2 + 1) * NG],
                                           dst_rows[0:NG - P, 1, j:GROUP:EPP], ident[0:NG - P, 0:NG - P])
                if j % 2:
                    last.then_inc(rows_turned, 1)
            pe.wait_ge(dve_made, ABS_MADE)
            nc.tensor.matmul(psC[0][:, 0:NG], ones[0:1, :], dst_f[0:1, :, 0], start=True, stop=True
                             ).then_inc(pe_made, 1)
            nc.tensor.matmul(psC[3][:, 0:NG], shift[:, :], dst_f[:, :, 0], start=True, stop=False)
            nc.tensor.matmul(psC[3][:, 0:NG], last_p[:, :], next_first[:, :], start=False, stop=True
                             ).then_inc(pe_made, 1)

            def products(g, k, h, buf):
                pe.wait_ge(onehot_ready, g + 1)
                pe.wait_ge(seg_copied, g + 1)
                multiply(seg_ps[buf % 2], buf, edges[:, k, h, :, :]).then_inc(seg_mm, 1)

            def turned(g, buf):
                pe.wait_ge(seg_copied, g + 1 + TWO)
                pe.wait_ge(hotsum_ready, g + 1)
                pe.wait_ge(group_added, g + 1)
                turn(turn_ps[buf % 2], seg[:, buf % 2, :], buf).then_inc(seg_turned, 1)

            def unit(i, k, first):
                pe.wait_ge(edges_in[k], i * 16 + 16)
                for h in range(2):
                    g = first + h
                    products(g, k, h, (2 * k + h) % NHOT)
                    if not is_number(g, 0):
                        turned(g - 1, (2 * k + h - 1) % NHOT)

            for k in range(RING):
                unit(0, k, 2 * k)
            pe.wait_ge(small_in, 16 * SMALLS)
            pe.wait_ge(weights_in, 64)
            pe.wait_ge(dve_made, ROWS_MADE)
            for k in range(2):
                nc.tensor.matmul(psC[2][:, k:k + 1], w1a_s[:, 2, k * P:(k + 1) * P], col("u"), start=True, stop=True)
            nc.tensor.matmul(psC[2][:, 2:3], ones[0:1, :], row("eps")[:, 0:1], start=True, stop=True)
            nc.tensor.matmul(psC[1][:, 0:3 * D], ones[0:1, :], rowf[:, :, :].rearrange("o a f -> o (a f)"),
                             start=True, stop=True).then_inc(pe_made, 1)
            with pe.Fori(1, TURNS) as i:
                for k in range(RING):
                    unit(i, k, i * RING_GROUPS + 2 * k)
            pe.wait_ge(edges_in[0], TURNS * 16 + 32)
            for h in range(2):
                g = NG - 2 + h
                products(g, 0, h, g % NHOT)
                turned(g - 1, (g - 1) % NHOT)
            turned(NG - 1, (NG - 1) % NHOT)

            def degrees(done):
                for i in range(DEG_STEPS):
                    if done + i >= 3:
                        pe.wait_ge(deg_read, done + i - 2)
                    for t in range(4 * i, min(4 * i + 4, TILES)):
                        last = nc.tensor.transpose(psC[i % 3][:, (t % 4) * P:(t % 4 + 1) * P],
                                                   acc[:, 1, t * P:(t + 1) * P], ident[:, :])
                    last.then_inc(deg_mm, 1)
                pe.wait_ge(deg_read, done + DEG_STEPS)

            pe.wait_ge(group_added, NG + TWO)
            pe.wait_ge(act_made, ROWS_SPREAD)
            pe.wait_ge(dve_made, BIAS_MADE)
            degrees(0)
            nc.tensor.matmul(psC[1][:, 0:TILES], ones[:, :], deg[:, :], start=True, stop=True).then_inc(total_mm, 1)

            pe.wait_ge(missed_ready, 1)
            missed = pe.value_load(flags_i[0:1, 0:1])
            with pe.If(missed != 0):
                sweep_pe(pe, SW[0], 16)
                pe.wait_ge(SW[0]["added"], NG * SWEEP)
                degrees(DEG_STEPS)

            pe.wait_ge(deg_final, 1)
            nc.tensor.matmul(psC[1][0:TILES, 0:P], deg[:, :], ones[:, :], start=True, stop=True).then_inc(totals_mm, 1)
            pe.wait_ge(totals_ready, 1)
            nc.tensor.matmul(psC[0][:, 0:TILES], upper[:, :], deg[:, :], start=True, stop=False)
            nc.tensor.matmul(psC[0][:, 0:TILES], totals[:, :], upper[0:TILES, 0:TILES], start=False, stop=True
                             ).then_inc(start_mm, 1)
            pe.wait_ge(start_ready, 1)
            pe.wait_ge(x_in, 32)
            mlp_turn(pe, xn, 0)
            pe.wait_ge(rdeg_ready, 2)
            for b in range(NBLK):
                if b >= 2:
                    pe.wait_ge(spread_act, b - 1)
                    pe.wait_ge(spread_dve, b - 1)
                for t in range(BT):
                    c = b * BT + t
                    last = nc.tensor.transpose(psB[b % 2][:, t // 4, (t % 4) * P:(t % 4 + 1) * P],
                                               rdeg[:, c:c + 1].to_broadcast([P, P]), ident[:, :])
                last.then_inc(spread_mm, 1)
            pe.wait_ge(spread_act, NBLK)
            pe.wait_ge(spread_dve, NBLK)

            for b in range(NBLK):
                mlp_hidden(pe, b, 0)
                if b + 1 < NBLK:
                    mlp_turn(pe, xn, b + 1)
                wait_hidden(pe, b, 0)
                if b:
                    block_slots(pe, b - 1)
                else:
                    pe.wait_ge(dve_made, BAD_MADE)
                    nc.tensor.matmul(psC[2][:, 0:1], ones[:, :], bad[:, 1:2], start=True, stop=True
                                     ).then_inc(bad_mm, 1)
                    pe.wait_ge(general_ready, 1)
                mlp_out(pe, b, 0)
            pe.wait_ge(slot_ready, TWO + NBLK - 1)
            block_slots(pe, NBLK - 1)
            pe.wait_ge(slot_ready, TWO + NBLK)

            general = pe.value_load(flags_i[0:1, 1:2])
            with pe.If(general == 0):
                def body(t, tb):
                    if is_number(t, 1):
                        pe.wait_ge(split_done, NBLK + ONE)
                    if is_number(t, TILES - 1):
                        pe.wait_ge(z_ready, TWO + BT)
                        mlp_turn(pe, zn, 0)
                    tile_build(pe, t, tb, (lambda g: tile_sum(pe, t - 1, 1 - tb, g)) if is_tile(t - 1) else None)

                over_tiles(pe, body)
                pe.wait_ge(evacuated, TWO + 8 * TILES)
                mlp_hidden(pe, NBLK, 1, 0)
                pe.wait_ge(z_ready, TWO + 2 * BT)
                mlp_turn(pe, zn, 1)
                tile_sum(pe, TILES - 1, 0)
                pe.wait_ge(z_ready, TWO + TILES)
            with pe.If(general != 0):
                sweep_pe(pe, SW[1], 16 * EPP)
                with pe.Fori(0, TILES) as t:
                    pe.wait_ge(acc_staged, t + 1)
                    pe.wait_ge(general_z, t + ONE)
                    nc.tensor.transpose(psC[1][:, 0:P], acc_tile[:, :], ident[:, :]).then_inc(summed, 1)
                pe.wait_ge(general_z, TILES + ONE)
                mlp_turn(pe, zn, 0)
                mlp_hidden(pe, NBLK, 1, 0)
                mlp_turn(pe, zn, 1)

            for b in range(NBLK):
                if b + 1 < NBLK:
                    mlp_hidden(pe, b + NBLK + 1, 1, (b + 1) % 2)
                if b + 2 < NBLK:
                    mlp_turn(pe, zn, b + 2)
                wait_hidden(pe, b + NBLK, 1)
                mlp_out(pe, b + NBLK, 1, b % 2)


_INS = ['x', 'src', 'dst', 'edge_attr_128', 'L0_gnn_u', 'L0_gnn_W1', 'L0_gnn_b1', 'L0_gnn_W2', 'L0_gnn_b2',
        'L1_gnn_eps', 'L1_gnn_W1', 'L1_gnn_b1', 'L1_gnn_g1', 'L1_gnn_beta1', 'L1_gnn_m1', 'L1_gnn_v1',
        'L1_gnn_W2', 'L1_gnn_b2', 'L1_gnn_g2', 'L1_gnn_beta2', 'L1_gnn_m2', 'L1_gnn_v2']


def kernel(**inputs):
    import numpy as _np
    import concourse.bacc as _bacc
    from concourse import mybir as _mybir
    from concourse.bass_utils import run_bass_kernel_spmd as _run

    nc = _bacc.Bacc("TRN2", target_bir_lowering=False, num_devices=1)
    arrays, args = {}, []
    for name in _INS:
        a = _np.ascontiguousarray(inputs[name])
        if a.ndim == 0:
            a = a.reshape(1, 1)
        arrays[f"in_{name}"] = a
        args.append(nc.dram_tensor(f"in_{name}", a.shape, _mybir.dt.from_np(a.dtype), kind="ExternalInput").ap())
    args.append(nc.dram_tensor("out_rows", (N, D), _mybir.dt.float32, kind="ExternalOutput").ap())
    build(nc, *args)
    r = _run(nc, [arrays], core_ids=[0])
    return r.results[0]["out_rows"]
```
